# Optimizing a Trainium2 kernel written in Bass

```python
import numpy as np
import jax
import jax.numpy as jnp

def _softmax(x, axis=-1):
    return jax.nn.softmax(x, axis=axis)

def _gelu(x):
    return jax.nn.gelu(x, approximate=True)

def _silu(x):
    return jax.nn.silu(x)

def _sigmoid(x):
    return jax.nn.sigmoid(x)

def _layernorm(x, axis=-1, eps=1e-05):
    m = jnp.mean(x, axis=axis, keepdims=True)
    v = jnp.var(x, axis=axis, keepdims=True)
    return (x - m) / jnp.sqrt(v + eps)

def _scatter_add(tgt, idx, src, axis=0):
    return tgt.at[idx].add(src)

def _segment_sum(src, seg, n):
    return jax.ops.segment_sum(src, seg, n)
kernel_name = 'mk_early_fusion_d2_tok_img512_r4_581f2e'

def setup_inputs(seed: int=0):
    np.random.seed(seed)
    _w = jnp.asarray

    def _rec_inputs():
        import jax
        import jax.numpy as jnp
        _rk = jax.random.key(seed)
        x = -0.000356955 + 1 * jax.random.normal(jax.random.fold_in(_rk, 1), (32, 3, 112, 112), jnp.float32)
        txt = -0.000284838 + 0.576988 * jax.random.normal(jax.random.fold_in(_rk, 2), (32, 77, 128), jnp.float32)
        return (x, txt)
    x, txt = _rec_inputs()

    def _L0_tok_setup():
        import jax, jax.numpy as jnp
        import numpy as np
        IMG = 112
        P = 16
        C = 3
        D = 128
        DC = 8
        DS = 4
        NH = IMG // P
        NPATCH = NH * NH
        PDIM = C * P * P
        BATCH = 32
        EPS = 1e-05
        key = jax.random.key(seed)
        ks = jax.random.split(key, 10)

        def lin(k, fan_in, shape):
            bound = 1.0 / np.sqrt(fan_in)
            return jax.random.uniform(k, shape, jnp.float32, -bound, bound)
        return {'images': jax.random.normal(ks[0], (BATCH, C, IMG, IMG), jnp.float32), 'W_patch': lin(ks[1], PDIM, (PDIM, D)), 'b_patch': jnp.zeros((D,), jnp.float32), 'pos_embed': jax.random.normal(ks[2], (1, NPATCH, D), jnp.float32) * 0.02, 'W_coord': lin(ks[3], D, (D, DC)), 'b_coord': jnp.zeros((DC,), jnp.float32), 'W_spinor': lin(ks[4], D, (D, DS)), 'b_spinor': jnp.zeros((DS,), jnp.float32), 'W_embed': lin(ks[5], DC, (DC, D)), 'b_embed': jnp.zeros((D,), jnp.float32), 'ln_gamma': jnp.ones((D,), jnp.float32), 'ln_beta': jnp.zeros((D,), jnp.float32), 'W_out': lin(ks[6], D, (D, D)), 'b_out': jnp.zeros((D,), jnp.float32)}
    _L0_tok_all = _L0_tok_setup()
    _L0_tok_in = {k: v for k, v in _L0_tok_all.items() if k in ('W_patch', 'b_patch', 'pos_embed', 'W_coord', 'b_coord', 'W_spinor', 'b_spinor', 'W_embed', 'b_embed', 'ln_gamma', 'ln_beta', 'W_out', 'b_out')}
    del _L0_tok_all

    def _L0_attn_setup():
        import jax, jax.numpy as jnp
        import numpy as np
        D_MODEL = 128
        N_HEADS = 8
        DH = D_MODEL // N_HEADS
        Q_PROJ = D_MODEL // 2
        KV_PROJ = 2 * D_MODEL // 3
        ROPE_DIM = D_MODEL // 8
        R = ROPE_DIM // N_HEADS
        THETA = 10000.0
        EPS = 1e-05
        B, S = (2, 512)

        def layernorm(x, g, b):
            m = jnp.mean(x, axis=-1, keepdims=True)
            v = jnp.var(x, axis=-1, keepdims=True)
            return (x - m) * jax.lax.rsqrt(v + EPS) * g + b

        def rope_cos_sin(seq_len, dtype):
            inv_freq = THETA ** (-jnp.arange(0, R, 2, dtype=jnp.float32) / R)
            ang = jnp.arange(seq_len, dtype=jnp.float32)[:, None] * inv_freq
            cos = jnp.concatenate([jnp.cos(ang), jnp.cos(ang)], axis=-1)
            sin = jnp.concatenate([jnp.sin(ang), jnp.sin(ang)], axis=-1)
            return (cos.astype(dtype), sin.astype(dtype))

        def apply_rope(x, cos, sin):
            x1, x2 = jnp.split(x, 2, axis=-1)
            rot = jnp.concatenate([-x2, x1], axis=-1)
            return x * cos + rot * sin

        def _reference_tuple_inner(x, W_dq, W_uq, W_qr, W_dkv, W_ukv, W_kr, W_o, q_ln_g, q_ln_b, kv_ln_g, kv_ln_b):
            b, s, d = x.shape
            cq = layernorm(x @ W_dq, q_ln_g, q_ln_b)
            Q = (cq @ W_uq).reshape(b, s, N_HEADS, DH).transpose(0, 2, 1, 3)
            Qr = (cq @ W_qr).reshape(b, s, N_HEADS, R).transpose(0, 2, 1, 3)
            cos, sin = rope_cos_sin(s, x.dtype)
            Qr = apply_rope(Qr, cos, sin)
            q = jnp.concatenate([Q, Qr], axis=-1)
            ckv = layernorm(x @ W_dkv, kv_ln_g, kv_ln_b)
            KV = ckv @ W_ukv
            K, V = (KV[..., :D_MODEL], KV[..., D_MODEL:])
            K = K.reshape(b, s, N_HEADS, DH).transpose(0, 2, 1, 3)
            Kr = (x @ W_kr).reshape(b, s, N_HEADS, R).transpose(0, 2, 1, 3)
            Kr = apply_rope(Kr, cos, sin)
            k = jnp.concatenate([K, Kr], axis=-1)
            v = V.reshape(b, s, N_HEADS, DH).transpose(0, 2, 1, 3)
            scale = 1.0 / jnp.sqrt(jnp.asarray(DH + R, x.dtype))
            scores = jnp.einsum('bhqd,bhkd->bhqk', q, k) * scale
            mask = jnp.tril(jnp.ones((s, s), dtype=bool))
            scores = jnp.where(mask, scores, jnp.finfo(scores.dtype).min)
            attn = jax.nn.softmax(scores, axis=-1)
            out = jnp.einsum('bhqk,bhkd->bhqd', attn, v)
            out = out.transpose(0, 2, 1, 3).reshape(b, s, d)
            return (out @ W_o.T, ckv)
        key = jax.random.key(seed)
        ks = jax.random.split(key, 9)
        p = lambda k, shape: 0.01 * jax.random.normal(k, shape, jnp.float32)
        return {'x': jax.random.normal(ks[0], (B, S, D_MODEL), jnp.float32), 'W_dq': p(ks[1], (D_MODEL, Q_PROJ)), 'W_uq': p(ks[2], (Q_PROJ, D_MODEL)), 'W_qr': p(ks[3], (Q_PROJ, ROPE_DIM)), 'W_dkv': p(ks[4], (D_MODEL, KV_PROJ)), 'W_ukv': p(ks[5], (KV_PROJ, 2 * D_MODEL)), 'W_kr': p(ks[6], (D_MODEL, ROPE_DIM)), 'W_o': p(ks[7], (D_MODEL, D_MODEL)), 'q_ln_g': jnp.ones((Q_PROJ,), jnp.float32), 'q_ln_b': jnp.zeros((Q_PROJ,), jnp.float32), 'kv_ln_g': jnp.ones((KV_PROJ,), jnp.float32), 'kv_ln_b': jnp.zeros((KV_PROJ,), jnp.float32)}
    _L0_attn_all = _L0_attn_setup()
    _L0_attn_in = {k: v for k, v in _L0_attn_all.items() if k in ('W_dq', 'W_uq', 'W_qr', 'W_dkv', 'W_ukv', 'W_kr', 'W_o', 'q_ln_g', 'q_ln_b', 'kv_ln_g', 'kv_ln_b')}
    del _L0_attn_all

    def _L0_ffn_setup():
        import jax, jax.numpy as jnp
        import numpy as np
        TOP_K = 2
        key = jax.random.key(seed)
        k1, k2, k3, k4 = jax.random.split(key, 4)
        B, S, d = (4, 512, 128)
        E, H = (32, 128)
        x = jax.random.normal(k1, (B, S, d), dtype=jnp.float32)
        expert_sel = jax.random.normal(k2, (E, d), dtype=jnp.float32) / np.sqrt(d).astype(np.float32)
        keys = jax.random.normal(k3, (E, d, H), dtype=jnp.float32) / np.sqrt(d).astype(np.float32)
        values = jax.random.normal(k4, (E, H, d), dtype=jnp.float32) / np.sqrt(E * H).astype(np.float32)
        return {'x': x, 'expert_sel': expert_sel, 'keys': keys, 'values': values}
    _L0_ffn_all = _L0_ffn_setup()
    _L0_ffn_in = {k: v for k, v in _L0_ffn_all.items() if k in ('expert_sel', 'keys', 'values')}
    del _L0_ffn_all

    def _L1_attn_setup():
        import jax, jax.numpy as jnp
        import numpy as np
        from math import sqrt
        key = jax.random.key(seed)
        k1, k2, k3, k4 = jax.random.split(key, 4)
        bs, N, D, H = (2, 1024, 128, 8)
        z = jax.random.normal(k1, (bs, N, D), dtype=jnp.float32)
        w_qkv = jax.random.normal(k2, (3 * D, D), dtype=jnp.float32) * (1.0 / sqrt(D))
        w_agg = jax.random.normal(k3, (D, D), dtype=jnp.float32) * (1.0 / sqrt(D))
        b_agg = jax.random.normal(k4, (D,), dtype=jnp.float32) * 0.01
        return {'z': z, 'w_qkv': w_qkv, 'w_agg': w_agg, 'b_agg': b_agg}
    _L1_attn_all = _L1_attn_setup()
    _L1_attn_in = {k: v for k, v in _L1_attn_all.items() if k in ('w_qkv', 'w_agg', 'b_agg')}
    del _L1_attn_all

    def _L1_ffn_setup():
        import jax, jax.numpy as jnp
        import numpy as np
        import math
        D_MODEL = 128
        N_EXPERTS = 128
        TOP_K = 8
        N_HEADS = 8
        D_KEYS = 128
        HALF = D_KEYS // 2
        N_BATCH, T_SEQ = (2, 512)
        key = jax.random.key(seed)
        k1, k2, k3, k4, k5, k6 = jax.random.split(key, 6)
        queries = jax.random.normal(k1, (N_BATCH, T_SEQ, D_MODEL), dtype=jnp.float32)
        bound_q = 1.0 / math.sqrt(D_MODEL)
        Wq = jax.random.uniform(k2, (N_HEADS * D_KEYS, D_MODEL), minval=-bound_q, maxval=bound_q, dtype=jnp.float32)
        bq = jax.random.uniform(k3, (N_HEADS * D_KEYS,), minval=-bound_q, maxval=bound_q, dtype=jnp.float32)
        bound_k = 1.0 / math.sqrt(HALF)
        keys = jax.random.uniform(k4, (N_HEADS, 2, N_EXPERTS, HALF), minval=-bound_k, maxval=bound_k, dtype=jnp.float32)
        std = D_MODEL ** (-0.5)
        w_down_embed = std * jax.random.normal(k5, (N_EXPERTS * N_EXPERTS, D_MODEL), dtype=jnp.float32)
        w_up_embed = std * jax.random.normal(k6, (N_EXPERTS * N_EXPERTS, D_MODEL), dtype=jnp.float32)
        return {'queries': queries, 'Wq': Wq, 'bq': bq, 'keys': keys, 'w_down_embed': w_down_embed, 'w_up_embed': w_up_embed}
    _L1_ffn_all = _L1_ffn_setup()
    _L1_ffn_in = {k: v for k, v in _L1_ffn_all.items() if k in ('Wq', 'bq', 'keys', 'w_down_embed', 'w_up_embed')}
    del _L1_ffn_all
    return {'x': x, 'txt': txt, 'L0_tok_W_patch': _L0_tok_in['W_patch'], 'L0_tok_b_patch': _L0_tok_in['b_patch'], 'L0_tok_pos_embed': _L0_tok_in['pos_embed'], 'L0_tok_W_coord': _L0_tok_in['W_coord'], 'L0_tok_b_coord': _L0_tok_in['b_coord'], 'L0_tok_W_spinor': _L0_tok_in['W_spinor'], 'L0_tok_b_spinor': _L0_tok_in['b_spinor'], 'L0_tok_W_embed': _L0_tok_in['W_embed'], 'L0_tok_b_embed': _L0_tok_in['b_embed'], 'L0_tok_ln_gamma': _L0_tok_in['ln_gamma'], 'L0_tok_ln_beta': _L0_tok_in['ln_beta'], 'L0_tok_W_out': _L0_tok_in['W_out'], 'L0_tok_b_out': _L0_tok_in['b_out'], 'L0_attn_W_dq': _L0_attn_in['W_dq'], 'L0_attn_W_uq': _L0_attn_in['W_uq'], 'L0_attn_W_qr': _L0_attn_in['W_qr'], 'L0_attn_W_dkv': _L0_attn_in['W_dkv'], 'L0_attn_W_ukv': _L0_attn_in['W_ukv'], 'L0_attn_W_kr': _L0_attn_in['W_kr'], 'L0_attn_W_o': _L0_attn_in['W_o'], 'L0_attn_q_ln_g': _L0_attn_in['q_ln_g'], 'L0_attn_q_ln_b': _L0_attn_in['q_ln_b'], 'L0_attn_kv_ln_g': _L0_attn_in['kv_ln_g'], 'L0_attn_kv_ln_b': _L0_attn_in['kv_ln_b'], 'L0_ffn_expert_sel': _L0_ffn_in['expert_sel'], 'L0_ffn_keys': _L0_ffn_in['keys'], 'L0_ffn_values': _L0_ffn_in['values'], 'L1_attn_w_qkv': _L1_attn_in['w_qkv'], 'L1_attn_w_agg': _L1_attn_in['w_agg'], 'L1_attn_b_agg': _L1_attn_in['b_agg'], 'L1_ffn_Wq': _L1_ffn_in['Wq'], 'L1_ffn_bq': _L1_ffn_in['bq'], 'L1_ffn_keys': _L1_ffn_in['keys'], 'L1_ffn_w_down_embed': _L1_ffn_in['w_down_embed'], 'L1_ffn_w_up_embed': _L1_ffn_in['w_up_embed']}

def reference(x, txt, L0_tok_W_patch, L0_tok_b_patch, L0_tok_pos_embed, L0_tok_W_coord, L0_tok_b_coord, L0_tok_W_spinor, L0_tok_b_spinor, L0_tok_W_embed, L0_tok_b_embed, L0_tok_ln_gamma, L0_tok_ln_beta, L0_tok_W_out, L0_tok_b_out, L0_attn_W_dq, L0_attn_W_uq, L0_attn_W_qr, L0_attn_W_dkv, L0_attn_W_ukv, L0_attn_W_kr, L0_attn_W_o, L0_attn_q_ln_g, L0_attn_q_ln_b, L0_attn_kv_ln_g, L0_attn_kv_ln_b, L0_ffn_expert_sel, L0_ffn_keys, L0_ffn_values, L1_attn_w_qkv, L1_attn_w_agg, L1_attn_b_agg, L1_ffn_Wq, L1_ffn_bq, L1_ffn_keys, L1_ffn_w_down_embed, L1_ffn_w_up_embed):
    import jax
    import jax.numpy as jnp

    def _L0_tok_ref(images, W_patch, b_patch, pos_embed, W_coord, b_coord, W_spinor, b_spinor, W_embed, b_embed, ln_gamma, ln_beta, W_out, b_out):
        import jax, jax.numpy as jnp
        import numpy as np
        IMG = 112
        P = 16
        C = 3
        D = 128
        DC = 8
        DS = 4
        NH = IMG // P
        NPATCH = NH * NH
        PDIM = C * P * P
        BATCH = 32
        EPS = 1e-05
        B = images.shape[0]
        patches = images.reshape(B, C, NH, P, NH, P)
        patches = patches.transpose(0, 2, 4, 1, 3, 5).reshape(B, NPATCH, PDIM)
        x = patches @ W_patch + b_patch + pos_embed
        coords = x @ W_coord + b_coord
        spinor = x @ W_spinor + b_spinor
        K0 = jnp.sum(spinor * spinor, axis=-1)
        x_manifold = coords @ W_embed + b_embed
        x_enh = x_manifold * K0[..., None] + x
        mu = jnp.mean(x_enh, axis=-1, keepdims=True)
        var = jnp.mean(jnp.square(x_enh - mu), axis=-1, keepdims=True)
        x_norm = (x_enh - mu) * jax.lax.rsqrt(var + EPS) * ln_gamma + ln_beta
        return x_norm @ W_out + b_out

    def _L0_attn_ref(x, W_dq, W_uq, W_qr, W_dkv, W_ukv, W_kr, W_o, q_ln_g, q_ln_b, kv_ln_g, kv_ln_b):
        import jax, jax.numpy as jnp
        import numpy as np
        D_MODEL = 128
        N_HEADS = 8
        DH = D_MODEL // N_HEADS
        Q_PROJ = D_MODEL // 2
        KV_PROJ = 2 * D_MODEL // 3
        ROPE_DIM = D_MODEL // 8
        R = ROPE_DIM // N_HEADS
        THETA = 10000.0
        EPS = 1e-05
        B, S = (2, 512)

        def layernorm(x, g, b):
            m = jnp.mean(x, axis=-1, keepdims=True)
            v = jnp.var(x, axis=-1, keepdims=True)
            return (x - m) * jax.lax.rsqrt(v + EPS) * g + b

        def rope_cos_sin(seq_len, dtype):
            inv_freq = THETA ** (-jnp.arange(0, R, 2, dtype=jnp.float32) / R)
            ang = jnp.arange(seq_len, dtype=jnp.float32)[:, None] * inv_freq
            cos = jnp.concatenate([jnp.cos(ang), jnp.cos(ang)], axis=-1)
            sin = jnp.concatenate([jnp.sin(ang), jnp.sin(ang)], axis=-1)
            return (cos.astype(dtype), sin.astype(dtype))

        def apply_rope(x, cos, sin):
            x1, x2 = jnp.split(x, 2, axis=-1)
            rot = jnp.concatenate([-x2, x1], axis=-1)
            return x * cos + rot * sin

        def _reference_tuple_inner(x, W_dq, W_uq, W_qr, W_dkv, W_ukv, W_kr, W_o, q_ln_g, q_ln_b, kv_ln_g, kv_ln_b):
            b, s, d = x.shape
            cq = layernorm(x @ W_dq, q_ln_g, q_ln_b)
            Q = (cq @ W_uq).reshape(b, s, N_HEADS, DH).transpose(0, 2, 1, 3)
            Qr = (cq @ W_qr).reshape(b, s, N_HEADS, R).transpose(0, 2, 1, 3)
            cos, sin = rope_cos_sin(s, x.dtype)
            Qr = apply_rope(Qr, cos, sin)
            q = jnp.concatenate([Q, Qr], axis=-1)
            ckv = layernorm(x @ W_dkv, kv_ln_g, kv_ln_b)
            KV = ckv @ W_ukv
            K, V = (KV[..., :D_MODEL], KV[..., D_MODEL:])
            K = K.reshape(b, s, N_HEADS, DH).transpose(0, 2, 1, 3)
            Kr = (x @ W_kr).reshape(b, s, N_HEADS, R).transpose(0, 2, 1, 3)
            Kr = apply_rope(Kr, cos, sin)
            k = jnp.concatenate([K, Kr], axis=-1)
            v = V.reshape(b, s, N_HEADS, DH).transpose(0, 2, 1, 3)
            scale = 1.0 / jnp.sqrt(jnp.asarray(DH + R, x.dtype))
            scores = jnp.einsum('bhqd,bhkd->bhqk', q, k) * scale
            mask = jnp.tril(jnp.ones((s, s), dtype=bool))
            scores = jnp.where(mask, scores, jnp.finfo(scores.dtype).min)
            attn = jax.nn.softmax(scores, axis=-1)
            out = jnp.einsum('bhqk,bhkd->bhqd', attn, v)
            out = out.transpose(0, 2, 1, 3).reshape(b, s, d)
            return (out @ W_o.T, ckv)
        return _reference_tuple_inner(x, W_dq, W_uq, W_qr, W_dkv, W_ukv, W_kr, W_o, q_ln_g, q_ln_b, kv_ln_g, kv_ln_b)[0]

    def _L0_ffn_ref(x, expert_sel, keys, values):
        import jax, jax.numpy as jnp
        import numpy as np
        TOP_K = 2
        B, S, d = x.shape
        E = keys.shape[0]
        xt = x.reshape(-1, d)
        T = xt.shape[0]
        sel = jax.nn.sigmoid(xt @ expert_sel.T)
        sel_val, sel_idx = jax.lax.top_k(sel, TOP_K)
        w = jnp.zeros((T, E), dtype=xt.dtype).at[jnp.arange(T)[:, None], sel_idx].add(sel_val)
        h = jax.nn.relu(jnp.einsum('td,edh->teh', xt, keys))
        out = jnp.einsum('teh,te,ehv->tv', h, w, values)
        return out.reshape(B, S, -1)

    def _L1_attn_ref(z, w_qkv, w_agg, b_agg):
        import jax, jax.numpy as jnp
        import numpy as np
        from math import sqrt
        bs, N, D = z.shape
        H = 8
        Dh = D // H
        qkv = jnp.einsum('bnd,ed->bne', z, w_qkv).reshape(bs, N, 3, H, Dh)
        q, k, v = jnp.moveaxis(qkv, 2, 0)
        q = q.transpose(0, 2, 1, 3)
        k = k.transpose(0, 2, 1, 3)
        v = v.transpose(0, 2, 1, 3)
        scores = jnp.einsum('bhnd,bhmd->bhnm', q, k) / sqrt(Dh)
        attn = jax.nn.softmax(scores, axis=-1)
        sa = jnp.einsum('bhnm,bhmd->bhnd', attn, v)
        sa = sa.transpose(0, 2, 1, 3).reshape(bs, N, H * Dh)
        out = jnp.einsum('bnd,ed->bne', sa, w_agg) + b_agg
        return out

    def _L1_ffn_ref(queries, Wq, bq, keys, w_down_embed, w_up_embed):
        import jax, jax.numpy as jnp
        import numpy as np
        import math
        D_MODEL = 128
        N_EXPERTS = 128
        TOP_K = 8
        N_HEADS = 8
        D_KEYS = 128
        HALF = D_KEYS // 2
        N_BATCH, T_SEQ = (2, 512)
        N, T, D = queries.shape
        H, E, K = (N_HEADS, N_EXPERTS, TOP_K)
        q_tok = queries.reshape(-1, D)
        qh = q_tok @ Wq.T + bq
        qh = qh.reshape(-1, H, 2, HALF)
        sub_scores = jnp.einsum('nhcf,hcef->nhce', qh, keys)
        s, idx = jax.lax.top_k(sub_scores, K)
        all_scores = (s[:, :, 0, :, None] + s[:, :, 1, None, :]).reshape(-1, H, K * K)
        all_idx = (idx[:, :, 0, :, None] * E + idx[:, :, 1, None, :]).reshape(-1, H, K * K)
        best_s, best_pos = jax.lax.top_k(all_scores, K)
        indices = jnp.take_along_axis(all_idx, best_pos, axis=-1)
        w_down = w_down_embed[indices]
        w_up = w_up_embed[indices]
        x = jnp.einsum('nd,nhkd->nhk', q_tok, w_down)
        x = jax.nn.gelu(x)
        vals = x * jax.nn.softmax(best_s, axis=-1)
        out = jnp.einsum('nhk,nhkd->nd', vals, w_up)
        return out.reshape(N, T, D)
    h = _L0_tok_ref(x, L0_tok_W_patch, L0_tok_b_patch, L0_tok_pos_embed, L0_tok_W_coord, L0_tok_b_coord, L0_tok_W_spinor, L0_tok_b_spinor, L0_tok_W_embed, L0_tok_b_embed, L0_tok_ln_gamma, L0_tok_ln_beta, L0_tok_W_out, L0_tok_b_out)
    h = jnp.concatenate([h, txt], axis=1)
    h = h + _L0_attn_ref(_layernorm(h, axis=-1), L0_attn_W_dq, L0_attn_W_uq, L0_attn_W_qr, L0_attn_W_dkv, L0_attn_W_ukv, L0_attn_W_kr, L0_attn_W_o, L0_attn_q_ln_g, L0_attn_q_ln_b, L0_attn_kv_ln_g, L0_attn_kv_ln_b)
    h = h + _L0_ffn_ref(_layernorm(h, axis=-1), L0_ffn_expert_sel, L0_ffn_keys, L0_ffn_values)
    h = h + _L1_attn_ref(_layernorm(h, axis=-1), L1_attn_w_qkv, L1_attn_w_agg, L1_attn_b_agg)
    h = h + _L1_ffn_ref(_layernorm(h, axis=-1), L1_ffn_Wq, L1_ffn_bq, L1_ffn_keys, L1_ffn_w_down_embed, L1_ffn_w_up_embed)
    return h

_drawn_inputs = setup_inputs


def setup_inputs(seed=0):
    import zlib

    import numpy as np

    out = dict(_drawn_inputs(seed))
    spreads = {'L0_tok_b_patch': (0.0, 0.1),
     'L0_tok_b_coord': (0.0, 0.1),
     'L0_tok_b_spinor': (0.0, 0.1),
     'L0_tok_b_embed': (0.0, 0.1),
     'L0_tok_ln_gamma': (1.0, 0.2),
     'L0_tok_ln_beta': (0.0, 0.1),
     'L0_tok_b_out': (0.0, 0.1),
     'L0_attn_q_ln_g': (1.0, 0.6),
     'L0_attn_q_ln_b': (0.0, 2.0),
     'L0_attn_kv_ln_g': (1.0, 0.6),
     'L0_attn_kv_ln_b': (0.0, 0.408)}
    factors = {'L0_attn_W_dq': 35.448,
     'L0_attn_W_uq': 34.076,
     'L0_attn_W_qr': 34.849,
     'L0_attn_W_kr': 34.862}
    for name, (base, spread) in spreads.items():
        noise = np.random.default_rng([zlib.crc32(name.encode()), seed]).standard_normal(out[name].shape)
        drawn = base * np.exp(spread * noise) if base else spread * noise
        out[name] = jnp.asarray(drawn.astype(out[name].dtype))
    for name, factor in factors.items():
        out[name] = (out[name] * factor).astype(out[name].dtype)
    return out
```

```python
import math
from contextlib import ExitStack

import concourse.bass as bass
import numpy as np
from concourse import mybir

F32 = mybir.dt.float32
U32 = mybir.dt.uint32
I32 = mybir.dt.int32
ALU = mybir.AluOpType
ACT = mybir.ActivationFunctionType
AXX = mybir.AxisListType.X

B, D = 32, 128
PAIRS = B // 2
IMG, PATCH, CH = 112, 16, 3
SIDE = IMG // PATCH
NTOK = SIDE * SIDE
NTXT = 77
S = NTOK + NTXT
KCH = CH * PATCH * PATCH // 128
DC, DS = 8, 4
HEADS, DH = 8, 16
HB = 4
RQ, RKV = 64, 85
HROWS = 32
E0, H0 = 32, 128
SLOT_OF = [(j, g) for j in range(2) for g in range(2)]
EG = 4
STEPS = 2 * E0 // EG
PH, NE, TOPK, HALF = 8, 128, 8, 64
KPT = PH * TOPK
QK = 16
QUARTERS = 2 * KPT // QK
SLOTS = 4
EPS = 1e-5
MASKED = -1e30
GELU_A, GELU_B = math.sqrt(2 / math.pi), 0.044715 * math.sqrt(2 / math.pi)

PACKS = {
    "tok": {"w_patch": (128, KCH * D), "pos": (128, NTOK), "b_patch": (128, 1), "w_cs": (128, DC + DS),
            "b_cs": (NTOK, DC + DS), "w_emb": (DC + 1, D), "ident": (128, 128), "ln_g": (128, 1),
            "ln_b": (128, 1), "w_out": (128, D), "b_out": (1, D), "ones": (1, 128)},
    "at0": {"w_down": (128, RQ + RKV), "q_g": (RQ, 1), "q_b": (RQ, 1), "kv_g": (RKV, 1), "kv_b": (RKV, 1),
            "w_q": (RQ, 256), "w_k": (RKV, 256), "w_kr": (128, 256), "w_v": (RKV, D), "w_o": (128, D),
            "rope_q": (128, S), "rope_k": (128, S), "mask": (S, S)},
    "moe": {"sel": (128, E0), "iota": (S, E0), "keys": (128, E0 * H0), "values": (128, E0 * D)},
    "at1": {"w_q": (128, 256), "w_k": (128, 256), "w_v": (128, D), "w_o": (128, D), "b_o": (1, D)},
    "pk": {"w_q": (128, PH * 128), "b_q": (128, PH), "keys": (128, PH * NE), "iota": (S, TOPK)},
}


def columns(pack):
    at, out = 0, {}
    for name, (_, n) in PACKS[pack].items():
        out[name] = at
        at += n
    return out, at


class Signal:

    def __init__(self, sem, per, credit=0):
        self.sem, self.per, self.credit = sem, per, credit

    def at(self, pair, n):
        return pair * self.per + (n + self.credit)


class Chain:

    def __init__(self, steps, pair):
        self.steps, self.pair, self.n, self.sem = steps, pair, 0, steps.sem

    def after(self, n):
        self.n += n
        assert self.n <= self.steps.per
        return self.steps.at(self.pair, self.n)

    def end(self):
        assert self.n == self.steps.per, (self.n, self.steps.per)


def fusion_program(nc, patches, txt, packs, rows, out):
    ctx = ExitStack()
    with ctx:
        def sb(name, shape, dt=F32):
            return ctx.enter_context(nc.sbuf_tensor("s_" + name, shape, dt))

        def signal(name, per, credit=0):
            return Signal(ctx.enter_context(nc.semaphore(name)), per, credit)

        where, packed = {}, {}
        for pack in PACKS:
            cols, width = columns(pack)
            packed[pack] = sb("w_" + pack, [128, width])
            for name, (r, n) in PACKS[pack].items():
                where[pack, name] = packed[pack][0:r, cols[name]:cols[name] + n]

        def W(pack, name):
            return where[pack, name]

        ident = W("tok", "ident")
        posb = sb("posb", [128, NTOK])

        pT = sb("patches", [128, KCH, 2 * NTOK])
        xT = sb("xT", [128, 2, NTOK])
        cs = sb("cs", [NTOK, 2, DC + DS])
        sq = sb("sq", [NTOK, 2, DS])
        ck = sb("ck", [NTOK, 2, DC + 1])
        ckT = sb("ckT", [DC + 1, 2, NTOK])
        xnT = sb("xnT", [128, 2, NTOK])
        h0, h1, h2 = (sb(f"h{n}", [S, 2, D]) for n in range(3))
        h3 = h1
        stats = sb("stats", [S, 4, 6])
        mv = sb("mv", [S, 4, 2])
        rs = sb("rs", [S, 4, 4])
        hn = sb("hn", [S, 2, D])
        xn = hn[0:NTOK, :, :]
        hnT = sb("hnT", [128, 2, S])
        cn = sb("cn", [S, 2, RQ + RKV])
        cqT = sb("cqT", [RQ, 2, S])
        ckvT = sb("ckvT", [RKV, 2, S])
        qT = sb("qT", [128, 2, 2, S])
        kT = sb("kT", [128, 2, 2, S])
        vA = sb("vA", [S, 2 * HEADS, DH + 1])
        mx = sb("mx", [S, 2 * HEADS])
        nmx = sb("nmx", [S, 2 * HEADS])
        prob = sb("prob", [S, 2 * HEADS, S])
        probT = sb("probT", [S, 2 * HEADS, S])
        rden = sb("rden", [S, 2 * HEADS, 1])
        o = sb("o", [S, 2 * HEADS, DH])
        oT = sb("oT", [128, 2, S])
        el = sb("el", [S, 2, E0])
        sel = sb("sel", [S, 2, E0])
        selmax = sb("selmax", [S, 2, 8])
        selidx = sb("selidx", [S, 2, 8], U32)
        selidf = sb("selidf", [S, 2, 8])
        wm = sb("wm", [S, 2, 2, E0])
        wmoe = sb("wmoe", [S, 2, E0])
        hid = sb("hid", [S, 2, EG * H0])
        hidT = sb("hidT", [128, 2, EG, S])
        qhT = sb("qhT", [128, PH, 2, S])
        s8 = sb("s8", [S, 2, PH, 2, TOPK])
        i8 = sb("i8", [S, 2, PH, 2, TOPK], U32)
        i8f = sb("i8f", [S, 2, PH, 2, TOPK])
        sums = sb("sums", [S, 2 * PH, TOPK, TOPK])
        best = sb("best", [S, 2 * PH, TOPK])
        bpos = sb("bpos", [S, 2 * PH, TOPK], U32)
        half_ = [sb(f"pos{n}", [S, 2 * PH, TOPK], U32) for n in range(2)]
        halff = [sb(f"posf{n}", [S, 2 * PH, TOPK]) for n in range(2)]
        onehot = probT[:, 0:8, :].rearrange("p a b -> p (a b)")[:, 0:2 * PH * TOPK * TOPK // 2]
        picked = [sb(f"picked{n}", [S, 2 * PH, TOPK]) for n in range(2)]
        idxf = sb("idxf", [S, 2, KPT])
        ez = sb("ez", [S, 2 * PH, TOPK])
        esum = sb("esum", [S, 2 * PH, 1])
        wnext = sb("wnext", [S, 2, KPT])
        qnext = sb("qnext", [S, 2, D])

        idx = sb("idx", [128, 2, KPT], U32)
        ring = sb("ring", [128, SLOTS, QK, 2 * D])
        wcur = sb("wcur", [S, 2, KPT])
        qcur = sb("qcur", [S, 2, D])
        hcur = sb("hcur", [S, 2, D])
        xd = sb("xd", [S, 2, QK])
        ga = sb("ga", [S, 2, QK])
        gb = sb("gb", [S, 2, QK])
        gu = sb("gu", [S, 2, QK])
        gt = sb("gt", [S, 2, QK])
        gv = sb("gv", [S, 2, QK])
        val = sb("val", [S, 2, QK])
        diag = sb("diag", [S, 2, QK, S])
        y = sb("y", [S, 2, D])

        ps = ctx.enter_context(nc.psum_tensor("ps", [128, 8, 512], F32))

        def bank(n, rows_, width):
            return ps[0:rows_, n, 0:width]

        loaded = {pack: signal("loaded_" + pack, 0) for pack in PACKS}
        consts = signal("consts", 0)
        passed_pool, passed_pe, passed_dve = (
            ctx.enter_context(nc.semaphore("passed_" + e)) for e in ("pool", "pe", "dve"))
        posb_ready = signal("posb_ready", 0)
        patches_in = signal("patches_in", 16)
        txt_in = signal("txt_in", 16)
        xT_mm = signal("xT_mm", 1)
        xT_sb = signal("xT_sb", 1)
        cs_mm = signal("cs_mm", 1)
        ck_sb = signal("ck_sb", 1)
        ckT_mm = signal("ckT_mm", 1)
        ckT_sb = signal("ckT_sb", 1)
        xenh_mm = signal("xenh_mm", 1)
        xn_sb = signal("xn_sb", 1)
        xnT_mm = signal("xnT_mm", 1)
        xnT_sb = signal("xnT_sb", 1)
        h0_mm = signal("h0_mm", 1)
        hn_sb = signal("hn_sb", 4)
        hnT_mm = signal("hnT_mm", 4)
        hnT_sb = signal("hnT_sb", 4)
        down_mm = signal("down_mm", 1)
        cn_sb = signal("cn_sb", 1)
        cT_mm = signal("cT_mm", 1)
        cT_sb = signal("cT_sb", 1)
        qkv_mm = [signal(f"qkv_mm{n}", 3) for n in range(2)]
        qk_sb = [signal(f"qk_sb{n}", 2) for n in range(2)]
        v_sb = [signal(f"v_sb{n}", 1) for n in range(2)]
        score_mm = [signal(f"score_mm{n}", 1) for n in range(2)]
        nmx_sb = [signal(f"nmx_sb{n}", 2) for n in range(2)]
        exp_sb = [signal(f"exp_sb{n}", 4) for n in range(2)]
        probT_mm = [signal(f"probT_mm{n}", 4) for n in range(2)]
        probT_sb = [signal(f"probT_sb{n}", 4) for n in range(2)]
        pv_mm = [signal(f"pv_mm{n}", 1) for n in range(2)]
        o_sb = [signal(f"o_sb{n}", 1) for n in range(2)]
        oT_mm = [signal(f"oT_mm{n}", 1) for n in range(2)]
        oT_sb = [signal(f"oT_sb{n}", 1) for n in range(2)]
        out_mm = [signal(f"out_mm{n}", 1) for n in range(2)]
        h1_sb = signal("h1_sb", 1)
        logit_mm = signal("logit_mm", 1)
        el_sb = signal("el_sb", 1)
        hid_mm = signal("hid_mm", STEPS)
        hid_sb = signal("hid_sb", STEPS)
        hidT_mm = signal("hidT_mm", STEPS)
        hidT_sb = signal("hidT_sb", STEPS)
        moe_mm = signal("moe_mm", STEPS)
        qh_mm = signal("qh_mm", PH // 2)
        qh_sb = signal("qh_sb", PH // 2)
        sub_mm = signal("sub_mm", 4)
        sub_read = signal("sub_read", 4)
        dif_sb = signal("dif_sb", 1)
        ez_sb = signal("ez_sb", 1)
        idx_ready = [signal(f"idx_ready{n}", 1) for n in range(2)]
        gathered = [signal(f"gathered{n}", 2 * 16 * QK) for n in range(SLOTS)]
        gu_sb = signal("gu_sb", QUARTERS)
        gt_sb = signal("gt_sb", QUARTERS)
        val_sb = signal("val_sb", QUARTERS)
        diag_sb = signal("diag_sb", QUARTERS)
        up_mm = signal("up_mm", QUARTERS, credit=QUARTERS)
        y_sb = signal("y_sb", 2, credit=2)
        stored = [signal(f"stored{n}", 16, credit=16) for n in range(2)]
        v_front = signal("v_front", 211)
        v_expert = signal("v_expert", 3 + QUARTERS * (QK + 3))

        block = ctx.enter_context(nc.Block())

        NQ, HQ = QUARTERS, QUARTERS // 2

        @block.gpsimd
        def _(pool):
            with pool.Fori(0, PAIRS) as pair:
                for k in range(NQ):
                    if k % HQ == 0:
                        pool.wait_ge(idx_ready[k // HQ].sem, idx_ready[k // HQ].at(pair, 1))
                        pool.sem_inc(passed_pool, 1)
                    pool.wait_ge(up_mm.sem, up_mm.at(pair, k - SLOTS + 1))
                    pool.sem_inc(passed_pool, 1)
                    for r in range(QK):
                        col = (k % HQ) * QK + r
                        pool.indirect_dma_start(
                            ring[:, k % SLOTS, r, :], None, rows,
                            bass.IndirectOffsetOnAxis(ap=idx[:, k // HQ, col:col + 1], axis=0),
                        ).then_inc(gathered[k % SLOTS].sem, 16)

        @block.sync
        def _(sp):
            def load(pair):
                sp.wait_ge(xT_mm.sem, xT_mm.at(pair, 0))
                sp.dma_start(pT[:, :, :].rearrange("p c t -> p (c t)"),
                             patches[bass.ds(pair, 1), :, :].rearrange("a p n -> p (a n)")
                             ).then_inc(patches_in.sem, 16)
                sp.wait_ge(h1_sb.sem, h1_sb.at(pair, 0))
                sp.dma_start(h0[NTOK:S, :, :],
                             txt[bass.ds(pair * 2, 2), :, :].rearrange("j s d -> s j d")
                             ).then_inc(txt_in.sem, 16)

            def store(pair):
                for j in range(2):
                    sp.wait_ge(y_sb.sem, y_sb.at(pair, j + 1))
                    sp.dma_start(out[bass.ds(pair * 2 + j, 1), :, :].rearrange("a s d -> s (a d)"),
                                 y[:, j, :]).then_inc(stored[j].sem, 16)

            sp.dma_start(packed["tok"][:, :], packs["tok"]).then_inc(loaded["tok"].sem, 16)
            load(0)
            sp.dma_start(packed["at0"][:, :], packs["at0"]).then_inc(loaded["at0"].sem, 16)
            sp.dma_start(packed["moe"][:, :], packs["moe"]).then_inc(loaded["moe"].sem, 16)
            sp.dma_start(packed["at1"][:, :], packs["at1"]).then_inc(loaded["at1"].sem, 16)
            sp.dma_start(packed["pk"][:, :], packs["pk"]).then_inc(loaded["pk"].sem, 16)
            sp.sem_inc(stored[0].sem, 16)
            sp.sem_inc(stored[1].sem, 16)
            load(1)
            with sp.Fori(2, PAIRS) as pair:
                load(pair)
                store(pair - 2)
            store(PAIRS - 2)
            store(PAIRS - 1)
            for j in range(2):
                sp.wait_ge(stored[j].sem, stored[j].at(PAIRS - 1, 16))

        @block.tensor
        def _(pe):
            def mm(out_, lhsT, rhs, start=True, stop=True):
                return pe.matmul(out_, lhsT, rhs, start=start, stop=stop)

            def hn_transpose(pair, n, src):
                pe.wait_ge(hn_sb.sem, hn_sb.at(pair, n))
                for j in range(2):
                    last = pe.transpose(ps[0:128, 4, j * S:(j + 1) * S], src[:, j, :], ident[0:S, 0:S])
                last.then_inc(hnT_mm.sem, 1)

            def tok_a(pair):
                if isinstance(pair, int):
                    pe.wait_ge(loaded["tok"].sem, 16)
                pe.wait_ge(patches_in.sem, patches_in.at(pair, 16))
                pe.wait_ge(sub_read.sem, sub_read.at(pair, 0))
                for c in range(KCH):
                    last = mm(bank(0, 128, 2 * NTOK), W("tok", "w_patch")[:, c * D:(c + 1) * D],
                              pT[:, c, :], c == 0, c == KCH - 1)
                last.then_inc(xT_mm.sem, 1)
                pe.wait_ge(xT_sb.sem, xT_sb.at(pair, 1))
                for j in range(2):
                    last = mm(ps[0:NTOK, 1, j * 12:(j + 1) * 12], xT[:, j, :], W("tok", "w_cs"))
                last.then_inc(cs_mm.sem, 1)
                pe.wait_ge(ck_sb.sem, ck_sb.at(pair, 1))
                pe.sem_inc(passed_pe, 1)
                for j in range(2):
                    last = pe.transpose(ps[0:DC + 1, 2, j * NTOK:(j + 1) * NTOK], ck[:, j, :],
                                        ident[0:NTOK, 0:NTOK])
                last.then_inc(ckT_mm.sem, 1)

            def tok_b(pair):
                pe.wait_ge(ckT_sb.sem, ckT_sb.at(pair, 1))
                for j in range(2):
                    o_ = ps[0:NTOK, 3, j * D:(j + 1) * D]
                    mm(o_, xT[:, j, :], ident, True, False)
                    last = mm(o_, ckT[:, j, :], W("tok", "w_emb"), False, True)
                last.then_inc(xenh_mm.sem, 1)
                pe.wait_ge(xn_sb.sem, xn_sb.at(pair, 1))
                pe.sem_inc(passed_pe, 1)
                for j in range(2):
                    last = pe.transpose(ps[0:128, 4, j * NTOK:(j + 1) * NTOK], xn[:, j, :],
                                        ident[0:NTOK, 0:NTOK])
                last.then_inc(xnT_mm.sem, 1)
                pe.wait_ge(xnT_sb.sem, xnT_sb.at(pair, 1))
                for j in range(2):
                    o_ = ps[0:NTOK, 5, j * D:(j + 1) * D]
                    mm(o_, xnT[:, j, :], W("tok", "w_out"), True, False)
                    last = mm(o_, W("tok", "ones")[:, 0:NTOK], W("tok", "b_out"), False, True)
                last.then_inc(h0_mm.sem, 1)

            def at0_down(pair):
                hn_transpose(pair, 1, hn)
                if isinstance(pair, int):
                    pe.wait_ge(loaded["at0"].sem, 16)
                pe.wait_ge(hnT_sb.sem, hnT_sb.at(pair, 1))
                for j in range(2):
                    last = mm(ps[0:S, 6, j * 149:(j + 1) * 149], hnT[:, j, :], W("at0", "w_down"))
                last.then_inc(down_mm.sem, 1)
                pe.wait_ge(cn_sb.sem, cn_sb.at(pair, 1))
                pe.sem_inc(passed_pe, 1)
                for j in range(2):
                    pe.transpose(ps[0:RQ, 5, j * S:(j + 1) * S], cn[:, j, 0:RQ], ident[0:S, 0:S])
                    last = pe.transpose(ps[0:RKV, 5, (2 + j) * S:(3 + j) * S], cn[:, j, RQ:RQ + RKV],
                                        ident[0:S, 0:S])
                last.then_inc(cT_mm.sem, 1)

            def at0_qkv(pair):
                pe.wait_ge(cT_sb.sem, cT_sb.at(pair, 1))
                for g in range(2):
                    last = mm(ps[:, 5, g * 2 * S:(g + 1) * 2 * S], W("at0", "w_q")[:, g * 128:(g + 1) * 128],
                              cqT[:, :, :])
                last.then_inc(qkv_mm[0].sem, 1)
                for g in range(2):
                    o_ = ps[:, 6, g * 2 * S:(g + 1) * 2 * S]
                    mm(o_, W("at0", "w_k")[:, g * 128:(g + 1) * 128], ckvT[:, :, :], True, False)
                    last = mm(o_, W("at0", "w_kr")[:, g * 128:(g + 1) * 128], hnT[:, :, :], False, True)
                last.then_inc(qkv_mm[0].sem, 1)
                for j in range(2):
                    last = mm(ps[0:S, 4, j * D:(j + 1) * D], ckvT[:, j, :], W("at0", "w_v"))
                last.then_inc(qkv_mm[0].sem, 1)

            def at1_qkv(pair):
                hn_transpose(pair, 3, hn)
                if isinstance(pair, int):
                    pe.wait_ge(loaded["at1"].sem, 16)
                pe.wait_ge(hnT_sb.sem, hnT_sb.at(pair, 3))
                for b, w in ((5, "w_q"), (6, "w_k")):
                    for g in range(2):
                        last = mm(ps[:, b, g * 2 * S:(g + 1) * 2 * S], W("at1", w)[:, g * 128:(g + 1) * 128],
                                  hnT[:, :, :])
                    last.then_inc(qkv_mm[1].sem, 1)
                for j in range(2):
                    last = mm(ps[0:S, 4, j * D:(j + 1) * D], hnT[:, j, :], W("at1", "w_v"))
                last.then_inc(qkv_mm[1].sem, 1)

            def scores(pair, n):
                pe.wait_ge(qk_sb[n].sem, qk_sb[n].at(pair, 2))
                if n == 0:
                    for b in range(4):
                        mm(ps[0:S, b, 0:HB * S].rearrange("p (h s) -> p h s", h=HB), ident[0:S, 0:S],
                           W("at0", "mask").unsqueeze(1).broadcast_to([S, HB, S]), True, False)
                for c, (j, g) in enumerate(SLOT_OF):
                    for b in range(4):
                        r = HROWS * b
                        last = mm(ps[0:S, b, c * S:(c + 1) * S], qT[r:r + HROWS, g, j, :],
                                  kT[r:r + HROWS, g, j, :], n == 1, n == 1 or c == 3)
                last.then_inc(score_mm[n].sem, 1)

            def attend(pair, n):
                for b in range(4):
                    pe.wait_ge(exp_sb[n].sem, exp_sb[n].at(pair, b + 1))
                    for h in range(HB):
                        last = pe.transpose(ps[0:S, b, h * S:(h + 1) * S], prob[:, b * HB + h, :],
                                            ident[0:S, 0:S])
                    last.then_inc(probT_mm[n].sem, 1)
                pe.wait_ge(v_sb[n].sem, v_sb[n].at(pair, 1))
                for b in range(4):
                    pe.wait_ge(probT_sb[n].sem, probT_sb[n].at(pair, b + 1))
                    for c, (j, g) in enumerate(SLOT_OF):
                        h = j * HEADS + g * HB + b
                        last = mm(ps[0:S, 4, h * (DH + 1):(h + 1) * (DH + 1)], probT[:, b * HB + c, :], vA[:, h, :])
                last.then_inc(pv_mm[n].sem, 1)
                pe.wait_ge(o_sb[n].sem, o_sb[n].at(pair, 1))
                for j in range(2):
                    last = pe.transpose(ps[0:128, 5, j * S:(j + 1) * S],
                                        o[:, j * HEADS:(j + 1) * HEADS, :].rearrange("p h d -> p (h d)"),
                                        ident[0:S, 0:S])
                last.then_inc(oT_mm[n].sem, 1)
                pe.wait_ge(oT_sb[n].sem, oT_sb[n].at(pair, 1))
                for j in range(2):
                    o_ = ps[0:S, 6, j * D:(j + 1) * D]
                    last = mm(o_, oT[:, j, :], W(f"at{n}", "w_o"), True, n == 0)
                    if n == 1:
                        last = mm(o_, W("tok", "ones")[:, 0:S], W("at1", "b_o"), False, True)
                last.then_inc(out_mm[n].sem, 1)

            def moe_logits(pair):
                hn_transpose(pair, 2, hn)
                if isinstance(pair, int):
                    pe.wait_ge(loaded["moe"].sem, 16)
                pe.wait_ge(hnT_sb.sem, hnT_sb.at(pair, 2))
                for j in range(2):
                    last = mm(ps[0:S, 5, j * E0:(j + 1) * E0], hnT[:, j, :], W("moe", "sel"))
                last.then_inc(logit_mm.sem, 1)

            def moe_steps(pair, first, last_):
                for n in range(first, last_):
                    if n < STEPS:
                        if n >= 2:
                            pe.wait_ge(hid_sb.sem, hid_sb.at(pair, n - 1))
                        e = n % (STEPS // 2) * EG
                        mm(bank(n % 2, S, EG * H0), hnT[:, n // (STEPS // 2), :],
                           W("moe", "keys")[:, e * H0:(e + EG) * H0]).then_inc(hid_mm.sem, 1)
                    m = n - 1
                    if 0 <= m < STEPS:
                        pe.wait_ge(hid_sb.sem, hid_sb.at(pair, m + 1))
                        if m >= 2:
                            pe.wait_ge(hidT_sb.sem, hidT_sb.at(pair, m - 1))
                        for q in range(EG):
                            last = pe.transpose(ps[0:128, 2 + m % 2, q * S:(q + 1) * S],
                                                hid[:, m % 2, q * H0:(q + 1) * H0], ident[0:S, 0:S])
                        last.then_inc(hidT_mm.sem, 1)
                    m = n - 2
                    if 0 <= m < STEPS:
                        pe.wait_ge(hidT_sb.sem, hidT_sb.at(pair, m + 1))
                        j, e = m // (STEPS // 2), m % (STEPS // 2) * EG
                        for q in range(EG):
                            last = mm(ps[0:S, 6, j * D:(j + 1) * D], hidT[:, m % 2, q, :],
                                      W("moe", "values")[:, (e + q) * D:(e + q + 1) * D],
                                      e + q == 0, e + q == E0 - 1)
                        last.then_inc(moe_mm.sem, 1)

            def pk_queries(pair):
                hn_transpose(pair, 4, qnext)
                if isinstance(pair, int):
                    pe.wait_ge(loaded["pk"].sem, 16)
                pe.wait_ge(hnT_sb.sem, hnT_sb.at(pair, 4))
                for m in range(PH // 2):
                    if m >= 2:
                        pe.wait_ge(qh_sb.sem, qh_sb.at(pair, m - 1))
                    for h in (2 * m, 2 * m + 1):
                        last = mm(ps[:, 5 + m % 2, (h % 2) * 2 * S:(h % 2 + 1) * 2 * S],
                                  W("pk", "w_q")[:, h * 128:(h + 1) * 128], hnT[:, :, :])
                    last.then_inc(qh_mm.sem, 1)
                pk_scores(pair, 0)

            def pk_scores(pair, j):
                for m in range(2):
                    if j == 0:
                        pe.wait_ge(qh_sb.sem, qh_sb.at(pair, 2 * m + 2))
                    else:
                        pe.wait_ge(sub_read.sem, sub_read.at(pair, m + 1))
                    for q in range(4):
                        h = 4 * m + q
                        for c in range(2):
                            last = mm(ps[0:S, 2 * m + c, q * NE:(q + 1) * NE],
                                      qhT[c * HALF:(c + 1) * HALF, h, j, :],
                                      W("pk", "keys")[c * HALF:(c + 1) * HALF, h * NE:(h + 1) * NE])
                    last.then_inc(sub_mm.sem, 1)

            def expert_up(pair, k):
                j = k // HQ
                pe.wait_ge(diag_sb.sem, diag_sb.at(pair, k + 1))
                if k % HQ == 0:
                    pe.wait_ge(y_sb.sem, y_sb.at(pair, j - 1))
                for r in range(QK):
                    last = mm(ps[0:S, 7, j * D:(j + 1) * D], diag[:, k % 2, r, :],
                              ring[0:S, k % SLOTS, r, D:2 * D],
                              k % HQ == 0 and r == 0, k % HQ == HQ - 1 and r == QK - 1)
                last.then_inc(up_mm.sem, 1)

            pe.sem_inc(up_mm.sem, NQ)

            def front(pair, ups):
                tok_a(pair)
                tok_b(pair)
                at0_down(pair)
                at0_qkv(pair)
                scores(pair, 0)
                attend(pair, 0)
                moe_logits(pair)
                ups(0)
                moe_steps(pair, 0, 4)
                moe_steps(pair, 4, 8)
                ups(1)
                moe_steps(pair, 8, 12)
                moe_steps(pair, 12, STEPS + 2)
                ups(2)
                at1_qkv(pair)
                scores(pair, 1)
                ups(3)
                attend(pair, 1)
                pk_queries(pair)
                ups(4)
                pk_scores(pair, 1)
                ups(5)

            front(0, lambda k: None)
            with pe.Fori(1, PAIRS) as pair:
                front(pair, lambda k: expert_up(pair - 1, k))
                expert_up(pair - 1, 6)
                expert_up(pair - 1, 7)
            for k in range(NQ):
                expert_up(PAIRS - 1, k)

        @block.scalar
        def _(act):
            def copy(out_, in_):
                return act.activation(out_, in_, ACT.Copy)

            def hn_evac(pair, n):
                act.wait_ge(hnT_mm.sem, hnT_mm.at(pair, n))
                copy(hnT[:, :, :].rearrange("p j s -> p (j s)"), bank(4, 128, 2 * S)).then_inc(hnT_sb.sem, 1)

            def tok_a(pair):
                if isinstance(pair, int):
                    act.wait_ge(loaded["tok"].sem, 16)
                act.wait_ge(ckT_mm.sem, ckT_mm.at(pair, 1))
                copy(ckT[:, :, :].rearrange("p j s -> p (j s)"), bank(2, DC + 1, 2 * NTOK)).then_inc(ckT_sb.sem, 1)

            def tok_b(pair):
                act.wait_ge(xnT_mm.sem, xnT_mm.at(pair, 1))
                act.activation(xnT[:, :, :].rearrange("p j s -> p (j s)"), bank(4, 128, 2 * NTOK), ACT.Identity,
                               scale=W("tok", "ln_g"), bias=W("tok", "ln_b")).then_inc(xnT_sb.sem, 1)

            def at0_latents(pair):
                hn_evac(pair, 1)
                if isinstance(pair, int):
                    act.wait_ge(loaded["at0"].sem, 16)
                act.wait_ge(cT_mm.sem, cT_mm.at(pair, 1))
                act.activation(cqT[:, :, :].rearrange("p j s -> p (j s)"), ps[0:RQ, 5, 0:2 * S], ACT.Identity,
                               scale=W("at0", "q_g"), bias=W("at0", "q_b"))
                act.activation(ckvT[:, :, :].rearrange("p j s -> p (j s)"), ps[0:RKV, 5, 2 * S:4 * S], ACT.Identity,
                               scale=W("at0", "kv_g"), bias=W("at0", "kv_b")).then_inc(cT_sb.sem, 1)

            def values(pair, n):
                act.wait_ge(qkv_mm[n].sem, qkv_mm[n].at(pair, 3))
                copy(vA[:, :, 0:DH], bank(4, S, 2 * D).rearrange("p (h d) -> p h d", d=DH)).then_inc(v_sb[n].sem, 1)

            def exps(pair, n):
                scale = 1.0 / math.sqrt(DH + 2 * (1 - n))
                for q in range(2):
                    act.wait_ge(nmx_sb[n].sem, nmx_sb[n].at(pair, q + 1))
                    for h in range(HEADS):
                        b, g = 2 * q + h // HB, q * HEADS + h
                        last = act.activation(prob[:, g, :], ps[0:S, b, (h % HB) * S:(h % HB + 1) * S], ACT.Exp,
                                              scale=scale, bias=nmx[:, g:g + 1])
                        if h % HB == HB - 1:
                            last.then_inc(exp_sb[n].sem, 1)

            def attend(pair, n):
                for b in range(4):
                    act.wait_ge(probT_mm[n].sem, probT_mm[n].at(pair, b + 1))
                    copy(probT[:, b * HB:(b + 1) * HB, :].rearrange("p h s -> p (h s)"),
                         bank(b, S, HB * S)).then_inc(probT_sb[n].sem, 1)
                act.wait_ge(oT_mm[n].sem, oT_mm[n].at(pair, 1))
                copy(oT[:, :, :].rearrange("p j s -> p (j s)"), bank(5, 128, 2 * S)).then_inc(oT_sb[n].sem, 1)

            def moe_router(pair):
                hn_evac(pair, 2)
                act.wait_ge(logit_mm.sem, logit_mm.at(pair, 1))
                act.activation(el[:, :, :].rearrange("p j e -> p (j e)"), bank(5, S, 2 * E0), ACT.Exp,
                               scale=-1.0).then_inc(el_sb.sem, 1)

            def moe_steps(pair, first, last_):
                for n in range(first, last_):
                    act.wait_ge(hidT_mm.sem, hidT_mm.at(pair, n + 1))
                    if n >= 2:
                        act.wait_ge(moe_mm.sem, moe_mm.at(pair, n - 1))
                    copy(hidT[:, n % 2, :, :].rearrange("p e s -> p (e s)"),
                         bank(2 + n % 2, 128, EG * S)).then_inc(hidT_sb.sem, 1)

            def at1_qk(pair):
                hn_evac(pair, 3)
                for n, (t, b) in enumerate(((qT, 5), (kT, 6))):
                    act.wait_ge(qkv_mm[1].sem, qkv_mm[1].at(pair, n + 1))
                    copy(t[:, :, :, :].rearrange("p g j s -> p (g j s)"), bank(b, 128, 4 * S)).then_inc(qk_sb[1].sem, 1)
                values(pair, 1)

            def pk_queries(pair):
                hn_evac(pair, 4)
                if isinstance(pair, int):
                    act.wait_ge(loaded["pk"].sem, 16)
                for m in range(PH // 2):
                    act.wait_ge(qh_mm.sem, qh_mm.at(pair, m + 1))
                    for h in (2 * m, 2 * m + 1):
                        last = act.activation(qhT[:, h, :, :].rearrange("p j s -> p (j s)"),
                                              ps[:, 5 + m % 2, (h % 2) * 2 * S:(h % 2 + 1) * 2 * S], ACT.Identity,
                                              bias=W("pk", "b_q")[:, h:h + 1])
                    last.then_inc(qh_sb.sem, 1)

            def pk_softmax(pair):
                act.wait_ge(dif_sb.sem, dif_sb.at(pair, 1))
                act.activation(ez[:, :, :].rearrange("p h k -> p (h k)"), ez[:, :, :].rearrange("p h k -> p (h k)"),
                               ACT.Exp).then_inc(ez_sb.sem, 1)

            def expert_tanh(pair, k):
                act.wait_ge(gu_sb.sem, gu_sb.at(pair, k + 1))
                act.activation(gt[:, k % 2, :], gu[:, k % 2, :], ACT.Tanh).then_inc(gt_sb.sem, 1)

            def expert_diag(pair, k):
                act.wait_ge(val_sb.sem, val_sb.at(pair, k + 1))
                act.wait_ge(up_mm.sem, up_mm.at(pair, k - 1))
                for r in range(QK):
                    last = act.activation(diag[:, k % 2, r, :], ident[0:S, 0:S], ACT.Copy,
                                          scale=val[:, k % 2, r:r + 1])
                last.then_inc(diag_sb.sem, 1)

            def front(pair, tanh, diags):
                tok_a(pair)
                tok_b(pair)
                at0_latents(pair)
                values(pair, 0)
                exps(pair, 0)
                tanh(0)
                attend(pair, 0)
                diags(0)
                moe_router(pair)
                tanh(1)
                moe_steps(pair, 0, 3)
                diags(1)
                moe_steps(pair, 3, 7)
                tanh(2)
                moe_steps(pair, 7, 11)
                diags(2)
                moe_steps(pair, 11, STEPS)
                tanh(3)
                at1_qk(pair)
                diags(3)
                exps(pair, 1)
                tanh(4)
                attend(pair, 1)
                diags(4)
                pk_queries(pair)
                tanh(5)
                diags(5)
                pk_softmax(pair)
                tanh(6)

            front(0, lambda k: None, lambda k: None)
            with act.Fori(1, PAIRS) as pair:
                front(pair, lambda k: expert_tanh(pair - 1, k), lambda k: expert_diag(pair - 1, k))
                expert_diag(pair - 1, 6)
                expert_tanh(pair - 1, 7)
                expert_diag(pair - 1, 7)
            for k in range(NQ):
                expert_tanh(PAIRS - 1, k)
                expert_diag(PAIRS - 1, k)

        @block.vector
        def _(dve):
            def rstd(c, n, np_):
                v, y_, a, b = (rs[0:np_, 0:n, q] for q in range(4))
                dve.tensor_scalar(v, mv[0:np_, 0:n, 1], EPS, None, ALU.add).then_inc(c.sem, 1)
                dve.wait_ge(c.sem, c.after(1))
                dve.tensor_scalar(y_.bitcast(I32), v.bitcast(I32), -0.5, 1597463007.0, ALU.mult, ALU.add).then_inc(c.sem, 1)
                dve.wait_ge(c.sem, c.after(1))
                for _ in range(3):
                    dve.scalar_tensor_tensor(a, y_, -0.5, y_, ALU.mult, ALU.mult).then_inc(c.sem, 1)
                    dve.wait_ge(c.sem, c.after(1))
                    dve.tensor_tensor(b, a, v, ALU.mult).then_inc(c.sem, 1)
                    dve.wait_ge(c.sem, c.after(1))
                    dve.scalar_tensor_tensor(y_, b, 1.5, y_, ALU.add, ALU.mult).then_inc(c.sem, 1)
                    dve.wait_ge(c.sem, c.after(1))

            def norm(c, srcs, dsts, sig):
                np_ = srcs[0].shape[0]
                for n, src in enumerate(srcs):
                    dve.bn_stats(stats[0:np_, n, :], src).then_inc(c.sem, 1)
                dve.wait_ge(c.sem, c.after(len(srcs)))
                dve.sem_inc(passed_dve, 1)
                for n in range(len(srcs)):
                    dve.bn_aggr(mv[0:np_, n, :], stats[0:np_, n, :]).then_inc(c.sem, 1)
                dve.wait_ge(c.sem, c.after(len(srcs)))
                rstd(c, len(srcs), np_)
                for n, (src, dst) in enumerate(zip(srcs, dsts)):
                    last = dve.tensor_scalar(dst, src, mv[0:np_, n, 0:1], rs[0:np_, n, 1:2], ALU.subtract, ALU.mult)
                last.then_inc(sig.sem, 1)

            def norm_h(c, h, dst, n=0):
                norm(c, [h[:, j, :] for j in range(2)], [dst[:, j, :] for j in range(2)], hn_sb)

            def tok_a(c, pair):
                dve.wait_ge(xT_mm.sem, xT_mm.at(pair, 1))
                dve.tensor_tensor(xT[:, :, :], bank(0, 128, 2 * NTOK).rearrange("p (j t) -> p j t", j=2),
                                  posb[:, :].unsqueeze(1).broadcast_to([128, 2, NTOK]), ALU.add
                                  ).then_inc(xT_sb.sem, 1)
                dve.wait_ge(cs_mm.sem, cs_mm.at(pair, 1))
                dve.tensor_tensor(cs[:, :, :], bank(1, NTOK, 24).rearrange("p (j t) -> p j t", j=2),
                                         W("tok", "b_cs").unsqueeze(1).broadcast_to([NTOK, 2, 12]), ALU.add).then_inc(c.sem, 1)
                dve.wait_ge(c.sem, c.after(1))
                dve.tensor_tensor(sq[:, :, :], cs[:, :, DC:], cs[:, :, DC:], ALU.mult).then_inc(c.sem, 1)
                dve.wait_ge(c.sem, c.after(1))
                dve.tensor_reduce(ck[:, :, DC:DC + 1], sq[:, :, :], AXX, ALU.add).then_inc(c.sem, 1)
                dve.wait_ge(c.sem, c.after(1))
                dve.tensor_tensor(ck[:, :, 0:DC], cs[:, :, 0:DC], ck[:, :, DC:DC + 1].broadcast_to([NTOK, 2, DC]),
                                  ALU.mult).then_inc(ck_sb.sem, 1)

            def tok_b(c, pair):
                dve.wait_ge(xenh_mm.sem, xenh_mm.at(pair, 1))
                norm(c, [ps[0:NTOK, 3, j * D:(j + 1) * D] for j in range(2)], [xn[:, j, :] for j in range(2)], xn_sb)
                dve.wait_ge(h0_mm.sem, h0_mm.at(pair, 1))
                dve.tensor_copy(h0[0:NTOK, :, :].rearrange("p j d -> p (j d)"), bank(5, NTOK, 2 * D)).then_inc(c.sem, 1)
                dve.wait_ge(c.sem, c.after(1))
                dve.wait_ge(txt_in.sem, txt_in.at(pair, 16))

            def at0_latents(c, pair):
                norm_h(c, h0, hn)
                dve.wait_ge(down_mm.sem, down_mm.at(pair, 1))
                parts = [(j, a, b) for j in range(2) for a, b in ((0, RQ), (RQ, RQ + RKV))]
                norm(c, [ps[0:S, 6, j * 149 + a:j * 149 + b] for j, a, b in parts],
                     [cn[:, j, a:b] for j, a, b in parts], cn_sb)

            def at0_rope(c, pair):
                for n, (t, b, w) in enumerate(((qT, 5, "rope_q"), (kT, 6, "rope_k"))):
                    dve.wait_ge(qkv_mm[0].sem, qkv_mm[0].at(pair, n + 1))
                    dve.tensor_tensor(t[:, :, :, :].rearrange("p g j s -> p (g j) s"),
                                      bank(b, 128, 4 * S).rearrange("p (a s) -> p a s", s=S),
                                      W("at0", w).unsqueeze(1).broadcast_to([128, 4, S]), ALU.mult
                                      ).then_inc(qk_sb[0].sem, 1)

            def maxima(c, pair, n):
                scale = 1.0 / math.sqrt(DH + 2 * (1 - n))
                for j in range(2):
                    dve.wait_ge(score_mm[n].sem, score_mm[n].at(pair, 1))
                    dve.tensor_reduce(mx[:, j * HEADS:(j + 1) * HEADS],
                                             ps[0:S, 2 * j:2 * j + 2, 0:HB * S].rearrange("p b (h s) -> p b h s", s=S),
                                             AXX, ALU.max).then_inc(c.sem, 1)
                    dve.wait_ge(c.sem, c.after(1))
                    dve.tensor_scalar(nmx[:, j * HEADS:(j + 1) * HEADS], mx[:, j * HEADS:(j + 1) * HEADS],
                                      -scale, None, ALU.mult).then_inc(nmx_sb[n].sem, 1)

            def attend(c, pair, n, h_in, h_out):
                dve.wait_ge(pv_mm[n].sem, pv_mm[n].at(pair, 1))
                pv = bank(4, S, 2 * HEADS * (DH + 1)).rearrange("p (h d) -> p h d", d=DH + 1)
                dve.reciprocal(rden[:, :, :], pv[:, :, DH:DH + 1]).then_inc(c.sem, 1)
                dve.wait_ge(c.sem, c.after(1))
                dve.tensor_tensor(o[:, :, :], pv[:, :, 0:DH], rden[:, :, :].broadcast_to([S, 2 * HEADS, DH]),
                                  ALU.mult).then_inc(o_sb[n].sem, 1)
                dve.wait_ge(out_mm[n].sem, out_mm[n].at(pair, 1))
                add = dve.tensor_tensor(h_out[:, :, :].rearrange("p j d -> p (j d)"),
                                        h_in[:, :, :].rearrange("p j d -> p (j d)"), bank(6, S, 2 * D), ALU.add)
                if n == 0:
                    add.then_inc(h1_sb.sem, 1)
                    dve.wait_ge(h1_sb.sem, h1_sb.at(pair, 1))
                else:
                    add.then_inc(c.sem, 1)
                    dve.wait_ge(c.sem, c.after(1))

            def moe_router(c, pair):
                norm_h(c, h1, hn)
                dve.wait_ge(el_sb.sem, el_sb.at(pair, 1))
                dve.tensor_scalar(el[:, :, :], el[:, :, :], 1.0, None, ALU.add).then_inc(c.sem, 1)
                dve.wait_ge(c.sem, c.after(1))
                dve.reciprocal(sel[:, :, :], el[:, :, :]).then_inc(c.sem, 1)
                dve.wait_ge(c.sem, c.after(1))
                dve.sem_inc(passed_dve, 1)
                for j in range(2):
                    dve.max(selmax[:, j, :], sel[:, j, :]).then_inc(c.sem, 1)
                dve.wait_ge(c.sem, c.after(2))
                dve.sem_inc(passed_dve, 1)
                for j in range(2):
                    dve.max_index(selidx[:, j, :], selmax[:, j, :], sel[:, j, :]).then_inc(c.sem, 1)
                dve.wait_ge(c.sem, c.after(2))
                dve.tensor_copy(selidf[:, :, :], selidx[:, :, :]).then_inc(c.sem, 1)
                dve.wait_ge(c.sem, c.after(1))
                for j in range(2):
                    for t in range(2):
                        dve.tensor_scalar(wm[:, t, j, :], W("moe", "iota"), selidf[:, j, t:t + 1],
                                                 selmax[:, j, t:t + 1], ALU.is_equal, ALU.mult).then_inc(c.sem, 1)
                dve.wait_ge(c.sem, c.after(4))
                dve.tensor_tensor(wmoe[:, :, :], wm[:, 0, :, :], wm[:, 1, :, :], ALU.add).then_inc(c.sem, 1)
                dve.wait_ge(c.sem, c.after(1))

            def moe_steps(c, pair, first, last_):
                for n in range(first, last_):
                    j, e = n // (STEPS // 2), n % (STEPS // 2) * EG
                    dve.wait_ge(hid_mm.sem, hid_mm.at(pair, n + 1))
                    if n >= 2:
                        dve.wait_ge(hidT_mm.sem, hidT_mm.at(pair, n - 1))
                    dve.scalar_tensor_tensor(hid[:, n % 2, :].rearrange("p (e h) -> p e h", e=EG),
                                             bank(n % 2, S, EG * H0).rearrange("p (e h) -> p e h", e=EG), 0.0,
                                             wmoe[:, j, e:e + EG].unsqueeze(2).broadcast_to([S, EG, H0]),
                                             ALU.max, ALU.mult).then_inc(hid_sb.sem, 1)

            def at1_norm(c, pair):
                dve.wait_ge(moe_mm.sem, moe_mm.at(pair, STEPS))
                dve.tensor_tensor(h2[:, :, :].rearrange("p j d -> p (j d)"),
                                         h1[:, :, :].rearrange("p j d -> p (j d)"), bank(6, S, 2 * D), ALU.add).then_inc(c.sem, 1)
                dve.wait_ge(c.sem, c.after(1))
                norm_h(c, h2, hn)

            def pk_top(c, pair, j):
                def keys(m):
                    return [(4 * m + q, half, ps[0:S, 2 * m + half, q * NE:(q + 1) * NE])
                            for half in range(2) for q in range(4)]

                def places(m, at):
                    dve.wait_ge(c.sem, at)
                    dve.sem_inc(passed_dve, 1)
                    for h, half, scores in keys(m):
                        last = dve.max_index(i8[:, j, h, half, :], s8[:, j, h, half, :], scores)
                    last.then_inc(sub_read.sem, 1)

                at = []
                for m in range(2):
                    dve.wait_ge(sub_mm.sem, sub_mm.at(pair, j * 2 + m + 1))
                    dve.sem_inc(passed_dve, 1)
                    for h, half, scores in keys(m):
                        dve.max(s8[:, j, h, half, :], scores).then_inc(c.sem, 1)
                    at.append(c.after(8))
                places(0, at[0])
                places(1, at[1])

            def pk_best(c, pair, j):
                hs = slice(j * PH, (j + 1) * PH)
                dve.tensor_tensor(sums[:, hs, :, :],
                                         s8[:, j, :, 0, :].unsqueeze(3).broadcast_to([S, PH, TOPK, TOPK]),
                                         s8[:, j, :, 1, :].unsqueeze(2).broadcast_to([S, PH, TOPK, TOPK]), ALU.add).then_inc(c.sem, 1)
                dve.wait_ge(c.sem, c.after(1))
                dve.sem_inc(passed_dve, 1)
                for h in range(j * PH, (j + 1) * PH):
                    dve.max(best[:, h, :], sums[:, h, :, :].rearrange("p a b -> p (a b)")).then_inc(c.sem, 1)
                dve.wait_ge(c.sem, c.after(PH))
                dve.sem_inc(passed_dve, 1)
                for h in range(j * PH, (j + 1) * PH):
                    dve.max_index(bpos[:, h, :], best[:, h, :], sums[:, h, :, :].rearrange("p a b -> p (a b)")).then_inc(c.sem, 1)
                dve.wait_ge(sub_read.sem, sub_read.at(pair, 2 * j + 2))
                dve.tensor_copy(i8f[:, j, :, :, :].rearrange("p h c k -> p (h c k)"),
                                       i8[:, j, :, :, :].rearrange("p h c k -> p (h c k)")).then_inc(c.sem, 1)
                dve.wait_ge(c.sem, c.after(PH + 1))
                dve.tensor_scalar(half_[0][:, hs, :], bpos[:, hs, :], 3, None, ALU.logical_shift_right).then_inc(c.sem, 1)
                dve.tensor_scalar(half_[1][:, hs, :], bpos[:, hs, :], 7, None, ALU.bitwise_and).then_inc(c.sem, 1)
                dve.wait_ge(c.sem, c.after(2))
                for t in range(2):
                    dve.tensor_copy(halff[t][:, hs, :], half_[t][:, hs, :]).then_inc(c.sem, 1)
                dve.wait_ge(c.sem, c.after(2))
                oh = onehot.rearrange("p (h k a) -> p h k a", h=PH, k=TOPK)
                for t in range(2):
                    dve.tensor_tensor(oh, halff[t][:, hs, :].unsqueeze(3).broadcast_to([S, PH, TOPK, TOPK]),
                                             W("pk", "iota").unsqueeze(1).unsqueeze(1).broadcast_to([S, PH, TOPK, TOPK]),
                                             ALU.is_equal).then_inc(c.sem, 1)
                    dve.wait_ge(c.sem, c.after(1))
                    dve.tensor_tensor(oh, oh,
                                             i8f[:, j, :, t, :].unsqueeze(2).broadcast_to([S, PH, TOPK, TOPK]),
                                             ALU.mult).then_inc(c.sem, 1)
                    dve.wait_ge(c.sem, c.after(1))
                    dve.tensor_reduce(picked[t][:, hs, :], oh, AXX, ALU.add).then_inc(c.sem, 1)
                    dve.wait_ge(c.sem, c.after(1))
                dve.scalar_tensor_tensor(idxf[:, j, :], picked[0][:, hs, :].rearrange("p h k -> p (h k)"),
                                                float(NE), picked[1][:, hs, :].rearrange("p h k -> p (h k)"),
                                                ALU.mult, ALU.add).then_inc(c.sem, 1)
                dve.wait_ge(c.sem, c.after(1))

            def pk_softmax(c, pair):
                dve.tensor_tensor(ez[:, :, :], best[:, :, :], best[:, :, 0:1].broadcast_to([S, 2 * PH, TOPK]),
                                  ALU.subtract).then_inc(dif_sb.sem, 1)
                if not isinstance(pair, int):
                    dve.wait_ge(gathered[SLOTS - 1].sem, gathered[SLOTS - 1].at(pair - 1, 16 * QK))
                dve.tensor_copy(idx[0:S, 0, :], idxf[:, 0, :]).then_inc(idx_ready[0].sem, 1)
                dve.wait_ge(ez_sb.sem, ez_sb.at(pair, 1))
                dve.tensor_reduce(esum[:, :, :], ez[:, :, :], AXX, ALU.add).then_inc(c.sem, 1)
                dve.wait_ge(c.sem, c.after(1))
                dve.reciprocal(esum[:, :, :], esum[:, :, :]).then_inc(c.sem, 1)
                dve.wait_ge(c.sem, c.after(1))
                dve.tensor_tensor(wnext[:, :, :].rearrange("p j (h k) -> p (j h) k", k=TOPK), ez[:, :, :],
                                         esum[:, :, :].broadcast_to([S, 2 * PH, TOPK]), ALU.mult).then_inc(c.sem, 1)
                dve.wait_ge(c.sem, c.after(1))

            def take_over(c, pair):
                dve.tensor_copy(idx[0:S, 1, :], idxf[:, 1, :]).then_inc(idx_ready[1].sem, 1)
                dve.wait_ge(y_sb.sem, y_sb.at(pair, 0))
                dve.tensor_copy(wcur[:, :, :], wnext[:, :, :]).then_inc(c.sem, 1)
                dve.tensor_copy(qcur[:, :, :], qnext[:, :, :]).then_inc(c.sem, 1)
                dve.tensor_copy(hcur[:, :, :], h3[:, :, :]).then_inc(c.sem, 1)
                dve.wait_ge(c.sem, c.after(3))

            def expert_dots(c, pair, k):
                j, b = k // HQ, k % 2
                dve.wait_ge(gathered[k % SLOTS].sem, gathered[k % SLOTS].at(pair, 16 * QK * (k // SLOTS + 1)))
                for r in range(QK):
                    row = ring[0:S, k % SLOTS, r, 0:D]
                    dve.tensor_tensor_reduce(out=row, in0=row, in1=qcur[:, j, :], scale=1.0, scalar=0.0,
                                                    op0=ALU.mult, op1=ALU.add, accum_out=xd[:, b, r:r + 1]).then_inc(c.sem, 1)
                dve.wait_ge(c.sem, c.after(QK))
                dve.tensor_tensor(ga[:, b, :], xd[:, b, :], xd[:, b, :], ALU.mult).then_inc(c.sem, 1)
                dve.wait_ge(c.sem, c.after(1))
                dve.tensor_scalar(gb[:, b, :], ga[:, b, :], GELU_B, GELU_A, ALU.mult, ALU.add).then_inc(c.sem, 1)
                dve.wait_ge(c.sem, c.after(1))
                dve.tensor_tensor(gu[:, b, :], gb[:, b, :], xd[:, b, :], ALU.mult).then_inc(gu_sb.sem, 1)

            def expert_values(c, pair, k):
                j, b, at = k // HQ, k % 2, (k % HQ) * QK
                dve.wait_ge(gt_sb.sem, gt_sb.at(pair, k + 1))
                dve.scalar_tensor_tensor(gv[:, b, :], gt[:, b, :], 1.0, xd[:, b, :], ALU.add, ALU.mult).then_inc(c.sem, 1)
                dve.wait_ge(c.sem, c.after(1))
                dve.scalar_tensor_tensor(val[:, b, :], gv[:, b, :], 0.5, wcur[:, j, at:at + QK], ALU.mult, ALU.mult
                                         ).then_inc(val_sb.sem, 1)

            def finish(c, pair, j):
                dve.wait_ge(up_mm.sem, up_mm.at(pair, (j + 1) * HQ))
                dve.wait_ge(stored[j].sem, stored[j].at(pair, 0))
                dve.tensor_tensor(y[:, j, :], hcur[:, j, :], ps[0:S, 7, j * D:(j + 1) * D], ALU.add
                                  ).then_inc(y_sb.sem, 1)

            def front(pair, dots, values, done):
                c = Chain(v_front, pair)
                tok_a(c, pair)
                tok_b(c, pair)
                at0_latents(c, pair)
                at0_rope(c, pair)
                maxima(c, pair, 0)
                dots(0)
                attend(c, pair, 0, h0, h1)
                values(0)
                moe_router(c, pair)
                dots(1)
                moe_steps(c, pair, 0, 4)
                values(1)
                moe_steps(c, pair, 4, 8)
                dots(2)
                moe_steps(c, pair, 8, 12)
                values(2)
                moe_steps(c, pair, 12, STEPS)
                dots(3)
                at1_norm(c, pair)
                values(3)
                maxima(c, pair, 1)
                dots(4)
                attend(c, pair, 1, h2, h3)
                values(4)
                done(0)
                norm_h(c, h3, qnext)
                dots(5)
                pk_top(c, pair, 0)
                pk_best(c, pair, 0)
                values(5)
                pk_top(c, pair, 1)
                pk_best(c, pair, 1)
                pk_softmax(c, pair)
                c.end()

            for t in (0,):
                dve.memset(vA[:, :, DH:DH + 1], 1.0).then_inc(consts.sem, 1)
                dve.memset(idx[:, :, :], 0).then_inc(consts.sem, 1)
            dve.sem_inc(y_sb.sem, 2)
            for pack in PACKS:
                if pack == "tok":
                    dve.wait_ge(loaded[pack].sem, 16)
            dve.tensor_scalar(posb[:, :], W("tok", "pos"), W("tok", "b_patch"), None, ALU.add
                              ).then_inc(posb_ready.sem, 1)
            dve.wait_ge(posb_ready.sem, 1)
            dve.wait_ge(consts.sem, 2)

            front(0, lambda k: None, lambda k: None, lambda j: None)
            with dve.Fori(1, PAIRS) as pair:
                c = Chain(v_expert, pair - 1)
                take_over(c, pair - 1)
                front(pair, lambda k: expert_dots(c, pair - 1, k), lambda k: expert_values(c, pair - 1, k),
                      lambda j: finish(c, pair - 1, j))
                expert_dots(c, pair - 1, 6)
                expert_values(c, pair - 1, 6)
                expert_dots(c, pair - 1, 7)
                expert_values(c, pair - 1, 7)
                finish(c, pair - 1, 1)
                c.end()
            c = Chain(v_expert, PAIRS - 1)
            take_over(c, PAIRS - 1)
            for k in range(NQ):
                expert_dots(c, PAIRS - 1, k)
                expert_values(c, PAIRS - 1, k)
                if k % HQ == HQ - 1:
                    finish(c, PAIRS - 1, k // HQ)
            c.end()


def _pack(pack, parts):
    cols, width = columns(pack)
    out = np.zeros((128, width), np.float32)
    for name, (r, n) in PACKS[pack].items():
        out[0:r, cols[name]:cols[name] + n] = parts[name].reshape(r, n)
    return out


def _rope_tables():
    t = np.arange(S, dtype=np.float32)
    cos, sin = np.cos(t), np.sin(t)
    tq = [cos, cos, -sin, -sin, cos, cos, sin, sin]
    tk = [cos, -sin, cos, -sin, cos, sin, cos, sin]
    out = []
    for rows_ in (tq, tk):
        a = np.zeros((4, HROWS, S), np.float32)
        a[:, 0:DH] = 1.0
        a[:, DH:DH + 8] = np.stack(rows_)
        out.append(a.reshape(128, S))
    return out


ROPE_Q = [0, 0, 1, 1, 1, 1, 0, 0]
ROPE_K = [0, 1, 0, 1, 1, 0, 1, 0]


def _head_rows(w, rope=None, order=None):
    n = (w if w is not None else rope).shape[0]
    out = np.zeros((n, HEADS, HROWS), np.float32)
    if w is not None:
        out[:, :, 0:DH] = w.reshape(n, HEADS, DH)
    if rope is not None:
        out[:, :, DH:DH + 8] = rope.reshape(n, HEADS, 2)[:, :, order]
    return out.reshape(n, HEADS * HROWS)


def _layouts(i):
    i = {k: np.asarray(v) for k, v in i.items()}
    tq, tk = _rope_tables()
    s, t = np.arange(S)[None, :], np.arange(S)[:, None]
    kv = i["L0_attn_W_ukv"]
    w1 = i["L1_attn_w_qkv"].reshape(3, D, D).transpose(0, 2, 1)
    packs = {
        "tok": {
            "w_patch": i["L0_tok_W_patch"].reshape(KCH, 128, D).transpose(1, 0, 2),
            "pos": i["L0_tok_pos_embed"][0].T, "b_patch": i["L0_tok_b_patch"],
            "w_cs": np.concatenate([i["L0_tok_W_coord"], i["L0_tok_W_spinor"]], 1),
            "b_cs": np.tile(np.concatenate([i["L0_tok_b_coord"], i["L0_tok_b_spinor"]])[None], (NTOK, 1)),
            "w_emb": np.concatenate([i["L0_tok_W_embed"], i["L0_tok_b_embed"][None]], 0),
            "ident": np.eye(128, dtype=np.float32), "ln_g": i["L0_tok_ln_gamma"], "ln_b": i["L0_tok_ln_beta"],
            "w_out": i["L0_tok_W_out"], "b_out": i["L0_tok_b_out"], "ones": np.ones(128, np.float32)},
        "at0": {
            "w_down": np.concatenate([i["L0_attn_W_dq"], i["L0_attn_W_dkv"]], 1),
            "q_g": i["L0_attn_q_ln_g"], "q_b": i["L0_attn_q_ln_b"],
            "kv_g": i["L0_attn_kv_ln_g"], "kv_b": i["L0_attn_kv_ln_b"],
            "w_q": _head_rows(i["L0_attn_W_uq"], i["L0_attn_W_qr"], ROPE_Q),
            "w_k": _head_rows(kv[:, 0:D]), "w_kr": _head_rows(None, i["L0_attn_W_kr"], ROPE_K),
            "w_v": kv[:, D:2 * D], "w_o": i["L0_attn_W_o"].T,
            "rope_q": tq, "rope_k": tk, "mask": np.where(s > t, np.float32(MASKED), np.float32(0.0))},
        "moe": {
            "sel": i["L0_ffn_expert_sel"].T,
            "iota": np.tile(np.arange(E0, dtype=np.float32)[None], (S, 1)),
            "keys": i["L0_ffn_keys"].transpose(1, 0, 2), "values": i["L0_ffn_values"].transpose(1, 0, 2)},
        "at1": {
            "w_q": _head_rows(w1[0]), "w_k": _head_rows(w1[1]), "w_v": w1[2],
            "w_o": i["L1_attn_w_agg"].T, "b_o": i["L1_attn_b_agg"]},
        "pk": {
            "w_q": i["L1_ffn_Wq"].T, "b_q": i["L1_ffn_bq"].reshape(PH, 128).T,
            "keys": i["L1_ffn_keys"].transpose(1, 3, 0, 2),
            "iota": np.tile(np.arange(TOPK, dtype=np.float32)[None], (S, 1))},
    }
    x = i["x"].reshape(PAIRS, 2, CH, SIDE, PATCH, SIDE, PATCH).transpose(0, 2, 4, 6, 1, 3, 5)
    x = x.reshape(PAIRS, KCH, 128, 2 * NTOK).transpose(0, 2, 1, 3).reshape(PAIRS, 128, KCH * 2 * NTOK)
    return {
        "patches": np.ascontiguousarray(x),
        "txt": np.ascontiguousarray(i["txt"]),
        "rows": np.concatenate([i["L1_ffn_w_down_embed"], i["L1_ffn_w_up_embed"]], 1),
        **{"pack_" + k: _pack(k, v) for k, v in packs.items()},
    }


def kernel(**inputs):
    import concourse.bacc as bacc
    from concourse.bass_utils import run_bass_kernel_spmd

    arrays = _layouts(inputs)
    nc = bacc.Bacc("TRN2", target_bir_lowering=False, num_devices=1)
    aps = {n: nc.dram_tensor(n, a.shape, mybir.dt.from_np(a.dtype), kind="ExternalInput").ap()
           for n, a in arrays.items()}
    out = nc.dram_tensor("out", (B, S, D), F32, kind="ExternalOutput").ap()
    fusion_program(nc, aps["patches"], aps["txt"], {k: aps["pack_" + k] for k in PACKS}, aps["rows"], out)
    result = run_bass_kernel_spmd(nc, [arrays], core_ids=[0])
    return result.results[0]["out"]
```

```python
import math
from contextlib import ExitStack

import concourse.bass as bass
import numpy as np
from concourse import mybir

F32 = mybir.dt.float32
BF16 = mybir.dt.bfloat16
U32 = mybir.dt.uint32
I32 = mybir.dt.int32
ALU = mybir.AluOpType
ACT = mybir.ActivationFunctionType
AXX = mybir.AxisListType.X

B, D = 32, 128
PAIRS = B // 2
IMG, PATCH, CH = 112, 16, 3
SIDE = IMG // PATCH
NTOK = SIDE * SIDE
NTXT = 77
S = NTOK + NTXT
KCH = CH * PATCH * PATCH // 128
DC, DS = 8, 4
HEADS, DH = 8, 16
HB = 4
RQ, RKV = 64, 85
HROWS = 32
E0, H0 = 32, 128
SLOT_OF = [(j, g) for j in range(2) for g in range(2)]
EG = 2
STEPS = E0 // EG
PH, NE, TOPK, HALF = 8, 128, 8, 64
KPT = PH * TOPK
QK = 16
QUARTERS = 2 * KPT // QK
A_STEPS, B_STEPS, E_STEPS = 45, 201, 155
N_CONSTS = 6
SLOTS = 4
EPS = 1e-5
MASKED = -1e30
RSQRT_MAGIC = float(0x5F1FFFF9)
RSQRT_STEPS = [(0.703952253, 0.703952253 * 2.38924456), (0.5 * (1 + 3.2e-7), 1.5 * (1 + 3.2e-7))]
GELU_A, GELU_B = math.sqrt(2 / math.pi), 0.044715 * math.sqrt(2 / math.pi)

SCHEDULE = """
    e_take a_x a_cs a_ck e_dots0 a_enh a_xnT e_values0 b_norm1 a_h0 b_hnT1 b_logits a_hnT b_router a_down
    m0 m1 m2 m3 m4 m5 m6 a_cT m7 m8 m9 m10 a_q m11 m12 m13 a_k m14 m15 a_v m16 e_up0 e_dots1 e_values1
    b_norm2 a_scores b_hnT2 a_exps e_up1 b_q a_pT e_dots2 b_k a_pv b_v e_values2 b_scores e_up2 b_exps
    b_pT e_dots3 b_pv b_oT e_values3 b_out b_hnT3 e_up3 e_dots4 b_qh e_sum0 e_values4 a_oT b_keys0 e_up4
    b_best0 e_dots5 b_keys1 e_values5 b_best1 b_softmax e_up5 e_dots6 e_values6 e_dots7 e_up6 e_values7
    a_out e_up7 e_sum1
""".split()

PACKS = {
    "tok": {"w_patch": (128, KCH * D), "pos": (128, NTOK), "b_patch": (128, 1), "w_cs": (128, DC + DS),
            "b_cs": (NTOK, DC + DS), "w_emb": (DC + 1, D), "ident": (128, 128), "ln_g": (128, 1),
            "ln_b": (128, 1), "w_out": (128, D), "b_out": (1, D), "ones": (1, 128)},
    "at0": {"w_down": (128, RQ + RKV), "q_g": (RQ, 1), "q_b": (RQ, 1), "kv_g": (RKV, 1), "kv_b": (RKV, 1),
            "w_q": (RQ, 256), "w_k": (RKV, 256), "w_kr": (128, 256), "w_v": (RKV, D), "w_o": (128, D),
            "rope_q": (128, S), "rope_k": (128, S), "mask": (S, S)},
    "moe": {"sel": (128, E0), "iota": (S, E0), "keys": (128, E0 * H0), "values": (128, E0 * D)},
    "at1": {"w_q": (128, 256), "w_k": (128, 256), "w_v": (128, D), "w_o": (128, D), "b_o": (1, D)},
    "pk": {"w_q": (128, PH * 128), "b_q": (128, PH), "keys": (128, PH * NE), "iota": (S, TOPK)},
}


def columns(pack):
    at, out = 0, {}
    for name, (_, n) in PACKS[pack].items():
        out[name] = at
        at += n
    return out, at


class Signal:

    def __init__(self, sem, per, credit=0):
        self.sem, self.per, self.credit = sem, per, credit

    def at(self, pair, n):
        return pair * self.per + (n + self.credit)


class Chain:

    def __init__(self, steps, pair):
        self.steps, self.pair, self.n, self.sem = steps, pair, 0, steps.sem

    def after(self, n):
        self.n += n
        assert self.n <= self.steps.per
        return self.steps.at(self.pair, self.n)

    def before(self, n):
        return self.steps.at(self.pair, self.n - n)

    def end(self):
        assert self.n == self.steps.per, (self.n, self.steps.per)


def fusion_program(nc, patches, txt, packs, rows, out):
    ctx = ExitStack()
    with ctx:
        def sb(name, shape, dt=F32):
            return ctx.enter_context(nc.sbuf_tensor("s_" + name, shape, dt))

        def signal(name, per, credit=0):
            return Signal(ctx.enter_context(nc.semaphore(name)), per, credit)

        where, packed = {}, {}
        for pack in PACKS:
            cols, width = columns(pack)
            packed[pack] = sb("w_" + pack, [128, width])
            for name, (r, n) in PACKS[pack].items():
                where[pack, name] = packed[pack][0:r, cols[name]:cols[name] + n]

        def W(pack, name):
            return where[pack, name]

        ident = W("tok", "ident")
        posb = sb("posb", [128, NTOK])
        ident16 = sb("ident16", [S, S], BF16)
        mask16 = sb("mask16", [S, S], BF16)

        pT = sb("patches", [128, KCH, 2 * NTOK])
        xT = sb("xT", [128, 2, NTOK])
        cs = sb("cs", [NTOK, 2, DC + DS])
        sq = sb("sq", [NTOK, 2, DS])
        ck = sb("ck", [NTOK, 2, DC + 1])
        ckT = sb("ckT", [DC + 1, 2, NTOK])
        xnT = sb("xnT", [128, 2, NTOK])
        h0 = sb("h0", [S, 2, D])
        hnA = sb("hnA", [S, 2, D])
        xn = hnA[0:NTOK, :, :]
        hnTA = sb("hnTA", [128, 2, S])
        cn = sb("cn", [S, 2, RQ + RKV])
        cqT = sb("cqT", [RQ, 2, S])
        ckvT = sb("ckvT", [RKV, 2, S])
        h1 = sb("h1", [S, 2, D])
        qT = sb("qT", [128, 2, 2, S])
        kT = sb("kT", [128, 2, 2, S])
        prob = sb("prob", [S, 2 * HEADS, S])
        probT = sb("probT", [S, 2 * HEADS, S])
        vA = [sb(f"vA{n}", [S, 2 * HEADS, DH + 1]) for n in range(2)]
        nmx = [sb(f"nmx{n}", [S, 2 * HEADS]) for n in range(2)]
        rden = [sb(f"rden{n}", [S, 2 * HEADS, 1]) for n in range(2)]
        o = [sb(f"o{n}", [S, 2 * HEADS, DH]) for n in range(2)]
        oT = [sb(f"oT{n}", [128, 2, S]) for n in range(2)]
        stats = [sb(f"stats{n}", [S, 4, 6]) for n in range(2)]
        mv = [sb(f"mv{n}", [S, 4, 2]) for n in range(2)]
        rs = [sb(f"rs{n}", [S, 4, 4]) for n in range(2)]

        hnB = sb("hnB", [S, 2, D])
        hnTB = sb("hnTB", [128, 2, S])
        h2 = sb("h2", [S, 2, D])
        el = sb("el", [S, 2, E0])
        sel = sb("sel", [S, 2, E0])
        selmax = sb("selmax", [S, 2, 8])
        selidx = sb("selidx", [S, 2, 8], U32)
        selidf = sb("selidf", [S, 2, 8])
        wm = sb("wm", [S, 2, 2, E0])
        wmoe = sb("wmoe", [S, 2, E0])
        hidT = sb("hidT", [128, 2, EG, 2, S])
        qhT = sb("qhT", [128, PH, 2, S])
        s8 = sb("s8", [S, 2, PH, 2, TOPK])
        i8 = sb("i8", [S, 2, PH, 2, TOPK], U32)
        sums = sb("sums", [S, PH, TOPK, TOPK])
        best = sb("best", [S, 2 * PH, TOPK])
        bpos = sb("bpos", [S, 2 * PH, TOPK], U32)
        place = [sb(f"place{n}", [S, 2 * PH, TOPK], U32) for n in range(2)]
        onehot = [probT[:, 4 * n:4 * n + 5, :].rearrange("p a b -> p (a b)")[:, 8 * n:8 * n + PH * TOPK * TOPK]
                  .rearrange("p (h k a) -> p h k a", h=PH, k=TOPK) for n in range(2)]
        picked = [sb(f"picked{n}", [S, PH, TOPK]) for n in range(2)]
        idxf = sb("idxf", [S, 2, KPT])
        ez = sb("ez", [S, 2 * PH, TOPK])
        esum = sb("esum", [S, 2 * PH, 1])
        wnext = sb("wnext", [S, 2, KPT])
        qnext = sb("qnext", [S, 2, D])

        idx = sb("idx", [128, 2, KPT], U32)
        ring = sb("ring", [128, SLOTS, QK, 2 * D])
        wcur = sb("wcur", [S, 2, KPT])
        hcur = sb("hcur", [S, 2, D])
        xd, ga, gb, gu, gt, gv, val = (sb(n, [S, 2, QK]) for n in ("xd", "ga", "gb", "gu", "gt", "gv", "val"))
        diag = sb("diag", [S, 2, QK, S])
        y = sb("y", [S, 2, D])

        ps = ctx.enter_context(nc.psum_tensor("ps", [128, 8, 512], F32))
        qcur = ps[0:S, 6, 0:2 * D].rearrange("p (j d) -> p j d", j=2)

        HID_BANKS, QH_BANKS = (2, 5), (5, 2, 3, 5)

        def bank(n, rows_, width):
            return ps[0:rows_, n, 0:width]

        loaded = {pack: signal("loaded_" + pack, 0) for pack in PACKS}
        consts = signal("consts", 0)
        passed_pool, passed_pe, passed_dve = (
            ctx.enter_context(nc.semaphore("passed_" + e)) for e in ("pool", "pe", "dve"))
        patches_in = signal("patches_in", 16)
        txt_in = signal("txt_in", 16)
        xT_mm = signal("xT_mm", 1)
        xT_sb = signal("xT_sb", 1)
        cs_mm = signal("cs_mm", 1)
        ck_sb = signal("ck_sb", 1)
        ckT_mm = signal("ckT_mm", 1)
        ckT_sb = signal("ckT_sb", 1)
        xenh_mm = signal("xenh_mm", 1)
        xn_sb = signal("xn_sb", 1)
        xnT_mm = signal("xnT_mm", 1)
        xnT_sb = signal("xnT_sb", 1)
        h0_mm = signal("h0_mm", 1)
        hnA_sb, hnTA_mm, hnTA_sb = signal("hnA_sb", 1), signal("hnTA_mm", 1), signal("hnTA_sb", 1)
        hnB_sb, hnTB_mm, hnTB_sb = signal("hnB_sb", 3), signal("hnTB_mm", 3), signal("hnTB_sb", 3)
        down_mm = signal("down_mm", 1)
        cn_sb = signal("cn_sb", 1)
        cT_mm = signal("cT_mm", 1)
        cT_sb = signal("cT_sb", 1)
        qkv_mm = [signal(f"qkv_mm{n}", 3) for n in range(2)]
        qk_sb = [signal(f"qk_sb{n}", 2) for n in range(2)]
        v_sb = [signal(f"v_sb{n}", 1) for n in range(2)]
        score_mm = [signal(f"score_mm{n}", 1) for n in range(2)]
        nmx_sb = [signal(f"nmx_sb{n}", 2) for n in range(2)]
        exp_sb = [signal(f"exp_sb{n}", 4) for n in range(2)]
        probT_mm = [signal(f"probT_mm{n}", 4) for n in range(2)]
        probT_sb = [signal(f"probT_sb{n}", 4) for n in range(2)]
        pv_mm = [signal(f"pv_mm{n}", 1) for n in range(2)]
        o_sb = [signal(f"o_sb{n}", 1) for n in range(2)]
        oT_mm = [signal(f"oT_mm{n}", 1) for n in range(2)]
        oT_sb = [signal(f"oT_sb{n}", 1) for n in range(2)]
        out_mm = [signal(f"out_mm{n}", 1) for n in range(2)]
        h1_sb = signal("h1_sb", 1)
        logit_mm = signal("logit_mm", 1)
        el_sb = signal("el_sb", 1)
        hid_mm = signal("hid_mm", STEPS)
        hid_sb = signal("hid_sb", STEPS)
        moe_mm = signal("moe_mm", STEPS)
        moe_sb = signal("moe_sb", STEPS)
        qh_mm = signal("qh_mm", PH // 2)
        qh_sb = signal("qh_sb", PH // 2)
        sub_mm = signal("sub_mm", 4)
        sub_read = signal("sub_read", 4)
        dif_sb = signal("dif_sb", 1)
        ez_sb = signal("ez_sb", 1)
        idx_ready = [signal(f"idx_ready{n}", 1) for n in range(2)]
        gathered = [signal(f"gathered{n}", 2 * 16 * QK) for n in range(SLOTS)]
        gu_sb = signal("gu_sb", QUARTERS)
        gt_sb = signal("gt_sb", QUARTERS)
        val_sb = signal("val_sb", QUARTERS)
        diag_sb = signal("diag_sb", QUARTERS)
        up_mm = signal("up_mm", QUARTERS, credit=QUARTERS)
        y_sb = signal("y_sb", 2, credit=2)
        stored = [signal(f"stored{n}", 16, credit=16) for n in range(2)]
        steps_a = signal("steps_a", A_STEPS)
        steps_b = signal("steps_b", B_STEPS)
        steps_e = signal("steps_e", E_STEPS)

        block = ctx.enter_context(nc.Block())

        NQ, HQ = QUARTERS, QUARTERS // 2

        def run(pieces, e=None, b=None, a=None):
            pair_of = {"a": a, "b": b, "m": b, "e": e}
            for name in SCHEDULE:
                if name in pieces and pair_of[name[0]] is not None:
                    pieces[name](pair_of[name[0]])

        @block.gpsimd
        def _(pool):
            with pool.Fori(0, PAIRS) as pair:
                for k in range(NQ):
                    if k % HQ == 0:
                        pool.wait_ge(idx_ready[k // HQ].sem, idx_ready[k // HQ].at(pair, 1))
                        pool.sem_inc(passed_pool, 1)
                    pool.wait_ge(up_mm.sem, up_mm.at(pair, k - SLOTS + 1))
                    pool.sem_inc(passed_pool, 1)
                    for r in range(QK):
                        col = (k % HQ) * QK + r
                        pool.indirect_dma_start(
                            ring[:, k % SLOTS, r, :], None, rows,
                            bass.IndirectOffsetOnAxis(ap=idx[:, k // HQ, col:col + 1], axis=0),
                        ).then_inc(gathered[k % SLOTS].sem, 16)

        @block.sync
        def _(sp):
            def load(pair):
                sp.wait_ge(xT_mm.sem, xT_mm.at(pair, 0))
                sp.dma_start(pT[:, :, :].rearrange("p c t -> p (c t)"),
                             patches[bass.ds(pair, 1), :, :].rearrange("a p n -> p (a n)")
                             ).then_inc(patches_in.sem, 16)
                sp.wait_ge(h1_sb.sem, h1_sb.at(pair, 0))
                sp.dma_start(h0[NTOK:S, :, :],
                             txt[bass.ds(pair * 2, 2), :, :].rearrange("j s d -> s j d")
                             ).then_inc(txt_in.sem, 16)

            def store(pair):
                for j in range(2):
                    sp.wait_ge(y_sb.sem, y_sb.at(pair, j + 1))
                    sp.dma_start(out[bass.ds(pair * 2 + j, 1), :, :].rearrange("a s d -> s (a d)"),
                                 y[:, j, :]).then_inc(stored[j].sem, 16)

            sp.sem_inc(stored[0].sem, 16)
            sp.sem_inc(stored[1].sem, 16)
            sp.dma_start(packed["tok"][:, :], packs["tok"]).then_inc(loaded["tok"].sem, 16)
            load(0)
            sp.dma_start(packed["at0"][:, :], packs["at0"]).then_inc(loaded["at0"].sem, 16)
            sp.dma_start(packed["moe"][:, :], packs["moe"]).then_inc(loaded["moe"].sem, 16)
            sp.dma_start(packed["at1"][:, :], packs["at1"]).then_inc(loaded["at1"].sem, 16)
            sp.dma_start(packed["pk"][:, :], packs["pk"]).then_inc(loaded["pk"].sem, 16)
            load(1)
            load(2)
            with sp.Fori(3, PAIRS) as pair:
                load(pair)
                store(pair - 3)
            for pair in range(PAIRS - 3, PAIRS):
                store(pair)
            for j in range(2):
                sp.wait_ge(stored[j].sem, stored[j].at(PAIRS - 1, 16))

        @block.tensor
        def _(pe):
            def mm(out_, lhsT, rhs, start=True, stop=True):
                return pe.matmul(out_, lhsT, rhs, start=start, stop=stop)

            def transposes(src, b, rows_=S):
                for j in range(2):
                    last = pe.transpose(ps[0:src.shape[2], b, j * rows_:(j + 1) * rows_], src[:, j, :],
                                        ident[0:rows_, 0:rows_])
                return last

            def a_x(pair):
                if isinstance(pair, int):
                    pe.wait_ge(loaded["tok"].sem, 16)
                pe.wait_ge(patches_in.sem, patches_in.at(pair, 16))
                pe.wait_ge(h1_sb.sem, h1_sb.at(pair, 0))
                for c in range(KCH):
                    last = mm(bank(4, 128, 2 * NTOK), W("tok", "w_patch")[:, c * D:(c + 1) * D],
                              pT[:, c, :], c == 0, c == KCH - 1)
                last.then_inc(xT_mm.sem, 1)

            def a_cs(pair):
                pe.wait_ge(xT_sb.sem, xT_sb.at(pair, 1))
                for j in range(2):
                    last = mm(ps[0:NTOK, 4, j * 12:(j + 1) * 12], xT[:, j, :], W("tok", "w_cs"))
                last.then_inc(cs_mm.sem, 1)

            def a_ck(pair):
                pe.wait_ge(ck_sb.sem, ck_sb.at(pair, 1))
                pe.sem_inc(passed_pe, 1)
                transposes(ck, 4, NTOK).then_inc(ckT_mm.sem, 1)

            def a_enh(pair):
                pe.wait_ge(ckT_sb.sem, ckT_sb.at(pair, 1))
                for j in range(2):
                    o_ = ps[0:NTOK, 4, j * D:(j + 1) * D]
                    mm(o_, xT[:, j, :], ident, True, False)
                    last = mm(o_, ckT[:, j, :], W("tok", "w_emb"), False, True)
                last.then_inc(xenh_mm.sem, 1)

            def a_xnT(pair):
                pe.wait_ge(xn_sb.sem, xn_sb.at(pair, 1))
                pe.sem_inc(passed_pe, 1)
                transposes(xn, 4, NTOK).then_inc(xnT_mm.sem, 1)

            def a_h0(pair):
                pe.wait_ge(xnT_sb.sem, xnT_sb.at(pair, 1))
                for j in range(2):
                    o_ = ps[0:NTOK, 4, j * D:(j + 1) * D]
                    mm(o_, xnT[:, j, :], W("tok", "w_out"), True, False)
                    last = mm(o_, W("tok", "ones")[:, 0:NTOK], W("tok", "b_out"), False, True)
                last.then_inc(h0_mm.sem, 1)

            def a_hnT(pair):
                pe.wait_ge(hnA_sb.sem, hnA_sb.at(pair, 1))
                transposes(hnA, 4).then_inc(hnTA_mm.sem, 1)

            def a_down(pair):
                if isinstance(pair, int):
                    pe.wait_ge(loaded["at0"].sem, 16)
                pe.wait_ge(hnTA_sb.sem, hnTA_sb.at(pair, 1))
                for j in range(2):
                    last = mm(ps[0:S, 4, j * 149:(j + 1) * 149], hnTA[:, j, :], W("at0", "w_down"))
                last.then_inc(down_mm.sem, 1)

            def a_cT(pair):
                pe.wait_ge(cn_sb.sem, cn_sb.at(pair, 1))
                pe.sem_inc(passed_pe, 1)
                for j in range(2):
                    pe.transpose(ps[0:RQ, 4, j * S:(j + 1) * S], cn[:, j, 0:RQ], ident[0:S, 0:S])
                    last = pe.transpose(ps[0:RKV, 4, (2 + j) * S:(3 + j) * S], cn[:, j, RQ:RQ + RKV],
                                        ident[0:S, 0:S])
                last.then_inc(cT_mm.sem, 1)

            def a_q(pair):
                pe.wait_ge(cT_sb.sem, cT_sb.at(pair, 1))
                for g in range(2):
                    last = mm(ps[:, 4, g * 2 * S:(g + 1) * 2 * S], W("at0", "w_q")[:, g * 128:(g + 1) * 128],
                              cqT[:, :, :])
                last.then_inc(qkv_mm[0].sem, 1)

            def a_k(pair):
                pe.wait_ge(qk_sb[0].sem, qk_sb[0].at(pair, 1))
                for g in range(2):
                    o_ = ps[:, 4, g * 2 * S:(g + 1) * 2 * S]
                    mm(o_, W("at0", "w_k")[:, g * 128:(g + 1) * 128], ckvT[:, :, :], True, False)
                    last = mm(o_, W("at0", "w_kr")[:, g * 128:(g + 1) * 128], hnTA[:, :, :], False, True)
                last.then_inc(qkv_mm[0].sem, 1)

            def a_v(pair):
                pe.wait_ge(qk_sb[0].sem, qk_sb[0].at(pair, 2))
                for j in range(2):
                    last = mm(ps[0:S, 4, j * D:(j + 1) * D], ckvT[:, j, :], W("at0", "w_v"))
                last.then_inc(qkv_mm[0].sem, 1)

            def head_scores(n):
                for c, (j, g) in enumerate(SLOT_OF):
                    for b in range(4):
                        r = HROWS * b
                        last = mm(ps[0:S, b, c * S:(c + 1) * S], qT[r:r + HROWS, g, j, :],
                                  kT[r:r + HROWS, g, j, :], n == 1, n == 1 or c == 3)
                return last

            def a_scores(pair):
                pe.wait_ge(qk_sb[0].sem, qk_sb[0].at(pair, 2))
                if not isinstance(pair, int) or pair > 0:
                    pe.wait_ge(moe_sb.sem, moe_sb.at(pair - 1, STEPS))
                for b in range(4):
                    mm(ps[0:S, b, 0:HB * S].rearrange("p (h s) -> p h s", h=HB), ident16[:, :],
                       mask16[:, :].unsqueeze(1).broadcast_to([S, HB, S]), True, False)
                head_scores(0).then_inc(score_mm[0].sem, 1)

            def b_scores(pair, with_a):
                pe.wait_ge(qk_sb[1].sem, qk_sb[1].at(pair, 2))
                if with_a:
                    pe.wait_ge(probT_sb[0].sem, probT_sb[0].at(pair + 1, 4))
                head_scores(1).then_inc(score_mm[1].sem, 1)

            def prob_transposes(pair, n):
                for b in range(4):
                    pe.wait_ge(exp_sb[n].sem, exp_sb[n].at(pair, b + 1))
                    for h in range(HB):
                        last = pe.transpose(ps[0:S, b, h * S:(h + 1) * S], prob[:, b * HB + h, :],
                                            ident[0:S, 0:S])
                    last.then_inc(probT_mm[n].sem, 1)

            def weighted_values(pair, n, to):
                pe.wait_ge(v_sb[n].sem, v_sb[n].at(pair, 1))
                for b in range(4):
                    pe.wait_ge(probT_sb[n].sem, probT_sb[n].at(pair, b + 1))
                    for c, (j, g) in enumerate(SLOT_OF):
                        h = j * HEADS + g * HB + b
                        last = mm(ps[0:S, to, h * (DH + 1):(h + 1) * (DH + 1)], probT[:, b * HB + c, :],
                                  vA[n][:, h, :])
                last.then_inc(pv_mm[n].sem, 1)

            def output_transposes(pair, n, to):
                pe.wait_ge(o_sb[n].sem, o_sb[n].at(pair, 1))
                transposes(o[n][:, :, :].rearrange("p (j h) d -> p j (h d)", j=2), to).then_inc(oT_mm[n].sem, 1)

            def output_projection(pair, n, to):
                pe.wait_ge(oT_sb[n].sem, oT_sb[n].at(pair, 1))
                for j in range(2):
                    o_ = ps[0:S, to, j * D:(j + 1) * D]
                    last = mm(o_, oT[n][:, j, :], W(f"at{n}", "w_o"), True, n == 0)
                    if n == 1:
                        last = mm(o_, W("tok", "ones")[:, 0:S], W("at1", "b_o"), False, True)
                last.then_inc(out_mm[n].sem, 1)

            def b_hnT(pair, n, to):
                pe.wait_ge(hnB_sb.sem, hnB_sb.at(pair, n))
                transposes(hnB if n < 3 else qnext, to).then_inc(hnTB_mm.sem, 1)

            def b_logits(pair):
                if isinstance(pair, int):
                    pe.wait_ge(loaded["moe"].sem, 16)
                pe.wait_ge(hnTB_sb.sem, hnTB_sb.at(pair, 1))
                for j in range(2):
                    last = mm(ps[0:S, 5, j * E0:(j + 1) * E0], hnTB[:, j, :], W("moe", "sel"))
                last.then_inc(logit_mm.sem, 1)

            def moe(n):
                def step(pair):
                    if n < STEPS:
                        if n == 1:
                            pe.wait_ge(el_sb.sem, el_sb.at(pair, 1))
                        if n >= 2:
                            pe.wait_ge(hid_sb.sem, hid_sb.at(pair, n - 1))
                        for q in range(EG):
                            e = n * EG + q
                            last = mm(ps[:, HID_BANKS[n % 2], q * 2 * S:(q + 1) * 2 * S],
                                      W("moe", "keys")[:, e * H0:(e + 1) * H0], hnTB[:, :, :])
                        last.then_inc(hid_mm.sem, 1)
                    m = n - 1
                    if m >= 0:
                        pe.wait_ge(hid_sb.sem, hid_sb.at(pair, m + 1))
                        if m >= 2:
                            pe.wait_ge(moe_sb.sem, moe_sb.at(pair, m - 1))
                        for q in range(EG):
                            e = m * EG + q
                            for j in range(2):
                                c = (2 * q + j) * D
                                last = mm(ps[0:S, m % 2, c:c + D], hidT[:, m % 2, q, j, :],
                                          W("moe", "values")[:, e * D:(e + 1) * D])
                        last.then_inc(moe_mm.sem, 1)
                return step

            def b_q(pair):
                if isinstance(pair, int):
                    pe.wait_ge(loaded["at1"].sem, 16)
                pe.wait_ge(hnTB_sb.sem, hnTB_sb.at(pair, 2))
                for g in range(2):
                    last = mm(ps[:, 5, g * 2 * S:(g + 1) * 2 * S], W("at1", "w_q")[:, g * 128:(g + 1) * 128],
                              hnTB[:, :, :])
                last.then_inc(qkv_mm[1].sem, 1)

            def b_k(pair):
                pe.wait_ge(qk_sb[1].sem, qk_sb[1].at(pair, 1))
                for g in range(2):
                    last = mm(ps[:, 5, g * 2 * S:(g + 1) * 2 * S], W("at1", "w_k")[:, g * 128:(g + 1) * 128],
                              hnTB[:, :, :])
                last.then_inc(qkv_mm[1].sem, 1)

            def b_v(pair):
                pe.wait_ge(qk_sb[1].sem, qk_sb[1].at(pair, 2))
                for j in range(2):
                    last = mm(ps[0:S, 5, j * D:(j + 1) * D], hnTB[:, j, :], W("at1", "w_v"))
                last.then_inc(qkv_mm[1].sem, 1)

            def b_qh(pair):
                if isinstance(pair, int):
                    pe.wait_ge(loaded["pk"].sem, 16)
                pe.wait_ge(hnTB_sb.sem, hnTB_sb.at(pair, 3))
                for m in range(PH // 2):
                    if m == 3:
                        pe.wait_ge(qh_sb.sem, qh_sb.at(pair, 1))
                    for h in (2 * m, 2 * m + 1):
                        last = mm(ps[:, QH_BANKS[m], (h % 2) * 2 * S:(h % 2 + 1) * 2 * S],
                                  W("pk", "w_q")[:, h * 128:(h + 1) * 128], hnTB[:, :, :])
                    last.then_inc(qh_mm.sem, 1)

            def b_keys(j):
                def keys(pair):
                    for m in range(2):
                        if j == 0:
                            pe.wait_ge(qh_sb.sem, qh_sb.at(pair, 2 * m + 2))
                        else:
                            pe.wait_ge(sub_read.sem, sub_read.at(pair, m + 1))
                        for q in range(4):
                            h = 4 * m + q
                            for c in range(2):
                                last = mm(ps[0:S, 2 * m + c, q * NE:(q + 1) * NE],
                                          qhT[c * HALF:(c + 1) * HALF, h, j, :],
                                          W("pk", "keys")[c * HALF:(c + 1) * HALF, h * NE:(h + 1) * NE])
                        last.then_inc(sub_mm.sem, 1)
                return keys

            def e_up(k):
                def up(pair):
                    j = k // HQ
                    pe.wait_ge(diag_sb.sem, diag_sb.at(pair, k + 1))
                    if k % HQ == 0:
                        pe.wait_ge(y_sb.sem, y_sb.at(pair, j - 1))
                    for r in range(QK):
                        last = mm(ps[0:S, 7, j * D:(j + 1) * D], diag[:, k % 2, r, :],
                                  ring[0:S, k % SLOTS, r, D:2 * D],
                                  k % HQ == 0 and r == 0, k % HQ == HQ - 1 and r == QK - 1)
                    last.then_inc(up_mm.sem, 1)
                return up

            def pieces(with_a):
                return {
                    "a_x": a_x, "a_cs": a_cs, "a_ck": a_ck, "a_enh": a_enh, "a_xnT": a_xnT, "a_h0": a_h0,
                    "a_hnT": a_hnT, "a_down": a_down, "a_cT": a_cT, "a_q": a_q, "a_k": a_k, "a_v": a_v,
                    "a_scores": a_scores,
                    "a_pT": lambda p: prob_transposes(p, 0), "a_pv": lambda p: weighted_values(p, 0, 4),
                    "a_oT": lambda p: output_transposes(p, 0, 4), "a_out": lambda p: output_projection(p, 0, 4),
                    "b_hnT1": lambda p: b_hnT(p, 1, 5), "b_hnT2": lambda p: b_hnT(p, 2, 5),
                    "b_hnT3": lambda p: b_hnT(p, 3, 5), "b_logits": b_logits,
                    "b_q": b_q, "b_k": b_k, "b_v": b_v, "b_scores": lambda p: b_scores(p, with_a),
                    "b_pT": lambda p: prob_transposes(p, 1), "b_pv": lambda p: weighted_values(p, 1, 5),
                    "b_oT": lambda p: output_transposes(p, 1, 5), "b_out": lambda p: output_projection(p, 1, 5),
                    "b_qh": b_qh, "b_keys0": b_keys(0), "b_keys1": b_keys(1),
                    **{f"m{n}": moe(n) for n in range(STEPS + 1)},
                    **{f"e_up{k}": e_up(k) for k in range(NQ)},
                }

            pe.sem_inc(up_mm.sem, NQ)
            pe.wait_ge(consts.sem, N_CONSTS)
            run(pieces(True), a=0)
            run(pieces(True), b=0, a=1)
            with pe.Fori(0, PAIRS - 2) as pair:
                run(pieces(True), e=pair, b=pair + 1, a=pair + 2)
            run(pieces(False), e=PAIRS - 2, b=PAIRS - 1)
            run(pieces(False), e=PAIRS - 1)

        @block.scalar
        def _(act):
            def copy(out_, in_, scale=1.0):
                return act.activation(out_, in_, ACT.Copy, scale=scale)

            def flat(t):
                return t.rearrange("p j s -> p (j s)")

            def a_ck(pair):
                act.wait_ge(ckT_mm.sem, ckT_mm.at(pair, 1))
                copy(flat(ckT[:, :, :]), bank(4, DC + 1, 2 * NTOK)).then_inc(ckT_sb.sem, 1)

            def a_xnT(pair):
                act.wait_ge(xnT_mm.sem, xnT_mm.at(pair, 1))
                act.activation(flat(xnT[:, :, :]), bank(4, 128, 2 * NTOK), ACT.Identity,
                               scale=W("tok", "ln_g"), bias=W("tok", "ln_b")).then_inc(xnT_sb.sem, 1)

            def a_hnT(pair):
                act.wait_ge(hnTA_mm.sem, hnTA_mm.at(pair, 1))
                copy(flat(hnTA[:, :, :]), bank(4, 128, 2 * S)).then_inc(hnTA_sb.sem, 1)

            def a_cT(pair):
                act.wait_ge(cT_mm.sem, cT_mm.at(pair, 1))
                act.activation(flat(cqT[:, :, :]), ps[0:RQ, 4, 0:2 * S], ACT.Identity,
                               scale=W("at0", "q_g"), bias=W("at0", "q_b"))
                act.activation(flat(ckvT[:, :, :]), ps[0:RKV, 4, 2 * S:4 * S], ACT.Identity,
                               scale=W("at0", "kv_g"), bias=W("at0", "kv_b")).then_inc(cT_sb.sem, 1)

            def values(pair, n, from_):
                act.wait_ge(qkv_mm[n].sem, qkv_mm[n].at(pair, 3))
                copy(vA[n][:, :, 0:DH], bank(from_, S, 2 * D).rearrange("p (h d) -> p h d", d=DH)
                     ).then_inc(v_sb[n].sem, 1)

            def exps(pair, n):
                for q in range(2):
                    act.wait_ge(nmx_sb[n].sem, nmx_sb[n].at(pair, q + 1))
                    for g in range(q * HEADS, (q + 1) * HEADS):
                        last = act.activation(prob[:, g, :], ps[0:S, g // HB, (g % HB) * S:(g % HB + 1) * S],
                                              ACT.Exp, bias=nmx[n][:, g:g + 1])
                        if g % HB == HB - 1:
                            last.then_inc(exp_sb[n].sem, 1)

            def prob_transposes(pair, n, with_a=False):
                if with_a:
                    act.wait_ge(pv_mm[0].sem, pv_mm[0].at(pair + 1, 1))
                for b in range(4):
                    act.wait_ge(probT_mm[n].sem, probT_mm[n].at(pair, b + 1))
                    copy(flat(probT[:, b * HB:(b + 1) * HB, :]), bank(b, S, HB * S)).then_inc(probT_sb[n].sem, 1)

            def output_transposes(pair, n, from_):
                act.wait_ge(oT_mm[n].sem, oT_mm[n].at(pair, 1))
                copy(flat(oT[n][:, :, :]), bank(from_, 128, 2 * S)).then_inc(oT_sb[n].sem, 1)

            def b_hnT(pair, n, from_):
                act.wait_ge(hnTB_mm.sem, hnTB_mm.at(pair, n))
                copy(flat(hnTB[:, :, :]), bank(from_, 128, 2 * S)).then_inc(hnTB_sb.sem, 1)

            def b_logits(pair):
                act.wait_ge(logit_mm.sem, logit_mm.at(pair, 1))
                act.activation(flat(el[:, :, :]), bank(5, S, 2 * E0), ACT.Exp, scale=-1.0).then_inc(el_sb.sem, 1)

            def moe(n):
                def step(pair):
                    act.wait_ge(hid_mm.sem, hid_mm.at(pair, n + 1))
                    if n >= 2:
                        act.wait_ge(moe_mm.sem, moe_mm.at(pair, n - 1))
                    act.activation(hidT[:, n % 2, :, :, :].rearrange("p e j s -> p (e j s)"),
                                   bank(HID_BANKS[n % 2], 128, EG * 2 * S), ACT.Relu).then_inc(hid_sb.sem, 1)
                return step

            def b_q(pair, with_a):
                act.wait_ge(qkv_mm[1].sem, qkv_mm[1].at(pair, 1))
                if with_a:
                    act.wait_ge(score_mm[0].sem, score_mm[0].at(pair + 1, 1))
                copy(qT[:, :, :, :].rearrange("p g j s -> p (g j s)"), bank(5, 128, 4 * S),
                     1.0 / math.sqrt(DH)).then_inc(qk_sb[1].sem, 1)

            def b_k(pair):
                act.wait_ge(qkv_mm[1].sem, qkv_mm[1].at(pair, 2))
                copy(kT[:, :, :, :].rearrange("p g j s -> p (g j s)"), bank(5, 128, 4 * S)
                     ).then_inc(qk_sb[1].sem, 1)

            def b_qh(pair):
                if isinstance(pair, int):
                    act.wait_ge(loaded["pk"].sem, 16)
                for m in range(PH // 2):
                    act.wait_ge(qh_mm.sem, qh_mm.at(pair, m + 1))
                    for h in (2 * m, 2 * m + 1):
                        last = act.activation(flat(qhT[:, h, :, :]),
                                              ps[:, QH_BANKS[m], (h % 2) * 2 * S:(h % 2 + 1) * 2 * S], ACT.Identity,
                                              bias=W("pk", "b_q")[:, h:h + 1])
                    last.then_inc(qh_sb.sem, 1)

            def b_softmax(pair):
                act.wait_ge(dif_sb.sem, dif_sb.at(pair, 1))
                act.activation(flat(ez[:, :, :]), flat(ez[:, :, :]), ACT.Exp).then_inc(ez_sb.sem, 1)

            def e_dots(k):
                def tanh(pair):
                    act.wait_ge(gu_sb.sem, gu_sb.at(pair, k + 1))
                    act.activation(gt[:, k % 2, :], gu[:, k % 2, :], ACT.Tanh).then_inc(gt_sb.sem, 1)
                return tanh

            def e_values(k):
                def diagonals(pair):
                    act.wait_ge(val_sb.sem, val_sb.at(pair, k + 1))
                    act.wait_ge(up_mm.sem, up_mm.at(pair, k - 1))
                    for r in range(QK):
                        last = act.activation(diag[:, k % 2, r, :], ident[0:S, 0:S], ACT.Copy,
                                              scale=val[:, k % 2, r:r + 1])
                    last.then_inc(diag_sb.sem, 1)
                return diagonals

            def pieces(with_a):
                return {
                    "a_ck": a_ck, "a_xnT": a_xnT, "a_hnT": a_hnT, "a_cT": a_cT, "a_v": lambda p: values(p, 0, 4),
                    "a_exps": lambda p: exps(p, 0), "a_pT": lambda p: prob_transposes(p, 0),
                    "a_oT": lambda p: output_transposes(p, 0, 4),
                    "b_hnT1": lambda p: b_hnT(p, 1, 5), "b_hnT2": lambda p: b_hnT(p, 2, 5),
                    "b_hnT3": lambda p: b_hnT(p, 3, 5), "b_logits": b_logits,
                    "b_q": lambda p: b_q(p, with_a), "b_k": b_k, "b_v": lambda p: values(p, 1, 5),
                    "b_exps": lambda p: exps(p, 1), "b_pT": lambda p: prob_transposes(p, 1, with_a),
                    "b_oT": lambda p: output_transposes(p, 1, 5), "b_qh": b_qh, "b_softmax": b_softmax,
                    **{f"m{n}": moe(n) for n in range(STEPS)},
                    **{f"e_dots{k}": e_dots(k) for k in range(NQ)},
                    **{f"e_values{k}": e_values(k) for k in range(NQ)},
                }

            act.wait_ge(loaded["tok"].sem, 16)
            act.wait_ge(loaded["at0"].sem, 16)
            copy(ident16[:, :], ident[0:S, 0:S]).then_inc(consts.sem, 1)
            copy(mask16[:, :], W("at0", "mask")).then_inc(consts.sem, 1)
            run(pieces(True), a=0)
            run(pieces(True), b=0, a=1)
            with act.Fori(0, PAIRS - 2) as pair:
                run(pieces(True), e=pair, b=pair + 1, a=pair + 2)
            run(pieces(False), e=PAIRS - 2, b=PAIRS - 1)
            run(pieces(False), e=PAIRS - 1)

        @block.vector
        def _(dve):
            def norm(c, t, srcs, dsts, done):
                np_, n_ = srcs[0].shape[0], len(srcs)
                for n, src in enumerate(srcs):
                    dve.bn_stats(stats[t][0:np_, n, :], src).then_inc(c.sem, 1)
                dve.wait_ge(c.sem, c.after(n_))
                dve.sem_inc(passed_dve, 1)
                for n in range(n_):
                    dve.bn_aggr(mv[t][0:np_, n, :], stats[t][0:np_, n, :]).then_inc(c.sem, 1)
                dve.wait_ge(c.sem, c.after(n_))
                v, y_, a, b = (rs[t][0:np_, 0:n_, q] for q in range(4))
                dve.tensor_scalar(v, mv[t][0:np_, 0:n_, 1], EPS, None, ALU.add).then_inc(c.sem, 1)
                dve.wait_ge(c.sem, c.after(1))
                dve.tensor_scalar(y_.bitcast(I32), v.bitcast(I32), -0.5, RSQRT_MAGIC, ALU.mult, ALU.add
                                  ).then_inc(c.sem, 1)
                for c1, c2 in RSQRT_STEPS:
                    dve.wait_ge(c.sem, c.after(1))
                    dve.scalar_tensor_tensor(a, y_, -c1, y_, ALU.mult, ALU.mult).then_inc(c.sem, 1)
                    dve.wait_ge(c.sem, c.after(1))
                    dve.tensor_tensor(b, a, v, ALU.mult).then_inc(c.sem, 1)
                    dve.wait_ge(c.sem, c.after(1))
                    dve.scalar_tensor_tensor(y_, b, c2, y_, ALU.add, ALU.mult).then_inc(c.sem, 1)
                dve.wait_ge(c.sem, c.after(1))
                for n, (src, dst) in enumerate(zip(srcs, dsts)):
                    last = dve.tensor_scalar(dst, src, mv[t][0:np_, n, 0:1], rs[t][0:np_, n, 1:2],
                                             ALU.subtract, ALU.mult)
                last.then_inc(done.sem, 1)

            def norm_pair(c, t, h, dst, done):
                norm(c, t, [h[:, j, :] for j in range(2)], [dst[:, j, :] for j in range(2)], done)

            def a_x(c, pair):
                dve.wait_ge(xT_mm.sem, xT_mm.at(pair, 1))
                dve.tensor_tensor(xT[:, :, :], bank(4, 128, 2 * NTOK).rearrange("p (j t) -> p j t", j=2),
                                  posb[:, :].unsqueeze(1).broadcast_to([128, 2, NTOK]), ALU.add
                                  ).then_inc(xT_sb.sem, 1)

            def a_cs(c, pair):
                dve.wait_ge(cs_mm.sem, cs_mm.at(pair, 1))
                dve.tensor_tensor(cs[:, :, :], bank(4, NTOK, 24).rearrange("p (j t) -> p j t", j=2),
                                  W("tok", "b_cs").unsqueeze(1).broadcast_to([NTOK, 2, 12]), ALU.add
                                  ).then_inc(c.sem, 1)
                dve.wait_ge(c.sem, c.after(1))
                dve.tensor_tensor(sq[:, :, :], cs[:, :, DC:], cs[:, :, DC:], ALU.mult).then_inc(c.sem, 1)
                dve.wait_ge(c.sem, c.after(1))
                dve.tensor_reduce(ck[:, :, DC:DC + 1], sq[:, :, :], AXX, ALU.add).then_inc(c.sem, 1)
                dve.wait_ge(c.sem, c.after(1))
                dve.tensor_tensor(ck[:, :, 0:DC], cs[:, :, 0:DC], ck[:, :, DC:DC + 1].broadcast_to([NTOK, 2, DC]),
                                  ALU.mult).then_inc(ck_sb.sem, 1)

            def a_enh(c, pair):
                dve.wait_ge(xenh_mm.sem, xenh_mm.at(pair, 1))
                norm(c, 0, [ps[0:NTOK, 4, j * D:(j + 1) * D] for j in range(2)], [xn[:, j, :] for j in range(2)],
                     xn_sb)

            def a_h0(c, pair):
                dve.wait_ge(h0_mm.sem, h0_mm.at(pair, 1))
                dve.tensor_copy(h0[0:NTOK, :, :].rearrange("p j d -> p (j d)"), bank(4, NTOK, 2 * D)
                                ).then_inc(c.sem, 1)
                dve.wait_ge(c.sem, c.after(1))
                dve.wait_ge(txt_in.sem, txt_in.at(pair, 16))
                norm_pair(c, 0, h0, hnA, hnA_sb)

            def a_down(c, pair):
                dve.wait_ge(down_mm.sem, down_mm.at(pair, 1))
                parts = [(j, a, b) for j in range(2) for a, b in ((0, RQ), (RQ, RQ + RKV))]
                norm(c, 0, [ps[0:S, 4, j * 149 + a:j * 149 + b] for j, a, b in parts],
                     [cn[:, j, a:b] for j, a, b in parts], cn_sb)

            def rope(pair, n, t, table, with_b):
                dve.wait_ge(qkv_mm[0].sem, qkv_mm[0].at(pair, n))
                if with_b:
                    dve.wait_ge(score_mm[1].sem, score_mm[1].at(pair - 2, 1))
                dve.tensor_tensor(t[:, :, :, :].rearrange("p g j s -> p (g j) s"),
                                  bank(4, 128, 4 * S).rearrange("p (a s) -> p a s", s=S),
                                  W("at0", table).unsqueeze(1).broadcast_to([128, 4, S]), ALU.mult
                                  ).then_inc(qk_sb[0].sem, 1)

            def maxima(pair, n):
                dve.wait_ge(score_mm[n].sem, score_mm[n].at(pair, 1))
                for q in range(2):
                    dve.tensor_reduce(nmx[n][:, q * HEADS:(q + 1) * HEADS],
                                      ps[0:S, 2 * q:2 * q + 2, 0:HB * S].rearrange("p b (h s) -> p b h s", s=S),
                                      AXX, ALU.max, negate=True).then_inc(nmx_sb[n].sem, 1)

            def normalized(c, pair, n, from_):
                dve.wait_ge(pv_mm[n].sem, pv_mm[n].at(pair, 1))
                pv = bank(from_, S, 2 * HEADS * (DH + 1)).rearrange("p (h d) -> p h d", d=DH + 1)
                dve.reciprocal(rden[n][:, :, :], pv[:, :, DH:DH + 1]).then_inc(c.sem, 1)
                dve.wait_ge(c.sem, c.after(1))
                dve.tensor_tensor(o[n][:, :, :], pv[:, :, 0:DH], rden[n][:, :, :].broadcast_to([S, 2 * HEADS, DH]),
                                  ALU.mult).then_inc(o_sb[n].sem, 1)

            def flat(t):
                return t.rearrange("p j d -> p (j d)")

            def a_out(c, pair):
                dve.wait_ge(out_mm[0].sem, out_mm[0].at(pair, 1))
                dve.tensor_tensor(flat(h1[:, :, :]), flat(h0[:, :, :]), bank(4, S, 2 * D), ALU.add
                                  ).then_inc(h1_sb.sem, 1)

            def b_norm1(c, pair):
                dve.wait_ge(h1_sb.sem, h1_sb.at(pair, 1))
                norm_pair(c, 1, h1, hnB, hnB_sb)

            def b_router(c, pair):
                dve.wait_ge(el_sb.sem, el_sb.at(pair, 1))
                dve.tensor_scalar(el[:, :, :], el[:, :, :], 1.0, None, ALU.add).then_inc(c.sem, 1)
                dve.wait_ge(c.sem, c.after(1))
                dve.reciprocal(sel[:, :, :], el[:, :, :]).then_inc(c.sem, 1)
                dve.wait_ge(c.sem, c.after(1))
                dve.sem_inc(passed_dve, 1)
                for j in range(2):
                    dve.max(selmax[:, j, :], sel[:, j, :]).then_inc(c.sem, 1)
                dve.wait_ge(c.sem, c.after(2))
                dve.sem_inc(passed_dve, 1)
                for j in range(2):
                    dve.max_index(selidx[:, j, :], selmax[:, j, :], sel[:, j, :]).then_inc(c.sem, 1)
                dve.wait_ge(c.sem, c.after(2))
                dve.tensor_copy(selidf[:, :, :], selidx[:, :, :]).then_inc(c.sem, 1)
                dve.wait_ge(c.sem, c.after(1))
                for j in range(2):
                    for t in range(2):
                        dve.tensor_scalar(wm[:, t, j, :], W("moe", "iota"), selidf[:, j, t:t + 1],
                                          selmax[:, j, t:t + 1], ALU.is_equal, ALU.mult).then_inc(c.sem, 1)
                dve.wait_ge(c.sem, c.after(4))
                dve.tensor_tensor(wmoe[:, :, :], wm[:, 0, :, :], wm[:, 1, :, :], ALU.add).then_inc(c.sem, 1)
                dve.wait_ge(c.sem, c.after(1))

            def moe(n):
                def step(c, pair):
                    m = n - 1
                    dve.wait_ge(moe_mm.sem, moe_mm.at(pair, m + 1))
                    for q in range(EG):
                        e = m * EG + q
                        for j in range(2):
                            if e > 0:
                                dve.wait_ge(c.sem, c.before(1))
                            col = (2 * q + j) * D
                            dve.scalar_tensor_tensor(h2[:, j, :], ps[0:S, m % 2, col:col + D],
                                                     wmoe[:, j, e:e + 1], (h1 if e == 0 else h2)[:, j, :],
                                                     ALU.mult, ALU.add).then_inc(c.sem, 1)
                            c.after(1)
                    dve.wait_ge(c.sem, c.after(0))
                    dve.sem_inc(moe_sb.sem, 1)
                return step

            def b_norm2(c, pair):
                norm_pair(c, 1, h2, hnB, hnB_sb)

            def b_out(c, pair):
                dve.wait_ge(out_mm[1].sem, out_mm[1].at(pair, 1))
                dve.tensor_tensor(flat(h2[:, :, :]), flat(h2[:, :, :]), bank(5, S, 2 * D), ALU.add
                                  ).then_inc(c.sem, 1)
                dve.wait_ge(c.sem, c.after(1))
                norm_pair(c, 1, h2, qnext, hnB_sb)

            def b_keys(j):
                def top(c, pair):
                    def keys(m):
                        return [(4 * m + q, half, ps[0:S, 2 * m + half, q * NE:(q + 1) * NE])
                                for half in range(2) for q in range(4)]

                    maxed = []
                    for m in range(2):
                        dve.wait_ge(sub_mm.sem, sub_mm.at(pair, j * 2 + m + 1))
                        dve.sem_inc(passed_dve, 1)
                        for h, half, scores in keys(m):
                            dve.max(s8[:, j, h, half, :], scores).then_inc(c.sem, 1)
                        maxed.append(c.after(8))
                    for m in range(2):
                        dve.wait_ge(c.sem, maxed[m])
                        dve.sem_inc(passed_dve, 1)
                        for h, half, scores in keys(m):
                            last = dve.max_index(i8[:, j, h, half, :], s8[:, j, h, half, :], scores)
                        last.then_inc(sub_read.sem, 1)
                return top

            def b_best(j):
                def best_rows(c, pair):
                    hs = slice(j * PH, (j + 1) * PH)
                    grid = [S, PH, TOPK, TOPK]
                    dve.tensor_tensor(sums[:, :, :, :], s8[:, j, :, 0, :].unsqueeze(3).broadcast_to(grid),
                                      s8[:, j, :, 1, :].unsqueeze(2).broadcast_to(grid), ALU.add
                                      ).then_inc(c.sem, 1)
                    dve.wait_ge(c.sem, c.after(1))
                    dve.sem_inc(passed_dve, 1)
                    for h in range(PH):
                        dve.max(best[:, j * PH + h, :], sums[:, h, :, :].rearrange("p a b -> p (a b)")
                                ).then_inc(c.sem, 1)
                    dve.wait_ge(c.sem, c.after(PH))
                    dve.sem_inc(passed_dve, 1)
                    for h in range(PH):
                        dve.max_index(bpos[:, j * PH + h, :], best[:, j * PH + h, :],
                                      sums[:, h, :, :].rearrange("p a b -> p (a b)")).then_inc(c.sem, 1)
                    dve.wait_ge(c.sem, c.after(PH))
                    dve.tensor_scalar(place[0][:, hs, :], bpos[:, hs, :], 3, None, ALU.logical_shift_right
                                      ).then_inc(c.sem, 1)
                    dve.tensor_scalar(place[1][:, hs, :], bpos[:, hs, :], 7, None, ALU.bitwise_and
                                      ).then_inc(c.sem, 1)
                    dve.wait_ge(sub_read.sem, sub_read.at(pair, 2 * j + 2))
                    for t in range(2):
                        dve.wait_ge(c.sem, c.after(1))
                        dve.tensor_tensor(onehot[t], place[t][:, hs, :].unsqueeze(3).broadcast_to(grid),
                                          W("pk", "iota").unsqueeze(1).unsqueeze(1).broadcast_to(grid),
                                          ALU.is_equal).then_inc(c.sem, 1)
                    for t in range(2):
                        dve.wait_ge(c.sem, c.after(1))
                        dve.tensor_tensor(onehot[t], onehot[t], i8[:, j, :, t, :].unsqueeze(2).broadcast_to(grid),
                                          ALU.mult).then_inc(c.sem, 1)
                    for t in range(2):
                        dve.wait_ge(c.sem, c.after(1))
                        dve.tensor_reduce(picked[t][:, :, :], onehot[t], AXX, ALU.add).then_inc(c.sem, 1)
                    dve.wait_ge(c.sem, c.after(2))
                    dve.scalar_tensor_tensor(idxf[:, j, :], picked[0][:, :, :].rearrange("p h k -> p (h k)"),
                                             float(NE), picked[1][:, :, :].rearrange("p h k -> p (h k)"),
                                             ALU.mult, ALU.add).then_inc(c.sem, 1)
                    dve.wait_ge(c.sem, c.after(1))
                return best_rows

            def b_softmax(c, pair):
                if not isinstance(pair, int) or pair > 0:
                    dve.wait_ge(gathered[SLOTS - 1].sem, gathered[SLOTS - 1].at(pair - 1, 16 * QK))
                dve.tensor_copy(idx[0:S, 0, :], idxf[:, 0, :]).then_inc(idx_ready[0].sem, 1)
                dve.tensor_tensor(ez[:, :, :], best[:, :, :], best[:, :, 0:1].broadcast_to([S, 2 * PH, TOPK]),
                                  ALU.subtract).then_inc(dif_sb.sem, 1)
                dve.wait_ge(ez_sb.sem, ez_sb.at(pair, 1))
                dve.tensor_reduce(esum[:, :, :], ez[:, :, :], AXX, ALU.add).then_inc(c.sem, 1)
                dve.wait_ge(c.sem, c.after(1))
                dve.reciprocal(esum[:, :, :], esum[:, :, :]).then_inc(c.sem, 1)
                dve.wait_ge(c.sem, c.after(1))
                dve.tensor_tensor(wnext[:, :, :].rearrange("p j (h k) -> p (j h) k", k=TOPK), ez[:, :, :],
                                  esum[:, :, :].broadcast_to([S, 2 * PH, TOPK]), ALU.mult).then_inc(c.sem, 1)
                dve.wait_ge(c.sem, c.after(1))

            def e_take(c, pair):
                dve.wait_ge(y_sb.sem, y_sb.at(pair, 0))
                dve.tensor_copy(idx[0:S, 1, :], idxf[:, 1, :]).then_inc(idx_ready[1].sem, 1)
                dve.tensor_copy(wcur[:, :, :], wnext[:, :, :]).then_inc(c.sem, 1)
                dve.tensor_copy(qcur, qnext[:, :, :]).then_inc(c.sem, 1)
                dve.tensor_copy(hcur[:, :, :], h2[:, :, :]).then_inc(c.sem, 1)
                dve.wait_ge(c.sem, c.after(3))

            def e_dots(k):
                def dots(c, pair):
                    b = k % 2
                    dve.wait_ge(gathered[k % SLOTS].sem, gathered[k % SLOTS].at(pair, 16 * QK * (k // SLOTS + 1)))
                    for r in range(QK):
                        row = ring[0:S, k % SLOTS, r, 0:D]
                        dve.tensor_tensor_reduce(out=row, in0=row, in1=qcur[:, k // HQ, :], scale=1.0, scalar=0.0,
                                                 op0=ALU.mult, op1=ALU.add, accum_out=xd[:, b, r:r + 1]
                                                 ).then_inc(c.sem, 1)
                    dve.wait_ge(c.sem, c.after(QK))
                    dve.tensor_tensor(ga[:, b, :], xd[:, b, :], xd[:, b, :], ALU.mult).then_inc(c.sem, 1)
                    dve.wait_ge(c.sem, c.after(1))
                    dve.tensor_scalar(gb[:, b, :], ga[:, b, :], GELU_B, GELU_A, ALU.mult, ALU.add
                                      ).then_inc(c.sem, 1)
                    dve.wait_ge(c.sem, c.after(1))
                    dve.tensor_tensor(gu[:, b, :], gb[:, b, :], xd[:, b, :], ALU.mult).then_inc(gu_sb.sem, 1)
                return dots

            def e_values(k):
                def values(c, pair):
                    j, b, at = k // HQ, k % 2, (k % HQ) * QK
                    dve.wait_ge(gt_sb.sem, gt_sb.at(pair, k + 1))
                    dve.scalar_tensor_tensor(gv[:, b, :], gt[:, b, :], 1.0, xd[:, b, :], ALU.add, ALU.mult
                                             ).then_inc(c.sem, 1)
                    dve.wait_ge(c.sem, c.after(1))
                    dve.scalar_tensor_tensor(val[:, b, :], gv[:, b, :], 0.5, wcur[:, j, at:at + QK],
                                             ALU.mult, ALU.mult).then_inc(val_sb.sem, 1)
                return values

            def e_sum(j):
                def total(c, pair):
                    dve.wait_ge(up_mm.sem, up_mm.at(pair, (j + 1) * HQ))
                    dve.wait_ge(stored[j].sem, stored[j].at(pair, 0))
                    dve.tensor_tensor(y[:, j, :], hcur[:, j, :], ps[0:S, 7, j * D:(j + 1) * D], ALU.add
                                      ).then_inc(y_sb.sem, 1)
                return total

            def chains(e=None, b=None, a=None):
                chain = {k: Chain(s, p) for k, s, p in (("a", steps_a, a), ("b", steps_b, b), ("e", steps_e, e))
                         if p is not None}
                with_b = a is not None and e is not None
                table = {
                    "a_x": a_x, "a_cs": a_cs, "a_enh": a_enh, "a_h0": a_h0, "a_down": a_down,
                    "a_q": lambda c, p: rope(p, 1, qT, "rope_q", with_b),
                    "a_k": lambda c, p: rope(p, 2, kT, "rope_k", with_b),
                    "a_scores": lambda c, p: maxima(p, 0),
                    "a_pv": lambda c, p: normalized(c, p, 0, 4), "a_out": a_out,
                    "b_norm1": b_norm1, "b_router": b_router, "b_norm2": b_norm2,
                    "b_scores": lambda c, p: maxima(p, 1), "b_pv": lambda c, p: normalized(c, p, 1, 5),
                    "b_out": b_out, "b_keys0": b_keys(0), "b_best0": b_best(0),
                    "b_keys1": b_keys(1), "b_best1": b_best(1), "b_softmax": b_softmax,
                    "e_take": e_take, "e_sum0": e_sum(0), "e_sum1": e_sum(1),
                    **{f"m{n}": moe(n) for n in range(1, STEPS + 1)},
                    **{f"e_dots{k}": e_dots(k) for k in range(NQ)},
                    **{f"e_values{k}": e_values(k) for k in range(NQ)},
                }

                def bound(name):
                    c = chain.get("b" if name[0] == "m" else name[0])
                    return lambda p: table[name](c, p)

                run({name: bound(name) for name in table}, e=e, b=b, a=a)
                for c in chain.values():
                    c.end()

            for n in range(2):
                dve.memset(vA[n][:, :, DH:DH + 1], 1.0).then_inc(consts.sem, 1)
            dve.memset(idx[:, :, :], 0).then_inc(consts.sem, 1)
            dve.sem_inc(y_sb.sem, 2)
            dve.wait_ge(loaded["tok"].sem, 16)
            dve.tensor_scalar(posb[:, :], W("tok", "pos"), W("tok", "b_patch"), None, ALU.add
                              ).then_inc(consts.sem, 1)
            dve.wait_ge(consts.sem, N_CONSTS)
            chains(a=0)
            chains(b=0, a=1)
            with dve.Fori(0, PAIRS - 2) as pair:
                chains(e=pair, b=pair + 1, a=pair + 2)
            chains(e=PAIRS - 2, b=PAIRS - 1)
            chains(e=PAIRS - 1)


def _pack(pack, parts):
    cols, width = columns(pack)
    out = np.zeros((128, width), np.float32)
    for name, (r, n) in PACKS[pack].items():
        out[0:r, cols[name]:cols[name] + n] = parts[name].reshape(r, n)
    return out


def _rope_tables():
    t = np.arange(S, dtype=np.float32)
    cos, sin = np.cos(t), np.sin(t)
    tq = [cos, cos, -sin, -sin, cos, cos, sin, sin]
    tk = [cos, -sin, cos, -sin, cos, sin, cos, sin]
    out = []
    for rows_ in (tq, tk):
        a = np.zeros((4, HROWS, S), np.float32)
        a[:, 0:DH] = 1.0
        a[:, DH:DH + 8] = np.stack(rows_)
        out.append(a.reshape(128, S))
    return out


ROPE_Q = [0, 0, 1, 1, 1, 1, 0, 0]
ROPE_K = [0, 1, 0, 1, 1, 0, 1, 0]


def _head_rows(w, rope=None, order=None):
    n = (w if w is not None else rope).shape[0]
    out = np.zeros((n, HEADS, HROWS), np.float32)
    if w is not None:
        out[:, :, 0:DH] = w.reshape(n, HEADS, DH)
    if rope is not None:
        out[:, :, DH:DH + 8] = rope.reshape(n, HEADS, 2)[:, :, order]
    return out.reshape(n, HEADS * HROWS)


def _layouts(i):
    i = {k: np.asarray(v) for k, v in i.items()}
    tq, tk = _rope_tables()
    tq = tq * np.float32(1 / math.sqrt(DH + 2))
    s, t = np.arange(S)[None, :], np.arange(S)[:, None]
    kv = i["L0_attn_W_ukv"]
    w1 = i["L1_attn_w_qkv"].reshape(3, D, D).transpose(0, 2, 1)
    packs = {
        "tok": {
            "w_patch": i["L0_tok_W_patch"].reshape(KCH, 128, D).transpose(1, 0, 2),
            "pos": i["L0_tok_pos_embed"][0].T, "b_patch": i["L0_tok_b_patch"],
            "w_cs": np.concatenate([i["L0_tok_W_coord"], i["L0_tok_W_spinor"]], 1),
            "b_cs": np.tile(np.concatenate([i["L0_tok_b_coord"], i["L0_tok_b_spinor"]])[None], (NTOK, 1)),
            "w_emb": np.concatenate([i["L0_tok_W_embed"], i["L0_tok_b_embed"][None]], 0),
            "ident": np.eye(128, dtype=np.float32), "ln_g": i["L0_tok_ln_gamma"], "ln_b": i["L0_tok_ln_beta"],
            "w_out": i["L0_tok_W_out"], "b_out": i["L0_tok_b_out"], "ones": np.ones(128, np.float32)},
        "at0": {
            "w_down": np.concatenate([i["L0_attn_W_dq"], i["L0_attn_W_dkv"]], 1),
            "q_g": i["L0_attn_q_ln_g"], "q_b": i["L0_attn_q_ln_b"],
            "kv_g": i["L0_attn_kv_ln_g"], "kv_b": i["L0_attn_kv_ln_b"],
            "w_q": _head_rows(i["L0_attn_W_uq"], i["L0_attn_W_qr"], ROPE_Q),
            "w_k": _head_rows(kv[:, 0:D]), "w_kr": _head_rows(None, i["L0_attn_W_kr"], ROPE_K),
            "w_v": kv[:, D:2 * D], "w_o": i["L0_attn_W_o"].T,
            "rope_q": tq, "rope_k": tk, "mask": np.where(s > t, np.float32(MASKED), np.float32(0.0))},
        "moe": {
            "sel": i["L0_ffn_expert_sel"].T,
            "iota": np.tile(np.arange(E0, dtype=np.float32)[None], (S, 1)),
            "keys": i["L0_ffn_keys"].transpose(1, 0, 2), "values": i["L0_ffn_values"].transpose(1, 0, 2)},
        "at1": {
            "w_q": _head_rows(w1[0]), "w_k": _head_rows(w1[1]), "w_v": w1[2],
            "w_o": i["L1_attn_w_agg"].T, "b_o": i["L1_attn_b_agg"]},
        "pk": {
            "w_q": i["L1_ffn_Wq"].T, "b_q": i["L1_ffn_bq"].reshape(PH, 128).T,
            "keys": i["L1_ffn_keys"].transpose(1, 3, 0, 2),
            "iota": np.tile(np.arange(TOPK, dtype=np.float32)[None], (S, 1))},
    }
    x = i["x"].reshape(PAIRS, 2, CH, SIDE, PATCH, SIDE, PATCH).transpose(0, 2, 4, 6, 1, 3, 5)
    x = x.reshape(PAIRS, KCH, 128, 2 * NTOK).transpose(0, 2, 1, 3).reshape(PAIRS, 128, KCH * 2 * NTOK)
    return {
        "patches": np.ascontiguousarray(x),
        "txt": np.ascontiguousarray(i["txt"]),
        "rows": np.concatenate([i["L1_ffn_w_down_embed"], i["L1_ffn_w_up_embed"]], 1),
        **{"pack_" + k: _pack(k, v) for k, v in packs.items()},
    }


def kernel(**inputs):
    import concourse.bacc as bacc
    from concourse.bass_utils import run_bass_kernel_spmd

    arrays = _layouts(inputs)
    nc = bacc.Bacc("TRN2", target_bir_lowering=False, num_devices=1)
    aps = {n: nc.dram_tensor(n, a.shape, mybir.dt.from_np(a.dtype), kind="ExternalInput").ap()
           for n, a in arrays.items()}
    out = nc.dram_tensor("out", (B, S, D), F32, kind="ExternalOutput").ap()
    fusion_program(nc, aps["patches"], aps["txt"], {k: aps["pack_" + k] for k in PACKS}, aps["rows"], out)
    result = run_bass_kernel_spmd(nc, [arrays], core_ids=[0])
    return result.results[0]["out"]
```

```python
import math
from contextlib import ExitStack

import concourse.bass as bass
import numpy as np
from concourse import mybir

F32 = mybir.dt.float32
BF16 = mybir.dt.bfloat16
U32 = mybir.dt.uint32
I32 = mybir.dt.int32
ALU = mybir.AluOpType
ACT = mybir.ActivationFunctionType
AXX = mybir.AxisListType.X

B, D = 32, 128
PAIRS = B // 2
IMG, PATCH, CH = 112, 16, 3
SIDE = IMG // PATCH
NTOK = SIDE * SIDE
NTXT = 77
S = NTOK + NTXT
KCH = CH * PATCH * PATCH // 128
DC, DS = 8, 4
HEADS, DH = 8, 16
HB = 4
RQ, RKV = 64, 85
HROWS = 32
E0, H0 = 32, 128
SLOT_OF = [(j, g) for j in range(2) for g in range(2)]
EG = 2
STEPS = E0 // EG
PH, NE, TOPK, HALF = 8, 128, 8, 64
KPT = PH * TOPK
QK = 16
QUARTERS = 2 * KPT // QK
HK = QK // 2
A_STEPS, B_STEPS, E_STEPS, X_STEPS = 45, 175, 155, 29
E_MAIN = E_STEPS - (QK + 3)
N_CONSTS = 6
SLOTS = 4
EPS = 1e-5
MASKED = -1e30
RSQRT_MAGIC = float(0x5F1FFFF9)
RSQRT_STEPS = [(0.703952253, 0.703952253 * 2.38924456), (0.5 * (1 + 3.2e-7), 1.5 * (1 + 3.2e-7))]
GELU_A, GELU_B = math.sqrt(2 / math.pi), 0.044715 * math.sqrt(2 / math.pi)

SCHEDULE = {
    "pe": """
        a_x b_hnT1 a_cs z_up7a b_logits a_ck m0 a_enh z_up7b m1 m2 a_xnT m3 a_h0 m4 m5 a_hnT m6 a_down
        m7 m8 a_cT m9 m10 m11 a_q m12 m13 m14 m15 m16 a_k e_up0a a_v a_scoresa a_scoresb b_hnT2 e_up0b
        b_q a_pTa b_k a_pTb a_pva a_pvb b_v b_scoresa b_scoresb e_up1a e_up1b e_up2a b_pTa b_pTb b_pva
        b_pvb b_oT b_out a_oT e_up2b e_up3a b_hnT3 e_up3b b_qha b_qhb b_keys0a b_keys1a a_out e_up4a
        e_up4b e_up5a e_up5b e_up6a e_up6b
    """.split(),
    "act": """
        z_dots7b z_values7a z_values7b b_hnT1 b_logits a_ck m0 m1 m2 a_xnT m3 m4 m5 a_hnT m6 m7 m8 m9
        a_cT m10 m11 e_dots0b m12 m13 m14 m15 e_values0a e_values0b a_v b_hnT2 a_expsa a_expsb b_q
        x_softmax a_pTa a_pTb b_k e_dots1b e_values1a e_values1b b_v e_dots2b e_values2a b_expsa
        b_expsb b_pTa b_pTb e_values2b e_dots3b e_values3a b_oT e_values3b e_dots4b b_hnT3 b_qha b_qhb
        a_oT e_values4a e_values4b e_dots5b b_softmax e_values5a e_values5b e_dots6b e_values6a
        e_values6b
    """.split(),
    "dve": """
        z_dots7a z_dots7b z_values7a b_norm1 a_x a_cs b_router a_enh z_sum1 m1 e_take m2 m3 a_h0 m4
        e_dots0a m5 m6 a_down m7 m8 m9 e_dots0b m10 m11 a_q e_values0a m12 m13 m14 m15 m16 a_k b_norm2
        x_best1a a_scoresb x_best1b x_softmax x_idx1 e_dots1a e_dots1b e_values1a e_dots2a a_pvb
        e_dots2b e_values2a e_dots3a b_scoresb e_dots3b e_values3a b_pvb e_dots4a b_out e_dots4b
        e_sum0 e_values4a e_dots5a e_dots5b b_keys0a b_keys0b b_best0a b_best0b b_keys1a b_keys1b
        a_out e_values5a b_idx0 b_softmax e_dots6a e_dots6b e_values6a
    """.split(),
}
START = {
    "pe": """
        a_x b_hnT1 a_cs b_logits a_ck m0 a_enh m1 m2 a_xnT m3 a_h0 m4 m5 a_hnT m6 a_down m7 m8 a_cT m9
        m10 a_q m11 m12 m13 m14 m15 m16 a_k a_v a_scoresa b_hnT2 a_scoresb b_q b_k a_pTa a_pTb b_v
        b_scoresa b_scoresb a_pva a_pvb b_pTa b_pTb b_pva b_pvb b_oT a_oT b_out b_hnT3 a_out b_qha
        b_qhb b_keys0a b_keys1a
    """.split(),
    "act": """
        b_hnT1 b_logits a_ck m0 m1 m2 a_xnT m3 m4 m5 m6 a_hnT m7 m8 a_cT m9 m10 m11 m12 m13 m14 m15
        a_v b_hnT2 b_q a_expsa b_k a_expsb a_pTa a_pTb b_v b_expsa b_expsb b_pTa b_pTb b_oT a_oT
        b_hnT3 b_qha b_qhb b_softmax
    """.split(),
    "dve": """
        b_norm1 a_x a_cs b_router a_enh m1 m2 m3 a_h0 m4 m5 m6 a_down m7 m8 m9 m10 m11 m12 m13 m14 a_q
        m15 m16 a_k b_norm2 a_scoresb b_scoresb a_pvb b_pvb b_out a_out b_keys0a b_keys0b b_best0a
        b_best0b b_idx0 b_keys1a b_keys1b b_softmax
    """.split(),
}

PACKS = {
    "tok": {"w_patch": (128, KCH * D), "pos": (128, NTOK), "b_patch": (128, 1), "w_cs": (128, DC + DS),
            "b_cs": (NTOK, DC + DS), "w_emb": (DC + 1, D), "ident": (128, 128), "ln_g": (128, 1),
            "ln_b": (128, 1), "w_out": (128, D), "b_out": (1, D), "ones": (1, 128)},
    "at0": {"w_down": (128, RQ + RKV), "q_g": (RQ, 1), "q_b": (RQ, 1), "kv_g": (RKV, 1), "kv_b": (RKV, 1),
            "w_q": (RQ, 256), "w_k": (RKV, 256), "w_kr": (128, 256), "w_v": (RKV, D), "w_o": (128, D),
            "rope_q": (128, S), "rope_k": (128, S), "mask": (S, S)},
    "moe": {"sel": (128, E0), "iota": (S, E0), "keys": (128, E0 * H0), "values": (128, E0 * D)},
    "at1": {"w_q": (128, 256), "w_k": (128, 256), "w_v": (128, D), "w_o": (128, D), "b_o": (1, D)},
    "pk": {"w_q": (128, PH * 128), "b_q": (128, PH), "keys": (128, PH * NE), "iota": (S, TOPK)},
}


def columns(pack):
    at, out = 0, {}
    for name, (_, n) in PACKS[pack].items():
        out[name] = at
        at += n
    return out, at


class Signal:

    def __init__(self, sem, per, credit=0):
        self.sem, self.per, self.credit = sem, per, credit

    def at(self, pair, n):
        return pair * self.per + (n + self.credit)


class Chain:

    def __init__(self, steps, pair, start=0, end=None):
        self.steps, self.pair, self.n, self.sem = steps, pair, start, steps.sem
        self.last = steps.per if end is None else end

    def after(self, n):
        self.n += n
        assert self.n <= self.steps.per
        return self.steps.at(self.pair, self.n)

    def before(self, n):
        return self.steps.at(self.pair, self.n - n)

    def end(self):
        assert self.n == self.last, (self.n, self.last)


def fusion_program(nc, patches, txt, packs, rows, out):
    ctx = ExitStack()
    with ctx:
        def sb(name, shape, dt=F32):
            return ctx.enter_context(nc.sbuf_tensor("s_" + name, shape, dt))

        def signal(name, per, credit=0):
            return Signal(ctx.enter_context(nc.semaphore(name)), per, credit)

        where, packed = {}, {}
        for pack in PACKS:
            cols, width = columns(pack)
            packed[pack] = sb("w_" + pack, [128, width])
            for name, (r, n) in PACKS[pack].items():
                where[pack, name] = packed[pack][0:r, cols[name]:cols[name] + n]

        def W(pack, name):
            return where[pack, name]

        ident = W("tok", "ident")
        posb = sb("posb", [128, NTOK])
        ident16 = sb("ident16", [S, S], BF16)
        mask16 = sb("mask16", [S, S], BF16)

        pT = sb("patches", [128, KCH, 2 * NTOK])
        xT = sb("xT", [128, 2, NTOK])
        cs = sb("cs", [NTOK, 2, DC + DS])
        sq = sb("sq", [NTOK, 2, DS])
        ck = sb("ck", [NTOK, 2, DC + 1])
        ckT = sb("ckT", [DC + 1, 2, NTOK])
        xnT = sb("xnT", [128, 2, NTOK])
        h0 = sb("h0", [S, 2, D])
        hnA = sb("hnA", [S, 2, D])
        xn = hnA[0:NTOK, :, :]
        hnTA = sb("hnTA", [128, 2, S])
        cn = sb("cn", [S, 2, RQ + RKV])
        cqT = sb("cqT", [RQ, 2, S])
        ckvT = sb("ckvT", [RKV, 2, S])
        h1 = sb("h1", [S, 2, D])
        qT = sb("qT", [128, 2, 2, S])
        kT = sb("kT", [128, 2, 2, S])
        prob = sb("prob", [S, 2 * HEADS, S])
        probT = sb("probT", [S, 2 * HEADS, S])
        vA = [sb(f"vA{n}", [S, 2 * HEADS, DH + 1]) for n in range(2)]
        nmx = [sb(f"nmx{n}", [S, 2 * HEADS]) for n in range(2)]
        rden = [sb(f"rden{n}", [S, 2 * HEADS, 1]) for n in range(2)]
        o = [sb(f"o{n}", [S, 2 * HEADS, DH]) for n in range(2)]
        oT = [sb(f"oT{n}", [128, 2, S]) for n in range(2)]
        stats = [sb(f"stats{n}", [S, 4, 6]) for n in range(2)]
        mv = [sb(f"mv{n}", [S, 4, 2]) for n in range(2)]
        rs = [sb(f"rs{n}", [S, 4, 4]) for n in range(2)]

        hnB = sb("hnB", [S, 2, D])
        hnTB = sb("hnTB", [128, 2, S])
        h2 = sb("h2", [S, 2, D])
        el = sb("el", [S, 2, E0])
        sel = sb("sel", [S, 2, E0])
        selmax = sb("selmax", [S, 2, 8])
        selidx = sb("selidx", [S, 2, 8], U32)
        selidf = sb("selidf", [S, 2, 8])
        wm = sb("wm", [S, 2, 2, E0])
        wmoe = sb("wmoe", [S, 2, E0])
        hidT = sb("hidT", [128, 2, EG, 2, S])
        qhT = sb("qhT", [128, PH, 2, S])
        s8 = sb("s8", [S, 2, PH, 2, TOPK])
        i8 = sb("i8", [S, 2, PH, 2, TOPK], U32)
        sums = sb("sums", [S, PH, TOPK, TOPK])
        best = sb("best", [S, 2 * PH, TOPK])
        bpos = sb("bpos", [S, 2 * PH, TOPK], U32)
        place = [sb(f"place{n}", [S, 2 * PH, TOPK], U32) for n in range(2)]
        onehot = [probT[:, 4 * n:4 * n + 5, :].rearrange("p a b -> p (a b)")[:, 8 * n:8 * n + PH * TOPK * TOPK]
                  .rearrange("p (h k a) -> p h k a", h=PH, k=TOPK) for n in range(2)]
        picked = [sb(f"picked{n}", [S, PH, TOPK]) for n in range(2)]
        idxf = sb("idxf", [S, 2, KPT])
        ez = sb("ez", [S, 2 * PH, TOPK])
        esum = sb("esum", [S, 2 * PH, 1])
        wnext = sb("wnext", [S, KPT])
        qnext = sb("qnext", [S, 2, D])

        idx = sb("idx", [128, 2, KPT], U32)
        ring = sb("ring", [128, SLOTS, QK, 2 * D])
        wcur = sb("wcur", [S, 2, KPT])
        hcur = sb("hcur", [S, 2, D])
        xd, ga, gb, gu, gt, gv, val = (sb(n, [S, 2, QK]) for n in ("xd", "ga", "gb", "gu", "gt", "gv", "val"))
        diag = sb("diag", [S, 2, QK, S])
        y = sb("y", [S, 2, D])

        ps = ctx.enter_context(nc.psum_tensor("ps", [128, 8, 512], F32))
        qcur = ps[0:S, 6, 0:2 * D].rearrange("p (j d) -> p j d", j=2)

        HID_BANKS, QH_BANKS = (2, 5), (5, 2, 3, 5)

        def bank(n, rows_, width):
            return ps[0:rows_, n, 0:width]

        loaded = {pack: signal("loaded_" + pack, 0) for pack in PACKS}
        consts = signal("consts", 0)
        passed_pool, passed_pe, passed_dve = (
            ctx.enter_context(nc.semaphore("passed_" + e)) for e in ("pool", "pe", "dve"))
        patches_in = signal("patches_in", 16)
        txt_in = signal("txt_in", 16)
        xT_mm = signal("xT_mm", 1)
        xT_sb = signal("xT_sb", 1)
        cs_mm = signal("cs_mm", 1)
        ck_sb = signal("ck_sb", 1)
        ckT_mm = signal("ckT_mm", 1)
        ckT_sb = signal("ckT_sb", 1)
        xenh_mm = signal("xenh_mm", 1)
        xn_sb = signal("xn_sb", 1)
        xnT_mm = signal("xnT_mm", 1)
        xnT_sb = signal("xnT_sb", 1)
        h0_mm = signal("h0_mm", 1)
        hnA_sb, hnTA_mm, hnTA_sb = signal("hnA_sb", 1), signal("hnTA_mm", 1), signal("hnTA_sb", 1)
        hnB_sb, hnTB_mm, hnTB_sb = signal("hnB_sb", 3), signal("hnTB_mm", 3), signal("hnTB_sb", 3)
        down_mm = signal("down_mm", 1)
        cn_sb = signal("cn_sb", 1)
        cT_mm = signal("cT_mm", 1)
        cT_sb = signal("cT_sb", 1)
        qkv_mm = [signal(f"qkv_mm{n}", 3) for n in range(2)]
        qk_sb = [signal(f"qk_sb{n}", 2) for n in range(2)]
        v_sb = [signal(f"v_sb{n}", 1) for n in range(2)]
        score_mm = [signal(f"score_mm{n}", 1) for n in range(2)]
        nmx_sb = [signal(f"nmx_sb{n}", 2) for n in range(2)]
        exp_sb = [signal(f"exp_sb{n}", 4) for n in range(2)]
        probT_mm = [signal(f"probT_mm{n}", 4) for n in range(2)]
        probT_sb = [signal(f"probT_sb{n}", 4) for n in range(2)]
        pv_mm = [signal(f"pv_mm{n}", 1) for n in range(2)]
        o_sb = [signal(f"o_sb{n}", 1) for n in range(2)]
        oT_mm = [signal(f"oT_mm{n}", 1) for n in range(2)]
        oT_sb = [signal(f"oT_sb{n}", 1) for n in range(2)]
        out_mm = [signal(f"out_mm{n}", 1) for n in range(2)]
        h1_sb = signal("h1_sb", 1)
        logit_mm = signal("logit_mm", 1)
        el_sb = signal("el_sb", 1)
        hid_mm = signal("hid_mm", STEPS)
        hid_sb = signal("hid_sb", STEPS)
        moe_mm = signal("moe_mm", STEPS)
        moe_sb = signal("moe_sb", STEPS)
        qh_mm = signal("qh_mm", PH // 2)
        qh_sb = signal("qh_sb", PH // 2)
        sub_mm = signal("sub_mm", 4)
        sub_read = signal("sub_read", 4)
        dif_sb = signal("dif_sb", 2)
        ez_sb = signal("ez_sb", 2)
        idx_ready = [signal(f"idx_ready{n}", 1) for n in range(2)]
        gathered = [signal(f"gathered{n}", 2 * 16 * QK) for n in range(SLOTS)]
        gu_sb = signal("gu_sb", QUARTERS)
        gt_sb = signal("gt_sb", QUARTERS)
        val_sb = signal("val_sb", QUARTERS)
        diag_sb = signal("diag_sb", 2 * QUARTERS)
        up_mm = signal("up_mm", QUARTERS, credit=QUARTERS)
        y_sb = signal("y_sb", 2, credit=2)
        stored = [signal(f"stored{n}", 16, credit=16) for n in range(2)]
        rows_sb = signal("rows_sb", 1)
        steps_a = signal("steps_a", A_STEPS)
        steps_b = signal("steps_b", B_STEPS)
        steps_e = signal("steps_e", E_STEPS)
        steps_x = signal("steps_x", X_STEPS)

        block = ctx.enter_context(nc.Block())

        NQ, HQ = QUARTERS, QUARTERS // 2

        def run(order, pieces, z=None, e=None, b=None, a=None):
            pair_of = {"a": a, "b": b, "m": b, "e": e, "x": e, "z": z}
            for name in order:
                if pair_of[name[0]] is not None:
                    pieces[name](pair_of[name[0]])

        def ez_of(k):
            return "e" if k < NQ - 1 else "z"

        @block.gpsimd
        def _(pool):
            with pool.Fori(0, PAIRS) as pair:
                for k in range(NQ):
                    if k % HQ == 0:
                        pool.wait_ge(idx_ready[k // HQ].sem, idx_ready[k // HQ].at(pair, 1))
                        pool.sem_inc(passed_pool, 1)
                    pool.wait_ge(up_mm.sem, up_mm.at(pair, k - SLOTS + 1))
                    pool.sem_inc(passed_pool, 1)
                    for r in range(QK):
                        col = (k % HQ) * QK + r
                        pool.indirect_dma_start(
                            ring[:, k % SLOTS, r, :], None, rows,
                            bass.IndirectOffsetOnAxis(ap=idx[:, k // HQ, col:col + 1], axis=0),
                        ).then_inc(gathered[k % SLOTS].sem, 16)

        @block.sync
        def _(sp):
            def load(pair):
                sp.wait_ge(xT_mm.sem, xT_mm.at(pair, 0))
                sp.dma_start(pT[:, :, :].rearrange("p c t -> p (c t)"),
                             patches[bass.ds(pair, 1), :, :].rearrange("a p n -> p (a n)")
                             ).then_inc(patches_in.sem, 16)
                sp.wait_ge(h1_sb.sem, h1_sb.at(pair, 0))
                sp.dma_start(h0[NTOK:S, :, :],
                             txt[bass.ds(pair * 2, 2), :, :].rearrange("j s d -> s j d")
                             ).then_inc(txt_in.sem, 16)

            def store(pair):
                for j in range(2):
                    sp.wait_ge(y_sb.sem, y_sb.at(pair, j + 1))
                    sp.dma_start(out[bass.ds(pair * 2 + j, 1), :, :].rearrange("a s d -> s (a d)"),
                                 y[:, j, :]).then_inc(stored[j].sem, 16)

            sp.sem_inc(stored[0].sem, 16)
            sp.sem_inc(stored[1].sem, 16)
            sp.dma_start(packed["tok"][:, :], packs["tok"]).then_inc(loaded["tok"].sem, 16)
            load(0)
            sp.dma_start(packed["at0"][:, :], packs["at0"]).then_inc(loaded["at0"].sem, 16)
            sp.dma_start(packed["moe"][:, :], packs["moe"]).then_inc(loaded["moe"].sem, 16)
            sp.dma_start(packed["at1"][:, :], packs["at1"]).then_inc(loaded["at1"].sem, 16)
            sp.dma_start(packed["pk"][:, :], packs["pk"]).then_inc(loaded["pk"].sem, 16)
            load(1)
            load(2)
            with sp.Fori(3, PAIRS) as pair:
                load(pair)
                store(pair - 3)
            for pair in range(PAIRS - 3, PAIRS):
                store(pair)
            for j in range(2):
                sp.wait_ge(stored[j].sem, stored[j].at(PAIRS - 1, 16))

        @block.tensor
        def _(pe):
            def mm(out_, lhsT, rhs, start=True, stop=True):
                return pe.matmul(out_, lhsT, rhs, start=start, stop=stop)

            def transposes(src, b, rows_=S):
                for j in range(2):
                    last = pe.transpose(ps[0:src.shape[2], b, j * rows_:(j + 1) * rows_], src[:, j, :],
                                        ident[0:rows_, 0:rows_])
                return last

            def a_x(pair):
                if isinstance(pair, int):
                    pe.wait_ge(loaded["tok"].sem, 16)
                pe.wait_ge(patches_in.sem, patches_in.at(pair, 16))
                pe.wait_ge(h1_sb.sem, h1_sb.at(pair, 0))
                for c in range(KCH):
                    last = mm(bank(4, 128, 2 * NTOK), W("tok", "w_patch")[:, c * D:(c + 1) * D],
                              pT[:, c, :], c == 0, c == KCH - 1)
                last.then_inc(xT_mm.sem, 1)

            def a_cs(pair):
                pe.wait_ge(xT_sb.sem, xT_sb.at(pair, 1))
                for j in range(2):
                    last = mm(ps[0:NTOK, 4, j * 12:(j + 1) * 12], xT[:, j, :], W("tok", "w_cs"))
                last.then_inc(cs_mm.sem, 1)

            def a_ck(pair):
                pe.wait_ge(ck_sb.sem, ck_sb.at(pair, 1))
                pe.sem_inc(passed_pe, 1)
                transposes(ck, 4, NTOK).then_inc(ckT_mm.sem, 1)

            def a_enh(pair):
                pe.wait_ge(ckT_sb.sem, ckT_sb.at(pair, 1))
                for j in range(2):
                    o_ = ps[0:NTOK, 4, j * D:(j + 1) * D]
                    mm(o_, xT[:, j, :], ident, True, False)
                    last = mm(o_, ckT[:, j, :], W("tok", "w_emb"), False, True)
                last.then_inc(xenh_mm.sem, 1)

            def a_xnT(pair):
                pe.wait_ge(xn_sb.sem, xn_sb.at(pair, 1))
                pe.sem_inc(passed_pe, 1)
                transposes(xn, 4, NTOK).then_inc(xnT_mm.sem, 1)

            def a_h0(pair):
                pe.wait_ge(xnT_sb.sem, xnT_sb.at(pair, 1))
                for j in range(2):
                    o_ = ps[0:NTOK, 4, j * D:(j + 1) * D]
                    mm(o_, xnT[:, j, :], W("tok", "w_out"), True, False)
                    last = mm(o_, W("tok", "ones")[:, 0:NTOK], W("tok", "b_out"), False, True)
                last.then_inc(h0_mm.sem, 1)

            def a_hnT(pair):
                pe.wait_ge(hnA_sb.sem, hnA_sb.at(pair, 1))
                transposes(hnA, 4).then_inc(hnTA_mm.sem, 1)

            def a_down(pair):
                if isinstance(pair, int):
                    pe.wait_ge(loaded["at0"].sem, 16)
                pe.wait_ge(hnTA_sb.sem, hnTA_sb.at(pair, 1))
                for j in range(2):
                    last = mm(ps[0:S, 4, j * 149:(j + 1) * 149], hnTA[:, j, :], W("at0", "w_down"))
                last.then_inc(down_mm.sem, 1)

            def a_cT(pair):
                pe.wait_ge(cn_sb.sem, cn_sb.at(pair, 1))
                pe.sem_inc(passed_pe, 1)
                for j in range(2):
                    pe.transpose(ps[0:RQ, 4, j * S:(j + 1) * S], cn[:, j, 0:RQ], ident[0:S, 0:S])
                    last = pe.transpose(ps[0:RKV, 4, (2 + j) * S:(3 + j) * S], cn[:, j, RQ:RQ + RKV],
                                        ident[0:S, 0:S])
                last.then_inc(cT_mm.sem, 1)

            def a_q(pair):
                pe.wait_ge(cT_sb.sem, cT_sb.at(pair, 1))
                for g in range(2):
                    last = mm(ps[:, 4, g * 2 * S:(g + 1) * 2 * S], W("at0", "w_q")[:, g * 128:(g + 1) * 128],
                              cqT[:, :, :])
                last.then_inc(qkv_mm[0].sem, 1)

            def a_k(pair):
                pe.wait_ge(qk_sb[0].sem, qk_sb[0].at(pair, 1))
                for g in range(2):
                    o_ = ps[:, 4, g * 2 * S:(g + 1) * 2 * S]
                    mm(o_, W("at0", "w_k")[:, g * 128:(g + 1) * 128], ckvT[:, :, :], True, False)
                    last = mm(o_, W("at0", "w_kr")[:, g * 128:(g + 1) * 128], hnTA[:, :, :], False, True)
                last.then_inc(qkv_mm[0].sem, 1)

            def a_v(pair):
                pe.wait_ge(qk_sb[0].sem, qk_sb[0].at(pair, 2))
                for j in range(2):
                    last = mm(ps[0:S, 4, j * D:(j + 1) * D], ckvT[:, j, :], W("at0", "w_v"))
                last.then_inc(qkv_mm[0].sem, 1)

            def head_scores(n, part):
                for c in (2 * part, 2 * part + 1):
                    j, g = SLOT_OF[c]
                    for b in range(4):
                        r = HROWS * b
                        last = mm(ps[0:S, b, c * S:(c + 1) * S], qT[r:r + HROWS, g, j, :],
                                  kT[r:r + HROWS, g, j, :], n == 1, n == 1 or c == 3)
                return last

            def a_scores_a(pair):
                pe.wait_ge(qk_sb[0].sem, qk_sb[0].at(pair, 2))
                if not isinstance(pair, int) or pair > 0:
                    pe.wait_ge(moe_sb.sem, moe_sb.at(pair - 1, STEPS))
                for b in range(4):
                    mm(ps[0:S, b, 0:HB * S].rearrange("p (h s) -> p h s", h=HB), ident16[:, :],
                       mask16[:, :].unsqueeze(1).broadcast_to([S, HB, S]), True, False)
                head_scores(0, 0)

            def b_scores_a(pair, with_a):
                pe.wait_ge(qk_sb[1].sem, qk_sb[1].at(pair, 2))
                if with_a:
                    pe.wait_ge(probT_sb[0].sem, probT_sb[0].at(pair + 1, 4))
                head_scores(1, 0)

            def scores_b(pair, n):
                head_scores(n, 1).then_inc(score_mm[n].sem, 1)

            def prob_transposes(pair, n, part):
                for b in (2 * part, 2 * part + 1):
                    pe.wait_ge(exp_sb[n].sem, exp_sb[n].at(pair, b + 1))
                    for h in range(HB):
                        last = pe.transpose(ps[0:S, b, h * S:(h + 1) * S], prob[:, b * HB + h, :],
                                            ident[0:S, 0:S])
                    last.then_inc(probT_mm[n].sem, 1)

            def weighted_values(pair, n, to, part):
                pe.wait_ge(v_sb[n].sem, v_sb[n].at(pair, 1))
                for b in (2 * part, 2 * part + 1):
                    pe.wait_ge(probT_sb[n].sem, probT_sb[n].at(pair, b + 1))
                    for c, (j, g) in enumerate(SLOT_OF):
                        h = j * HEADS + g * HB + b
                        last = mm(ps[0:S, to, h * (DH + 1):(h + 1) * (DH + 1)], probT[:, b * HB + c, :],
                                  vA[n][:, h, :])
                if part == 1:
                    last.then_inc(pv_mm[n].sem, 1)

            def output_transposes(pair, n, to):
                pe.wait_ge(o_sb[n].sem, o_sb[n].at(pair, 1))
                transposes(o[n][:, :, :].rearrange("p (j h) d -> p j (h d)", j=2), to).then_inc(oT_mm[n].sem, 1)

            def output_projection(pair, n, to):
                pe.wait_ge(oT_sb[n].sem, oT_sb[n].at(pair, 1))
                for j in range(2):
                    o_ = ps[0:S, to, j * D:(j + 1) * D]
                    last = mm(o_, oT[n][:, j, :], W(f"at{n}", "w_o"), True, n == 0)
                    if n == 1:
                        last = mm(o_, W("tok", "ones")[:, 0:S], W("at1", "b_o"), False, True)
                last.then_inc(out_mm[n].sem, 1)

            def b_hnT(pair, n, to):
                pe.wait_ge(hnB_sb.sem, hnB_sb.at(pair, n))
                transposes(hnB if n < 3 else qnext, to).then_inc(hnTB_mm.sem, 1)

            def b_logits(pair):
                if isinstance(pair, int):
                    pe.wait_ge(loaded["moe"].sem, 16)
                pe.wait_ge(hnTB_sb.sem, hnTB_sb.at(pair, 1))
                for j in range(2):
                    last = mm(ps[0:S, 5, j * E0:(j + 1) * E0], hnTB[:, j, :], W("moe", "sel"))
                last.then_inc(logit_mm.sem, 1)

            def moe(n):
                def step(pair):
                    if n < STEPS:
                        if n == 1:
                            pe.wait_ge(el_sb.sem, el_sb.at(pair, 1))
                        if n >= 2:
                            pe.wait_ge(hid_sb.sem, hid_sb.at(pair, n - 1))
                        for q in range(EG):
                            e = n * EG + q
                            last = mm(ps[:, HID_BANKS[n % 2], q * 2 * S:(q + 1) * 2 * S],
                                      W("moe", "keys")[:, e * H0:(e + 1) * H0], hnTB[:, :, :])
                        last.then_inc(hid_mm.sem, 1)
                    m = n - 1
                    if m >= 0:
                        pe.wait_ge(hid_sb.sem, hid_sb.at(pair, m + 1))
                        if m >= 2:
                            pe.wait_ge(moe_sb.sem, moe_sb.at(pair, m - 1))
                        for q in range(EG):
                            e = m * EG + q
                            for j in range(2):
                                c = (2 * q + j) * D
                                last = mm(ps[0:S, m % 2, c:c + D], hidT[:, m % 2, q, j, :],
                                          W("moe", "values")[:, e * D:(e + 1) * D])
                        last.then_inc(moe_mm.sem, 1)
                return step

            def b_q(pair):
                if isinstance(pair, int):
                    pe.wait_ge(loaded["at1"].sem, 16)
                pe.wait_ge(hnTB_sb.sem, hnTB_sb.at(pair, 2))
                for g in range(2):
                    last = mm(ps[:, 5, g * 2 * S:(g + 1) * 2 * S], W("at1", "w_q")[:, g * 128:(g + 1) * 128],
                              hnTB[:, :, :])
                last.then_inc(qkv_mm[1].sem, 1)

            def b_k(pair):
                pe.wait_ge(qk_sb[1].sem, qk_sb[1].at(pair, 1))
                for g in range(2):
                    last = mm(ps[:, 5, g * 2 * S:(g + 1) * 2 * S], W("at1", "w_k")[:, g * 128:(g + 1) * 128],
                              hnTB[:, :, :])
                last.then_inc(qkv_mm[1].sem, 1)

            def b_v(pair):
                pe.wait_ge(qk_sb[1].sem, qk_sb[1].at(pair, 2))
                for j in range(2):
                    last = mm(ps[0:S, 5, j * D:(j + 1) * D], hnTB[:, j, :], W("at1", "w_v"))
                last.then_inc(qkv_mm[1].sem, 1)

            def b_qh(pair, part):
                if isinstance(pair, int):
                    pe.wait_ge(loaded["pk"].sem, 16)
                pe.wait_ge(hnTB_sb.sem, hnTB_sb.at(pair, 3))
                for m in (2 * part, 2 * part + 1):
                    if m == 3:
                        pe.wait_ge(qh_sb.sem, qh_sb.at(pair, 1))
                    for h in (2 * m, 2 * m + 1):
                        last = mm(ps[:, QH_BANKS[m], (h % 2) * 2 * S:(h % 2 + 1) * 2 * S],
                                  W("pk", "w_q")[:, h * 128:(h + 1) * 128], hnTB[:, :, :])
                    last.then_inc(qh_mm.sem, 1)

            def b_keys(j):
                def keys(pair):
                    for m in range(2):
                        if j == 0:
                            pe.wait_ge(qh_sb.sem, qh_sb.at(pair, 2 * m + 2))
                        else:
                            pe.wait_ge(sub_read.sem, sub_read.at(pair, m + 1))
                        for q in range(4):
                            h = 4 * m + q
                            for c in range(2):
                                last = mm(ps[0:S, 2 * m + c, q * NE:(q + 1) * NE],
                                          qhT[c * HALF:(c + 1) * HALF, h, j, :],
                                          W("pk", "keys")[c * HALF:(c + 1) * HALF, h * NE:(h + 1) * NE])
                        last.then_inc(sub_mm.sem, 1)
                return keys

            def e_up(k, part):
                def up(pair):
                    j = k // HQ
                    pe.wait_ge(diag_sb.sem, diag_sb.at(pair, 2 * k + part + 1))
                    if k % HQ == 0 and part == 0:
                        pe.wait_ge(y_sb.sem, y_sb.at(pair, j - 1))
                    for r in range(part * HK, (part + 1) * HK):
                        last = mm(ps[0:S, 7, j * D:(j + 1) * D], diag[:, k % 2, r, :],
                                  ring[0:S, k % SLOTS, r, D:2 * D],
                                  k % HQ == 0 and r == 0, k % HQ == HQ - 1 and r == QK - 1)
                    if part == 1:
                        last.then_inc(up_mm.sem, 1)
                return up

            def pieces(with_a):
                return {
                    "a_x": a_x, "a_cs": a_cs, "a_ck": a_ck, "a_enh": a_enh, "a_xnT": a_xnT, "a_h0": a_h0,
                    "a_hnT": a_hnT, "a_down": a_down, "a_cT": a_cT, "a_q": a_q, "a_k": a_k, "a_v": a_v,
                    "a_scoresa": a_scores_a, "a_scoresb": lambda p: scores_b(p, 0),
                    "a_pTa": lambda p: prob_transposes(p, 0, 0), "a_pTb": lambda p: prob_transposes(p, 0, 1),
                    "a_pva": lambda p: weighted_values(p, 0, 4, 0), "a_pvb": lambda p: weighted_values(p, 0, 4, 1),
                    "a_oT": lambda p: output_transposes(p, 0, 4), "a_out": lambda p: output_projection(p, 0, 4),
                    "b_hnT1": lambda p: b_hnT(p, 1, 5), "b_hnT2": lambda p: b_hnT(p, 2, 5),
                    "b_hnT3": lambda p: b_hnT(p, 3, 5), "b_logits": b_logits,
                    "b_q": b_q, "b_k": b_k, "b_v": b_v,
                    "b_scoresa": lambda p: b_scores_a(p, with_a), "b_scoresb": lambda p: scores_b(p, 1),
                    "b_pTa": lambda p: prob_transposes(p, 1, 0), "b_pTb": lambda p: prob_transposes(p, 1, 1),
                    "b_pva": lambda p: weighted_values(p, 1, 5, 0), "b_pvb": lambda p: weighted_values(p, 1, 5, 1),
                    "b_oT": lambda p: output_transposes(p, 1, 5), "b_out": lambda p: output_projection(p, 1, 5),
                    "b_qha": lambda p: b_qh(p, 0), "b_qhb": lambda p: b_qh(p, 1),
                    "b_keys0a": b_keys(0), "b_keys1a": b_keys(1),
                    **{f"m{n}": moe(n) for n in range(STEPS + 1)},
                    **{f"{ez_of(k)}_up{k}{x}": e_up(k, part) for k in range(NQ) for part, x in enumerate("ab")},
                }

            pe.sem_inc(up_mm.sem, NQ)
            pe.wait_ge(consts.sem, N_CONSTS)
            run(SCHEDULE["pe"], pieces(True), a=0)
            run(START["pe"], pieces(True), b=0, a=1)
            run(SCHEDULE["pe"], pieces(True), e=0, b=1, a=2)
            with pe.Fori(1, PAIRS - 2) as pair:
                run(SCHEDULE["pe"], pieces(True), z=pair - 1, e=pair, b=pair + 1, a=pair + 2)
            run(SCHEDULE["pe"], pieces(False), z=PAIRS - 3, e=PAIRS - 2, b=PAIRS - 1)
            run(SCHEDULE["pe"], pieces(False), z=PAIRS - 2, e=PAIRS - 1)
            run(SCHEDULE["pe"], pieces(False), z=PAIRS - 1)

        @block.scalar
        def _(act):
            def copy(out_, in_, scale=1.0):
                return act.activation(out_, in_, ACT.Copy, scale=scale)

            def flat(t):
                return t.rearrange("p j s -> p (j s)")

            def a_ck(pair):
                act.wait_ge(ckT_mm.sem, ckT_mm.at(pair, 1))
                copy(flat(ckT[:, :, :]), bank(4, DC + 1, 2 * NTOK)).then_inc(ckT_sb.sem, 1)

            def a_xnT(pair):
                act.wait_ge(xnT_mm.sem, xnT_mm.at(pair, 1))
                act.activation(flat(xnT[:, :, :]), bank(4, 128, 2 * NTOK), ACT.Identity,
                               scale=W("tok", "ln_g"), bias=W("tok", "ln_b")).then_inc(xnT_sb.sem, 1)

            def a_hnT(pair):
                act.wait_ge(hnTA_mm.sem, hnTA_mm.at(pair, 1))
                copy(flat(hnTA[:, :, :]), bank(4, 128, 2 * S)).then_inc(hnTA_sb.sem, 1)

            def a_cT(pair):
                act.wait_ge(cT_mm.sem, cT_mm.at(pair, 1))
                act.activation(flat(cqT[:, :, :]), ps[0:RQ, 4, 0:2 * S], ACT.Identity,
                               scale=W("at0", "q_g"), bias=W("at0", "q_b"))
                act.activation(flat(ckvT[:, :, :]), ps[0:RKV, 4, 2 * S:4 * S], ACT.Identity,
                               scale=W("at0", "kv_g"), bias=W("at0", "kv_b")).then_inc(cT_sb.sem, 1)

            def values(pair, n, from_):
                act.wait_ge(qkv_mm[n].sem, qkv_mm[n].at(pair, 3))
                copy(vA[n][:, :, 0:DH], bank(from_, S, 2 * D).rearrange("p (h d) -> p h d", d=DH)
                     ).then_inc(v_sb[n].sem, 1)

            def exps(pair, n, part):
                act.wait_ge(nmx_sb[n].sem, nmx_sb[n].at(pair, part + 1))
                for g in range(part * HEADS, (part + 1) * HEADS):
                    last = act.activation(prob[:, g, :], ps[0:S, g // HB, (g % HB) * S:(g % HB + 1) * S],
                                          ACT.Exp, bias=nmx[n][:, g:g + 1])
                    if g % HB == HB - 1:
                        last.then_inc(exp_sb[n].sem, 1)

            def prob_transposes(pair, n, part, with_a=False):
                if with_a:
                    act.wait_ge(pv_mm[0].sem, pv_mm[0].at(pair + 1, 1))
                if n == 0 and (not isinstance(pair, int) or pair >= 2):
                    act.wait_ge(rows_sb.sem, rows_sb.at(pair - 2, 1))
                for b in (2 * part, 2 * part + 1):
                    act.wait_ge(probT_mm[n].sem, probT_mm[n].at(pair, b + 1))
                    copy(flat(probT[:, b * HB:(b + 1) * HB, :]), bank(b, S, HB * S)).then_inc(probT_sb[n].sem, 1)

            def output_transposes(pair, n, from_):
                act.wait_ge(oT_mm[n].sem, oT_mm[n].at(pair, 1))
                copy(flat(oT[n][:, :, :]), bank(from_, 128, 2 * S)).then_inc(oT_sb[n].sem, 1)

            def b_hnT(pair, n, from_):
                act.wait_ge(hnTB_mm.sem, hnTB_mm.at(pair, n))
                copy(flat(hnTB[:, :, :]), bank(from_, 128, 2 * S)).then_inc(hnTB_sb.sem, 1)

            def b_logits(pair):
                act.wait_ge(logit_mm.sem, logit_mm.at(pair, 1))
                act.activation(flat(el[:, :, :]), bank(5, S, 2 * E0), ACT.Exp, scale=-1.0).then_inc(el_sb.sem, 1)

            def moe(n):
                def step(pair):
                    act.wait_ge(hid_mm.sem, hid_mm.at(pair, n + 1))
                    if n >= 2:
                        act.wait_ge(moe_mm.sem, moe_mm.at(pair, n - 1))
                    act.activation(hidT[:, n % 2, :, :, :].rearrange("p e j s -> p (e j s)"),
                                   bank(HID_BANKS[n % 2], 128, EG * 2 * S), ACT.Relu).then_inc(hid_sb.sem, 1)
                return step

            def b_q(pair, with_a):
                act.wait_ge(qkv_mm[1].sem, qkv_mm[1].at(pair, 1))
                if with_a:
                    act.wait_ge(score_mm[0].sem, score_mm[0].at(pair + 1, 1))
                copy(qT[:, :, :, :].rearrange("p g j s -> p (g j s)"), bank(5, 128, 4 * S),
                     1.0 / math.sqrt(DH)).then_inc(qk_sb[1].sem, 1)

            def b_k(pair):
                act.wait_ge(qkv_mm[1].sem, qkv_mm[1].at(pair, 2))
                copy(kT[:, :, :, :].rearrange("p g j s -> p (g j s)"), bank(5, 128, 4 * S)
                     ).then_inc(qk_sb[1].sem, 1)

            def b_qh(pair, part):
                if isinstance(pair, int):
                    act.wait_ge(loaded["pk"].sem, 16)
                for m in (2 * part, 2 * part + 1):
                    act.wait_ge(qh_mm.sem, qh_mm.at(pair, m + 1))
                    for h in (2 * m, 2 * m + 1):
                        last = act.activation(flat(qhT[:, h, :, :]),
                                              ps[:, QH_BANKS[m], (h % 2) * 2 * S:(h % 2 + 1) * 2 * S], ACT.Identity,
                                              bias=W("pk", "b_q")[:, h:h + 1])
                    last.then_inc(qh_sb.sem, 1)

            def key_exps(pair, j):
                act.wait_ge(dif_sb.sem, dif_sb.at(pair, j + 1))
                part = flat(ez[:, j * PH:(j + 1) * PH, :])
                act.activation(part, part, ACT.Exp).then_inc(ez_sb.sem, 1)

            def e_dots(k):
                def tanh(pair):
                    act.wait_ge(gu_sb.sem, gu_sb.at(pair, k + 1))
                    act.activation(gt[:, k % 2, :], gu[:, k % 2, :], ACT.Tanh).then_inc(gt_sb.sem, 1)
                return tanh

            def e_values(k, part):
                def diagonals(pair):
                    act.wait_ge(val_sb.sem, val_sb.at(pair, k + 1))
                    act.wait_ge(up_mm.sem, up_mm.at(pair, k - 1))
                    for r in range(part * HK, (part + 1) * HK):
                        last = act.activation(diag[:, k % 2, r, :], ident[0:S, 0:S], ACT.Copy,
                                              scale=val[:, k % 2, r:r + 1])
                    last.then_inc(diag_sb.sem, 1)
                return diagonals

            def pieces(with_a):
                return {
                    "a_ck": a_ck, "a_xnT": a_xnT, "a_hnT": a_hnT, "a_cT": a_cT, "a_v": lambda p: values(p, 0, 4),
                    "a_expsa": lambda p: exps(p, 0, 0), "a_expsb": lambda p: exps(p, 0, 1),
                    "a_pTa": lambda p: prob_transposes(p, 0, 0), "a_pTb": lambda p: prob_transposes(p, 0, 1),
                    "a_oT": lambda p: output_transposes(p, 0, 4),
                    "b_hnT1": lambda p: b_hnT(p, 1, 5), "b_hnT2": lambda p: b_hnT(p, 2, 5),
                    "b_hnT3": lambda p: b_hnT(p, 3, 5), "b_logits": b_logits,
                    "b_q": lambda p: b_q(p, with_a), "b_k": b_k, "b_v": lambda p: values(p, 1, 5),
                    "b_expsa": lambda p: exps(p, 1, 0), "b_expsb": lambda p: exps(p, 1, 1),
                    "b_pTa": lambda p: prob_transposes(p, 1, 0, with_a),
                    "b_pTb": lambda p: prob_transposes(p, 1, 1, with_a),
                    "b_oT": lambda p: output_transposes(p, 1, 5),
                    "b_qha": lambda p: b_qh(p, 0), "b_qhb": lambda p: b_qh(p, 1), "b_softmax": lambda p: key_exps(p, 0),
                    "x_softmax": lambda p: key_exps(p, 1),
                    **{f"m{n}": moe(n) for n in range(STEPS)},
                    **{f"{ez_of(k)}_dots{k}b": e_dots(k) for k in range(NQ)},
                    **{f"{ez_of(k)}_values{k}{x}": e_values(k, part)
                       for k in range(NQ) for part, x in enumerate("ab")},
                }

            act.wait_ge(loaded["tok"].sem, 16)
            act.wait_ge(loaded["at0"].sem, 16)
            copy(ident16[:, :], ident[0:S, 0:S]).then_inc(consts.sem, 1)
            copy(mask16[:, :], W("at0", "mask")).then_inc(consts.sem, 1)
            run(SCHEDULE["act"], pieces(True), a=0)
            run(START["act"], pieces(True), b=0, a=1)
            run(SCHEDULE["act"], pieces(True), e=0, b=1, a=2)
            with act.Fori(1, PAIRS - 2) as pair:
                run(SCHEDULE["act"], pieces(True), z=pair - 1, e=pair, b=pair + 1, a=pair + 2)
            run(SCHEDULE["act"], pieces(False), z=PAIRS - 3, e=PAIRS - 2, b=PAIRS - 1)
            run(SCHEDULE["act"], pieces(False), z=PAIRS - 2, e=PAIRS - 1)
            run(SCHEDULE["act"], pieces(False), z=PAIRS - 1)

        @block.vector
        def _(dve):
            def norm(c, t, srcs, dsts, done):
                np_, n_ = srcs[0].shape[0], len(srcs)
                for n, src in enumerate(srcs):
                    dve.bn_stats(stats[t][0:np_, n, :], src).then_inc(c.sem, 1)
                dve.wait_ge(c.sem, c.after(n_))
                dve.sem_inc(passed_dve, 1)
                for n in range(n_):
                    dve.bn_aggr(mv[t][0:np_, n, :], stats[t][0:np_, n, :]).then_inc(c.sem, 1)
                dve.wait_ge(c.sem, c.after(n_))
                v, y_, a, b = (rs[t][0:np_, 0:n_, q] for q in range(4))
                dve.tensor_scalar(v, mv[t][0:np_, 0:n_, 1], EPS, None, ALU.add).then_inc(c.sem, 1)
                dve.wait_ge(c.sem, c.after(1))
                dve.tensor_scalar(y_.bitcast(I32), v.bitcast(I32), -0.5, RSQRT_MAGIC, ALU.mult, ALU.add
                                  ).then_inc(c.sem, 1)
                for c1, c2 in RSQRT_STEPS:
                    dve.wait_ge(c.sem, c.after(1))
                    dve.scalar_tensor_tensor(a, y_, -c1, y_, ALU.mult, ALU.mult).then_inc(c.sem, 1)
                    dve.wait_ge(c.sem, c.after(1))
                    dve.tensor_tensor(b, a, v, ALU.mult).then_inc(c.sem, 1)
                    dve.wait_ge(c.sem, c.after(1))
                    dve.scalar_tensor_tensor(y_, b, c2, y_, ALU.add, ALU.mult).then_inc(c.sem, 1)
                dve.wait_ge(c.sem, c.after(1))
                for n, (src, dst) in enumerate(zip(srcs, dsts)):
                    last = dve.tensor_scalar(dst, src, mv[t][0:np_, n, 0:1], rs[t][0:np_, n, 1:2],
                                             ALU.subtract, ALU.mult)
                last.then_inc(done.sem, 1)

            def norm_pair(c, t, h, dst, done):
                norm(c, t, [h[:, j, :] for j in range(2)], [dst[:, j, :] for j in range(2)], done)

            def a_x(c, pair):
                dve.wait_ge(xT_mm.sem, xT_mm.at(pair, 1))
                dve.tensor_tensor(xT[:, :, :], bank(4, 128, 2 * NTOK).rearrange("p (j t) -> p j t", j=2),
                                  posb[:, :].unsqueeze(1).broadcast_to([128, 2, NTOK]), ALU.add
                                  ).then_inc(xT_sb.sem, 1)

            def a_cs(c, pair):
                dve.wait_ge(cs_mm.sem, cs_mm.at(pair, 1))
                dve.tensor_tensor(cs[:, :, :], bank(4, NTOK, 24).rearrange("p (j t) -> p j t", j=2),
                                  W("tok", "b_cs").unsqueeze(1).broadcast_to([NTOK, 2, 12]), ALU.add
                                  ).then_inc(c.sem, 1)
                dve.wait_ge(c.sem, c.after(1))
                dve.tensor_tensor(sq[:, :, :], cs[:, :, DC:], cs[:, :, DC:], ALU.mult).then_inc(c.sem, 1)
                dve.wait_ge(c.sem, c.after(1))
                dve.tensor_reduce(ck[:, :, DC:DC + 1], sq[:, :, :], AXX, ALU.add).then_inc(c.sem, 1)
                dve.wait_ge(c.sem, c.after(1))
                dve.tensor_tensor(ck[:, :, 0:DC], cs[:, :, 0:DC], ck[:, :, DC:DC + 1].broadcast_to([NTOK, 2, DC]),
                                  ALU.mult).then_inc(ck_sb.sem, 1)

            def a_enh(c, pair):
                dve.wait_ge(xenh_mm.sem, xenh_mm.at(pair, 1))
                norm(c, 0, [ps[0:NTOK, 4, j * D:(j + 1) * D] for j in range(2)], [xn[:, j, :] for j in range(2)],
                     xn_sb)

            def a_h0(c, pair):
                dve.wait_ge(h0_mm.sem, h0_mm.at(pair, 1))
                dve.tensor_copy(h0[0:NTOK, :, :].rearrange("p j d -> p (j d)"), bank(4, NTOK, 2 * D)
                                ).then_inc(c.sem, 1)
                dve.wait_ge(c.sem, c.after(1))
                dve.wait_ge(txt_in.sem, txt_in.at(pair, 16))
                norm_pair(c, 0, h0, hnA, hnA_sb)

            def a_down(c, pair):
                dve.wait_ge(down_mm.sem, down_mm.at(pair, 1))
                parts = [(j, a, b) for j in range(2) for a, b in ((0, RQ), (RQ, RQ + RKV))]
                norm(c, 0, [ps[0:S, 4, j * 149 + a:j * 149 + b] for j, a, b in parts],
                     [cn[:, j, a:b] for j, a, b in parts], cn_sb)

            def rope(pair, n, t, table, with_b):
                dve.wait_ge(qkv_mm[0].sem, qkv_mm[0].at(pair, n))
                if with_b:
                    dve.wait_ge(score_mm[1].sem, score_mm[1].at(pair - 2, 1))
                dve.tensor_tensor(t[:, :, :, :].rearrange("p g j s -> p (g j) s"),
                                  bank(4, 128, 4 * S).rearrange("p (a s) -> p a s", s=S),
                                  W("at0", table).unsqueeze(1).broadcast_to([128, 4, S]), ALU.mult
                                  ).then_inc(qk_sb[0].sem, 1)

            def maxima(pair, n):
                dve.wait_ge(score_mm[n].sem, score_mm[n].at(pair, 1))
                for q in range(2):
                    dve.tensor_reduce(nmx[n][:, q * HEADS:(q + 1) * HEADS],
                                      ps[0:S, 2 * q:2 * q + 2, 0:HB * S].rearrange("p b (h s) -> p b h s", s=S),
                                      AXX, ALU.max, negate=True).then_inc(nmx_sb[n].sem, 1)

            def normalized(c, pair, n, from_):
                dve.wait_ge(pv_mm[n].sem, pv_mm[n].at(pair, 1))
                pv = bank(from_, S, 2 * HEADS * (DH + 1)).rearrange("p (h d) -> p h d", d=DH + 1)
                dve.reciprocal(rden[n][:, :, :], pv[:, :, DH:DH + 1]).then_inc(c.sem, 1)
                dve.wait_ge(c.sem, c.after(1))
                dve.tensor_tensor(o[n][:, :, :], pv[:, :, 0:DH], rden[n][:, :, :].broadcast_to([S, 2 * HEADS, DH]),
                                  ALU.mult).then_inc(o_sb[n].sem, 1)

            def flat(t):
                return t.rearrange("p j d -> p (j d)")

            def a_out(c, pair):
                dve.wait_ge(out_mm[0].sem, out_mm[0].at(pair, 1))
                dve.tensor_tensor(flat(h1[:, :, :]), flat(h0[:, :, :]), bank(4, S, 2 * D), ALU.add
                                  ).then_inc(h1_sb.sem, 1)

            def b_norm1(c, pair):
                dve.wait_ge(h1_sb.sem, h1_sb.at(pair, 1))
                norm_pair(c, 1, h1, hnB, hnB_sb)

            def b_router(c, pair):
                dve.wait_ge(el_sb.sem, el_sb.at(pair, 1))
                dve.tensor_scalar(el[:, :, :], el[:, :, :], 1.0, None, ALU.add).then_inc(c.sem, 1)
                dve.wait_ge(c.sem, c.after(1))
                dve.reciprocal(sel[:, :, :], el[:, :, :]).then_inc(c.sem, 1)
                dve.wait_ge(c.sem, c.after(1))
                dve.sem_inc(passed_dve, 1)
                for j in range(2):
                    dve.max(selmax[:, j, :], sel[:, j, :]).then_inc(c.sem, 1)
                dve.wait_ge(c.sem, c.after(2))
                dve.sem_inc(passed_dve, 1)
                for j in range(2):
                    dve.max_index(selidx[:, j, :], selmax[:, j, :], sel[:, j, :]).then_inc(c.sem, 1)
                dve.wait_ge(c.sem, c.after(2))
                dve.tensor_copy(selidf[:, :, :], selidx[:, :, :]).then_inc(c.sem, 1)
                dve.wait_ge(c.sem, c.after(1))
                for j in range(2):
                    for t in range(2):
                        dve.tensor_scalar(wm[:, t, j, :], W("moe", "iota"), selidf[:, j, t:t + 1],
                                          selmax[:, j, t:t + 1], ALU.is_equal, ALU.mult).then_inc(c.sem, 1)
                dve.wait_ge(c.sem, c.after(4))
                dve.tensor_tensor(wmoe[:, :, :], wm[:, 0, :, :], wm[:, 1, :, :], ALU.add).then_inc(c.sem, 1)
                dve.wait_ge(c.sem, c.after(1))

            def moe(n):
                def step(c, pair):
                    m = n - 1
                    dve.wait_ge(moe_mm.sem, moe_mm.at(pair, m + 1))
                    for q in range(EG):
                        e = m * EG + q
                        for j in range(2):
                            if e > 0:
                                dve.wait_ge(c.sem, c.before(1))
                            col = (2 * q + j) * D
                            dve.scalar_tensor_tensor(h1[:, j, :], ps[0:S, m % 2, col:col + D],
                                                     wmoe[:, j, e:e + 1], h1[:, j, :],
                                                     ALU.mult, ALU.add).then_inc(c.sem, 1)
                            c.after(1)
                    dve.wait_ge(c.sem, c.after(0))
                    dve.sem_inc(moe_sb.sem, 1)
                return step

            def b_norm2(c, pair):
                norm_pair(c, 1, h1, hnB, hnB_sb)

            def b_out(c, pair):
                dve.wait_ge(out_mm[1].sem, out_mm[1].at(pair, 1))
                dve.tensor_tensor(flat(h2[:, :, :]), flat(h1[:, :, :]), bank(5, S, 2 * D), ALU.add
                                  ).then_inc(c.sem, 1)
                dve.wait_ge(c.sem, c.after(1))
                norm_pair(c, 1, h2, qnext, hnB_sb)

            def keys(m):
                return [(4 * m + q, half, ps[0:S, 2 * m + half, q * NE:(q + 1) * NE])
                        for half in range(2) for q in range(4)]

            def b_keys(j):
                def top(c, pair):
                    for m in range(2):
                        dve.wait_ge(sub_mm.sem, sub_mm.at(pair, j * 2 + m + 1))
                        dve.sem_inc(passed_dve, 1)
                        for h, half, scores in keys(m):
                            dve.max(s8[:, j, h, half, :], scores).then_inc(c.sem, 1)
                        c.after(8)
                return top

            def b_places(j):
                def places(c, pair):
                    dve.wait_ge(c.sem, c.after(0))
                    dve.sem_inc(passed_dve, 1)
                    for m in range(2):
                        for h, half, scores in keys(m):
                            last = dve.max_index(i8[:, j, h, half, :], s8[:, j, h, half, :], scores)
                        last.then_inc(sub_read.sem, 1)
                return places

            def b_best(j):
                def best_sums(c, pair):
                    grid = [S, PH, TOPK, TOPK]
                    dve.tensor_tensor(sums[:, :, :, :], s8[:, j, :, 0, :].unsqueeze(3).broadcast_to(grid),
                                      s8[:, j, :, 1, :].unsqueeze(2).broadcast_to(grid), ALU.add
                                      ).then_inc(c.sem, 1)
                    dve.wait_ge(c.sem, c.after(1))
                    dve.sem_inc(passed_dve, 1)
                    for h in range(PH):
                        dve.max(best[:, j * PH + h, :], sums[:, h, :, :].rearrange("p a b -> p (a b)")
                                ).then_inc(c.sem, 1)
                    dve.wait_ge(c.sem, c.after(PH))
                    dve.sem_inc(passed_dve, 1)
                    for h in range(PH):
                        dve.max_index(bpos[:, j * PH + h, :], best[:, j * PH + h, :],
                                      sums[:, h, :, :].rearrange("p a b -> p (a b)")).then_inc(c.sem, 1)
                    dve.wait_ge(c.sem, c.after(PH))
                return best_sums

            def b_rows(j):
                def best_rows(c, pair):
                    hs = slice(j * PH, (j + 1) * PH)
                    grid = [S, PH, TOPK, TOPK]
                    dve.tensor_scalar(place[0][:, hs, :], bpos[:, hs, :], 3, None, ALU.logical_shift_right
                                      ).then_inc(c.sem, 1)
                    dve.tensor_scalar(place[1][:, hs, :], bpos[:, hs, :], 7, None, ALU.bitwise_and
                                      ).then_inc(c.sem, 1)
                    dve.wait_ge(sub_read.sem, sub_read.at(pair, 2 * j + 2))
                    for t in range(2):
                        dve.wait_ge(c.sem, c.after(1))
                        dve.tensor_tensor(onehot[t], place[t][:, hs, :].unsqueeze(3).broadcast_to(grid),
                                          W("pk", "iota").unsqueeze(1).unsqueeze(1).broadcast_to(grid),
                                          ALU.is_equal).then_inc(c.sem, 1)
                    for t in range(2):
                        dve.wait_ge(c.sem, c.after(1))
                        dve.tensor_tensor(onehot[t], onehot[t], i8[:, j, :, t, :].unsqueeze(2).broadcast_to(grid),
                                          ALU.mult).then_inc(c.sem, 1)
                    for t in range(2):
                        dve.wait_ge(c.sem, c.after(1))
                        dve.tensor_reduce(picked[t][:, :, :], onehot[t], AXX, ALU.add).then_inc(c.sem, 1)
                    dve.wait_ge(c.sem, c.after(2))
                    dve.scalar_tensor_tensor(idxf[:, j, :], picked[0][:, :, :].rearrange("p h k -> p (h k)"),
                                             float(NE), picked[1][:, :, :].rearrange("p h k -> p (h k)"),
                                             ALU.mult, ALU.add).then_inc(c.sem, 1)
                    dve.wait_ge(c.sem, c.after(1))
                    if j == 1:
                        dve.sem_inc(rows_sb.sem, 1)
                return best_rows

            def softmax(c, pair, j, weights):
                hs = slice(j * PH, (j + 1) * PH)
                dve.tensor_tensor(ez[:, hs, :], best[:, hs, :], best[:, hs, 0:1].broadcast_to([S, PH, TOPK]),
                                  ALU.subtract).then_inc(dif_sb.sem, 1)
                dve.wait_ge(ez_sb.sem, ez_sb.at(pair, j + 1))
                if j == 1 and (not isinstance(pair, int) or pair > 0):
                    dve.wait_ge(val_sb.sem, val_sb.at(pair, 0))
                dve.tensor_reduce(esum[:, hs, :], ez[:, hs, :], AXX, ALU.add).then_inc(c.sem, 1)
                dve.wait_ge(c.sem, c.after(1))
                dve.reciprocal(esum[:, hs, :], esum[:, hs, :]).then_inc(c.sem, 1)
                dve.wait_ge(c.sem, c.after(1))
                dve.tensor_tensor(weights.rearrange("p (h k) -> p h k", k=TOPK), ez[:, hs, :],
                                  esum[:, hs, :].broadcast_to([S, PH, TOPK]), ALU.mult).then_inc(c.sem, 1)
                dve.wait_ge(c.sem, c.after(1))

            def indices(c, pair, j):
                if not isinstance(pair, int) or pair > 0:
                    dve.wait_ge(gathered[SLOTS - 1].sem, gathered[SLOTS - 1].at(pair - 1, (j + 1) * 16 * QK))
                dve.tensor_copy(idx[0:S, j, :], idxf[:, j, :]).then_inc(idx_ready[j].sem, 1)

            def e_take(c, pair):
                dve.wait_ge(y_sb.sem, y_sb.at(pair, 0))
                dve.tensor_copy(wcur[:, 0, :], wnext[:, :]).then_inc(c.sem, 1)
                dve.tensor_copy(qcur, qnext[:, :, :]).then_inc(c.sem, 1)
                dve.tensor_copy(hcur[:, :, :], h2[:, :, :]).then_inc(c.sem, 1)
                dve.wait_ge(c.sem, c.after(3))

            def e_dots(k, part):
                def dots(c, pair):
                    b = k % 2
                    dve.wait_ge(gathered[k % SLOTS].sem, gathered[k % SLOTS].at(pair, 16 * QK * (k // SLOTS + 1)))
                    for r in range(part * HK, (part + 1) * HK):
                        row = ring[0:S, k % SLOTS, r, 0:D]
                        dve.tensor_tensor_reduce(out=row, in0=row, in1=qcur[:, k // HQ, :], scale=1.0, scalar=0.0,
                                                 op0=ALU.mult, op1=ALU.add, accum_out=xd[:, b, r:r + 1]
                                                 ).then_inc(c.sem, 1)
                    c.after(HK)
                    if part == 0:
                        return
                    dve.wait_ge(c.sem, c.after(0))
                    dve.tensor_tensor(ga[:, b, :], xd[:, b, :], xd[:, b, :], ALU.mult).then_inc(c.sem, 1)
                    dve.wait_ge(c.sem, c.after(1))
                    dve.tensor_scalar(gb[:, b, :], ga[:, b, :], GELU_B, GELU_A, ALU.mult, ALU.add
                                      ).then_inc(c.sem, 1)
                    dve.wait_ge(c.sem, c.after(1))
                    dve.tensor_tensor(gu[:, b, :], gb[:, b, :], xd[:, b, :], ALU.mult).then_inc(gu_sb.sem, 1)
                return dots

            def e_values(k):
                def values(c, pair):
                    j, b, at = k // HQ, k % 2, (k % HQ) * QK
                    dve.wait_ge(gt_sb.sem, gt_sb.at(pair, k + 1))
                    dve.scalar_tensor_tensor(gv[:, b, :], gt[:, b, :], 1.0, xd[:, b, :], ALU.add, ALU.mult
                                             ).then_inc(c.sem, 1)
                    dve.wait_ge(c.sem, c.after(1))
                    dve.scalar_tensor_tensor(val[:, b, :], gv[:, b, :], 0.5, wcur[:, j, at:at + QK],
                                             ALU.mult, ALU.mult).then_inc(val_sb.sem, 1)
                return values

            def e_sum(j):
                def total(c, pair):
                    dve.wait_ge(up_mm.sem, up_mm.at(pair, (j + 1) * HQ))
                    dve.wait_ge(stored[j].sem, stored[j].at(pair, 0))
                    dve.tensor_tensor(y[:, j, :], hcur[:, j, :], ps[0:S, 7, j * D:(j + 1) * D], ALU.add
                                      ).then_inc(y_sb.sem, 1)
                return total

            def chains(order, z=None, e=None, b=None, a=None):
                chain = {k: Chain(s, p) for k, s, p in (("a", steps_a, a), ("b", steps_b, b), ("x", steps_x, e))
                         if p is not None}
                if e is not None:
                    chain["e"] = Chain(steps_e, e, end=E_MAIN)
                if z is not None:
                    chain["z"] = Chain(steps_e, z, start=E_MAIN)
                with_b = a is not None and e is not None
                table = {
                    "a_x": a_x, "a_cs": a_cs, "a_enh": a_enh, "a_h0": a_h0, "a_down": a_down,
                    "a_q": lambda c, p: rope(p, 1, qT, "rope_q", with_b),
                    "a_k": lambda c, p: rope(p, 2, kT, "rope_k", with_b),
                    "a_scoresb": lambda c, p: maxima(p, 0),
                    "a_pvb": lambda c, p: normalized(c, p, 0, 4), "a_out": a_out,
                    "b_norm1": b_norm1, "b_router": b_router, "b_norm2": b_norm2,
                    "b_scoresb": lambda c, p: maxima(p, 1), "b_pvb": lambda c, p: normalized(c, p, 1, 5),
                    "b_out": b_out,
                    "b_best0a": b_best(0), "b_best0b": b_rows(0), "b_idx0": lambda c, p: indices(c, p, 0),
                    "b_softmax": lambda c, p: softmax(c, p, 0, wnext[:, :]),
                    "x_best1a": b_best(1), "x_best1b": b_rows(1), "x_idx1": lambda c, p: indices(c, p, 1),
                    "x_softmax": lambda c, p: softmax(c, p, 1, wcur[:, 1, :]),
                    **{f"b_keys{j}a": b_keys(j) for j in range(2)}, **{f"b_keys{j}b": b_places(j) for j in range(2)},
                    "e_take": e_take, "e_sum0": e_sum(0), "z_sum1": e_sum(1),
                    **{f"m{n}": moe(n) for n in range(1, STEPS + 1)},
                    **{f"{ez_of(k)}_dots{k}{x}": e_dots(k, part)
                       for k in range(NQ) for part, x in enumerate("ab")},
                    **{f"{ez_of(k)}_values{k}a": e_values(k) for k in range(NQ)},
                }

                def bound(name):
                    c = chain.get("b" if name[0] == "m" else name[0])
                    return lambda p: table[name](c, p)

                run(order, {name: bound(name) for name in table}, z=z, e=e, b=b, a=a)
                for c in chain.values():
                    c.end()

            for n in range(2):
                dve.memset(vA[n][:, :, DH:DH + 1], 1.0).then_inc(consts.sem, 1)
            dve.memset(idx[:, :, :], 0).then_inc(consts.sem, 1)
            dve.sem_inc(y_sb.sem, 2)
            dve.wait_ge(loaded["tok"].sem, 16)
            dve.tensor_scalar(posb[:, :], W("tok", "pos"), W("tok", "b_patch"), None, ALU.add
                              ).then_inc(consts.sem, 1)
            dve.wait_ge(consts.sem, N_CONSTS)
            chains(SCHEDULE["dve"], a=0)
            chains(START["dve"], b=0, a=1)
            chains(SCHEDULE["dve"], e=0, b=1, a=2)
            with dve.Fori(1, PAIRS - 2) as pair:
                chains(SCHEDULE["dve"], z=pair - 1, e=pair, b=pair + 1, a=pair + 2)
            chains(SCHEDULE["dve"], z=PAIRS - 3, e=PAIRS - 2, b=PAIRS - 1)
            chains(SCHEDULE["dve"], z=PAIRS - 2, e=PAIRS - 1)
            chains(SCHEDULE["dve"], z=PAIRS - 1)


def _pack(pack, parts):
    cols, width = columns(pack)
    out = np.zeros((128, width), np.float32)
    for name, (r, n) in PACKS[pack].items():
        out[0:r, cols[name]:cols[name] + n] = parts[name].reshape(r, n)
    return out


def _rope_tables():
    t = np.arange(S, dtype=np.float32)
    cos, sin = np.cos(t), np.sin(t)
    tq = [cos, cos, -sin, -sin, cos, cos, sin, sin]
    tk = [cos, -sin, cos, -sin, cos, sin, cos, sin]
    out = []
    for rows_ in (tq, tk):
        a = np.zeros((4, HROWS, S), np.float32)
        a[:, 0:DH] = 1.0
        a[:, DH:DH + 8] = np.stack(rows_)
        out.append(a.reshape(128, S))
    return out


ROPE_Q = [0, 0, 1, 1, 1, 1, 0, 0]
ROPE_K = [0, 1, 0, 1, 1, 0, 1, 0]


def _head_rows(w, rope=None, order=None):
    n = (w if w is not None else rope).shape[0]
    out = np.zeros((n, HEADS, HROWS), np.float32)
    if w is not None:
        out[:, :, 0:DH] = w.reshape(n, HEADS, DH)
    if rope is not None:
        out[:, :, DH:DH + 8] = rope.reshape(n, HEADS, 2)[:, :, order]
    return out.reshape(n, HEADS * HROWS)


def _layouts(i):
    i = {k: np.asarray(v) for k, v in i.items()}
    tq, tk = _rope_tables()
    tq = tq * np.float32(1 / math.sqrt(DH + 2))
    s, t = np.arange(S)[None, :], np.arange(S)[:, None]
    kv = i["L0_attn_W_ukv"]
    w1 = i["L1_attn_w_qkv"].reshape(3, D, D).transpose(0, 2, 1)
    packs = {
        "tok": {
            "w_patch": i["L0_tok_W_patch"].reshape(KCH, 128, D).transpose(1, 0, 2),
            "pos": i["L0_tok_pos_embed"][0].T, "b_patch": i["L0_tok_b_patch"],
            "w_cs": np.concatenate([i["L0_tok_W_coord"], i["L0_tok_W_spinor"]], 1),
            "b_cs": np.tile(np.concatenate([i["L0_tok_b_coord"], i["L0_tok_b_spinor"]])[None], (NTOK, 1)),
            "w_emb": np.concatenate([i["L0_tok_W_embed"], i["L0_tok_b_embed"][None]], 0),
            "ident": np.eye(128, dtype=np.float32), "ln_g": i["L0_tok_ln_gamma"], "ln_b": i["L0_tok_ln_beta"],
            "w_out": i["L0_tok_W_out"], "b_out": i["L0_tok_b_out"], "ones": np.ones(128, np.float32)},
        "at0": {
            "w_down": np.concatenate([i["L0_attn_W_dq"], i["L0_attn_W_dkv"]], 1),
            "q_g": i["L0_attn_q_ln_g"], "q_b": i["L0_attn_q_ln_b"],
            "kv_g": i["L0_attn_kv_ln_g"], "kv_b": i["L0_attn_kv_ln_b"],
            "w_q": _head_rows(i["L0_attn_W_uq"], i["L0_attn_W_qr"], ROPE_Q),
            "w_k": _head_rows(kv[:, 0:D]), "w_kr": _head_rows(None, i["L0_attn_W_kr"], ROPE_K),
            "w_v": kv[:, D:2 * D], "w_o": i["L0_attn_W_o"].T,
            "rope_q": tq, "rope_k": tk, "mask": np.where(s > t, np.float32(MASKED), np.float32(0.0))},
        "moe": {
            "sel": i["L0_ffn_expert_sel"].T,
            "iota": np.tile(np.arange(E0, dtype=np.float32)[None], (S, 1)),
            "keys": i["L0_ffn_keys"].transpose(1, 0, 2), "values": i["L0_ffn_values"].transpose(1, 0, 2)},
        "at1": {
            "w_q": _head_rows(w1[0]), "w_k": _head_rows(w1[1]), "w_v": w1[2],
            "w_o": i["L1_attn_w_agg"].T, "b_o": i["L1_attn_b_agg"]},
        "pk": {
            "w_q": i["L1_ffn_Wq"].T, "b_q": i["L1_ffn_bq"].reshape(PH, 128).T,
            "keys": i["L1_ffn_keys"].transpose(1, 3, 0, 2),
            "iota": np.tile(np.arange(TOPK, dtype=np.float32)[None], (S, 1))},
    }
    x = i["x"].reshape(PAIRS, 2, CH, SIDE, PATCH, SIDE, PATCH).transpose(0, 2, 4, 6, 1, 3, 5)
    x = x.reshape(PAIRS, KCH, 128, 2 * NTOK).transpose(0, 2, 1, 3).reshape(PAIRS, 128, KCH * 2 * NTOK)
    return {
        "patches": np.ascontiguousarray(x),
        "txt": np.ascontiguousarray(i["txt"]),
        "rows": np.concatenate([i["L1_ffn_w_down_embed"], i["L1_ffn_w_up_embed"]], 1),
        **{"pack_" + k: _pack(k, v) for k, v in packs.items()},
    }


def kernel(**inputs):
    import concourse.bacc as bacc
    from concourse.bass_utils import run_bass_kernel_spmd

    arrays = _layouts(inputs)
    nc = bacc.Bacc("TRN2", target_bir_lowering=False, num_devices=1)
    aps = {n: nc.dram_tensor(n, a.shape, mybir.dt.from_np(a.dtype), kind="ExternalInput").ap()
           for n, a in arrays.items()}
    out = nc.dram_tensor("out", (B, S, D), F32, kind="ExternalOutput").ap()
    fusion_program(nc, aps["patches"], aps["txt"], {k: aps["pack_" + k] for k in PACKS}, aps["rows"], out)
    result = run_bass_kernel_spmd(nc, [arrays], core_ids=[0])
    return result.results[0]["out"]
```
